# Optimizing a Trainium2 kernel written in Bass

```python
import numpy as np
import jax
import jax.numpy as jnp

def _softmax(x, axis=-1):
    return jax.nn.softmax(x, axis=axis)

def _gelu(x):
    return jax.nn.gelu(x, approximate=True)

def _silu(x):
    return jax.nn.silu(x)

def _sigmoid(x):
    return jax.nn.sigmoid(x)

def _layernorm(x, axis=-1, eps=1e-05):
    m = jnp.mean(x, axis=axis, keepdims=True)
    v = jnp.var(x, axis=axis, keepdims=True)
    return (x - m) / jnp.sqrt(v + eps)

def _scatter_add(tgt, idx, src, axis=0):
    return tgt.at[idx].add(src)

def _segment_sum(src, seg, n):
    return jax.ops.segment_sum(src, seg, n)
kernel_name = 'mk_adaln_d1_jaxref_r8_900f2b'

def setup_inputs(seed: int=0):
    np.random.seed(seed)
    _w = jnp.asarray

    def _L0_attn_setup():
        import jax, jax.numpy as jnp
        import numpy as np
        D_MODEL = 128
        NHEAD = 16
        HEAD_DIM = D_MODEL // NHEAD
        ROTARY_DIM = HEAD_DIM
        D_INNER = 2 * D_MODEL
        HEADDIM = 64
        H_SSM = D_INNER // HEADDIM
        D_STATE = 128
        D_CONV = 4
        CHUNK = 32
        CONV_DIM = D_INNER + 2 * D_STATE
        D_IN_PROJ = 2 * D_INNER + 2 * D_STATE + H_SSM
        EPS = 1e-05

        def rmsnorm(x, w):
            var = jnp.mean(x * x, axis=-1, keepdims=True)
            return x * jax.lax.rsqrt(var + EPS) * w

        def apply_rope(q):
            T = q.shape[1]
            half = ROTARY_DIM // 2
            inv_freq = 1.0 / 10000.0 ** (jnp.arange(0, ROTARY_DIM, 2, dtype=jnp.float32) / ROTARY_DIM)
            freqs = jnp.arange(T, dtype=jnp.float32)[:, None] * inv_freq[None, :]
            cos = jnp.cos(freqs)[None, :, None, :]
            sin = jnp.sin(freqs)[None, :, None, :]
            q1 = q[..., :half]
            q2 = q[..., half:ROTARY_DIM]
            rest = q[..., ROTARY_DIM:]
            return jnp.concatenate([q1 * cos - q2 * sin, q2 * cos + q1 * sin, rest], axis=-1)

        def segsum(x):
            T = x.shape[-1]
            xc = jnp.cumsum(x, axis=-1)
            ss = xc[..., :, None] - xc[..., None, :]
            mask = jnp.tril(jnp.ones((T, T), dtype=bool))
            return jnp.where(mask, ss, -jnp.inf)

        def ssd(x, dt, A, Bm, Cm):
            b, l, h, p = x.shape
            n = Bm.shape[-1]
            c = l // CHUNK
            xdt = (x * dt[..., None]).reshape(b, c, CHUNK, h, p)
            Adt = (dt * A).reshape(b, c, CHUNK, h).transpose(0, 3, 1, 2)
            Br = Bm.reshape(b, c, CHUNK, n)
            Cr = Cm.reshape(b, c, CHUNK, n)
            Acs = jnp.cumsum(Adt, axis=-1)
            Lmat = jnp.exp(segsum(Adt))
            Y_diag = jnp.einsum('bcln,bcsn,bhcls,bcshp->bclhp', Cr, Br, Lmat, xdt)
            decay_states = jnp.exp(Acs[..., -1:] - Acs)
            states = jnp.einsum('bcln,bhcl,bclhp->bchpn', Br, decay_states, xdt)
            A_chunk = jnp.pad(Acs[..., -1], ((0, 0), (0, 0), (1, 0)))
            decay_chunk = jnp.exp(segsum(A_chunk))
            states = jnp.concatenate([jnp.zeros_like(states[:, :1]), states], axis=1)
            new_states = jnp.einsum('bhzc,bchpn->bzhpn', decay_chunk, states)
            states_prev = new_states[:, :-1]
            Y_off = jnp.einsum('bcln,bchpn,bhcl->bclhp', Cr, states_prev, jnp.exp(Acs))
            return (Y_diag + Y_off).reshape(b, l, h, p)
        key = jax.random.key(seed)
        ks = jax.random.split(key, 8)
        B, T = (2, 256)
        return {'x': jax.random.normal(ks[0], (B, T, D_MODEL), dtype=jnp.float32), 'W_in': jax.random.normal(ks[1], (3 * D_MODEL, D_MODEL), dtype=jnp.float32) * 0.02, 'W_zxbcdt': jax.random.normal(ks[2], (D_IN_PROJ, D_MODEL), dtype=jnp.float32) * 0.02, 'conv_w': jax.random.normal(ks[3], (CONV_DIM, D_CONV), dtype=jnp.float32) * 0.2, 'conv_b': jnp.zeros((CONV_DIM,), dtype=jnp.float32), 'dt_bias': jax.random.normal(ks[4], (H_SSM,), dtype=jnp.float32) * 0.5, 'A_log': jax.random.normal(ks[5], (H_SSM,), dtype=jnp.float32) * 0.5, 'D_param': jax.random.normal(ks[6], (H_SSM,), dtype=jnp.float32), 'norm_pre_w': jnp.ones((D_MODEL,), dtype=jnp.float32), 'norm_gated_w': jnp.ones((D_INNER,), dtype=jnp.float32), 'W_out': jax.random.normal(ks[7], (D_MODEL, D_INNER), dtype=jnp.float32) * 0.02}
    _L0_attn_in = _L0_attn_setup()

    def _L0_ffn_setup():
        import jax, jax.numpy as jnp
        import numpy as np
        EMBED_DIM = 128
        HIDDEN_DIM = 512
        NUM_EXPERTS = 8
        TOP_K = 2
        key = jax.random.key(seed)
        ks = jax.random.split(key, 4)
        std1 = float(np.sqrt(2.0 / EMBED_DIM))
        std2 = float(np.sqrt(2.0 / HIDDEN_DIM))
        x = jax.random.normal(ks[0], (1, 256, EMBED_DIM), dtype=jnp.float32)
        w_router = jax.random.normal(ks[1], (EMBED_DIM, NUM_EXPERTS), dtype=jnp.float32) * 0.02
        w1 = jax.random.normal(ks[2], (NUM_EXPERTS, EMBED_DIM, HIDDEN_DIM), dtype=jnp.float32) * std1
        b1 = jnp.zeros((NUM_EXPERTS, HIDDEN_DIM), dtype=jnp.float32)
        w2 = jax.random.normal(ks[3], (NUM_EXPERTS, HIDDEN_DIM, EMBED_DIM), dtype=jnp.float32) * std2
        b2 = jnp.zeros((NUM_EXPERTS, EMBED_DIM), dtype=jnp.float32)
        return {'x': x, 'w_router': w_router, 'w1': w1, 'b1': b1, 'w2': w2, 'b2': b2}
    _L0_ffn_in = _L0_ffn_setup()
    _L0_c = _w((lambda *s: np.random.randn(*s).astype(np.float32) * 0.05)(8, 128))
    _L0_wmod = _w((lambda *s: np.random.randn(*s).astype(np.float32) * 0.05)(128, 6 * 128) * 128 ** (-0.5))
    _d = {'L0_attn_x': _L0_attn_in['x'], 'L0_attn_W_in': _L0_attn_in['W_in'], 'L0_attn_W_zxbcdt': _L0_attn_in['W_zxbcdt'], 'L0_attn_conv_w': _L0_attn_in['conv_w'], 'L0_attn_conv_b': _L0_attn_in['conv_b'], 'L0_attn_dt_bias': _L0_attn_in['dt_bias'], 'L0_attn_A_log': _L0_attn_in['A_log'], 'L0_attn_D_param': _L0_attn_in['D_param'], 'L0_attn_norm_pre_w': _L0_attn_in['norm_pre_w'], 'L0_attn_norm_gated_w': _L0_attn_in['norm_gated_w'], 'L0_attn_W_out': _L0_attn_in['W_out'], 'L0_ffn_w_router': _L0_ffn_in['w_router'], 'L0_ffn_w1': _L0_ffn_in['w1'], 'L0_ffn_b1': _L0_ffn_in['b1'], 'L0_ffn_w2': _L0_ffn_in['w2'], 'L0_ffn_b2': _L0_ffn_in['b2'], 'L0_c': _L0_c, 'L0_wmod': _L0_wmod}
    _x0 = _d['L0_attn_x']
    _d['L0_attn_x'] = jax.random.normal(jax.random.fold_in(jax.random.key(seed), 1), (8, 512, 128), dtype=_x0.dtype)
    del _x0
    return _d

def reference(L0_attn_x, L0_attn_W_in, L0_attn_W_zxbcdt, L0_attn_conv_w, L0_attn_conv_b, L0_attn_dt_bias, L0_attn_A_log, L0_attn_D_param, L0_attn_norm_pre_w, L0_attn_norm_gated_w, L0_attn_W_out, L0_ffn_w_router, L0_ffn_w1, L0_ffn_b1, L0_ffn_w2, L0_ffn_b2, L0_c, L0_wmod):

    def _L0_attn_ref(x, W_in, W_zxbcdt, conv_w, conv_b, dt_bias, A_log, D_param, norm_pre_w, norm_gated_w, W_out):
        import jax, jax.numpy as jnp
        import numpy as np
        D_MODEL = 128
        NHEAD = 16
        HEAD_DIM = D_MODEL // NHEAD
        ROTARY_DIM = HEAD_DIM
        D_INNER = 2 * D_MODEL
        HEADDIM = 64
        H_SSM = D_INNER // HEADDIM
        D_STATE = 128
        D_CONV = 4
        CHUNK = 32
        CONV_DIM = D_INNER + 2 * D_STATE
        D_IN_PROJ = 2 * D_INNER + 2 * D_STATE + H_SSM
        EPS = 1e-05

        def rmsnorm(x, w):
            var = jnp.mean(x * x, axis=-1, keepdims=True)
            return x * jax.lax.rsqrt(var + EPS) * w

        def apply_rope(q):
            T = q.shape[1]
            half = ROTARY_DIM // 2
            inv_freq = 1.0 / 10000.0 ** (jnp.arange(0, ROTARY_DIM, 2, dtype=jnp.float32) / ROTARY_DIM)
            freqs = jnp.arange(T, dtype=jnp.float32)[:, None] * inv_freq[None, :]
            cos = jnp.cos(freqs)[None, :, None, :]
            sin = jnp.sin(freqs)[None, :, None, :]
            q1 = q[..., :half]
            q2 = q[..., half:ROTARY_DIM]
            rest = q[..., ROTARY_DIM:]
            return jnp.concatenate([q1 * cos - q2 * sin, q2 * cos + q1 * sin, rest], axis=-1)

        def segsum(x):
            T = x.shape[-1]
            xc = jnp.cumsum(x, axis=-1)
            ss = xc[..., :, None] - xc[..., None, :]
            mask = jnp.tril(jnp.ones((T, T), dtype=bool))
            return jnp.where(mask, ss, -jnp.inf)

        def ssd(x, dt, A, Bm, Cm):
            b, l, h, p = x.shape
            n = Bm.shape[-1]
            c = l // CHUNK
            xdt = (x * dt[..., None]).reshape(b, c, CHUNK, h, p)
            Adt = (dt * A).reshape(b, c, CHUNK, h).transpose(0, 3, 1, 2)
            Br = Bm.reshape(b, c, CHUNK, n)
            Cr = Cm.reshape(b, c, CHUNK, n)
            Acs = jnp.cumsum(Adt, axis=-1)
            Lmat = jnp.exp(segsum(Adt))
            Y_diag = jnp.einsum('bcln,bcsn,bhcls,bcshp->bclhp', Cr, Br, Lmat, xdt)
            decay_states = jnp.exp(Acs[..., -1:] - Acs)
            states = jnp.einsum('bcln,bhcl,bclhp->bchpn', Br, decay_states, xdt)
            A_chunk = jnp.pad(Acs[..., -1], ((0, 0), (0, 0), (1, 0)))
            decay_chunk = jnp.exp(segsum(A_chunk))
            states = jnp.concatenate([jnp.zeros_like(states[:, :1]), states], axis=1)
            new_states = jnp.einsum('bhzc,bchpn->bzhpn', decay_chunk, states)
            states_prev = new_states[:, :-1]
            Y_off = jnp.einsum('bcln,bchpn,bhcl->bclhp', Cr, states_prev, jnp.exp(Acs))
            return (Y_diag + Y_off).reshape(b, l, h, p)
        N, T, _ = x.shape
        qkv = (x @ W_in.T).reshape(N, T, 3, NHEAD, HEAD_DIM)
        q = apply_rope(qkv[:, :, 0]).reshape(N, T, D_MODEL)
        residual = q
        h = rmsnorm(q, norm_pre_w)
        zxbcdt = h @ W_zxbcdt.T
        z = zxbcdt[..., :D_INNER]
        xBC = zxbcdt[..., D_INNER:D_INNER + CONV_DIM]
        dt = jax.nn.softplus(zxbcdt[..., -H_SSM:] + dt_bias)
        xp = jnp.pad(xBC, ((0, 0), (D_CONV - 1, 0), (0, 0)))
        conv_out = conv_b
        for k in range(D_CONV):
            conv_out = conv_out + xp[:, k:k + T, :] * conv_w[:, k]
        xBC = jax.nn.silu(conv_out)
        x_ssm = xBC[..., :D_INNER].reshape(N, T, H_SSM, HEADDIM)
        Bm = xBC[..., D_INNER:D_INNER + D_STATE]
        Cm = xBC[..., D_INNER + D_STATE:]
        A = -jnp.exp(A_log)
        y = ssd(x_ssm, dt, A, Bm, Cm) + D_param[None, None, :, None] * x_ssm
        y = y.reshape(N, T, D_INNER)
        y = rmsnorm(y * jax.nn.silu(z), norm_gated_w)
        out = y @ W_out.T
        return out + residual

    def _L0_ffn_ref(x, w_router, w1, b1, w2, b2):
        import jax, jax.numpy as jnp
        import numpy as np
        EMBED_DIM = 128
        HIDDEN_DIM = 512
        NUM_EXPERTS = 8
        TOP_K = 2
        orig_shape = x.shape
        xf = x.reshape(-1, EMBED_DIM)
        logits = xf @ w_router
        probs = jax.nn.softmax(logits, axis=-1)
        topk_w, topk_idx = jax.lax.top_k(probs, TOP_K)
        mask = jax.nn.one_hot(topk_idx, NUM_EXPERTS, dtype=xf.dtype)
        weights = jnp.sum(topk_w[..., None] * mask, axis=1)
        h = jnp.einsum('te,ieh->tih', xf, w1) + b1
        h = jax.nn.gelu(h)
        out = jnp.einsum('tih,ihe->tie', h, w2) + b2
        out = jnp.sum(out * weights[..., None], axis=1)
        return out.reshape(orig_shape)
    x = L0_attn_x
    mod = (_silu(L0_c) @ L0_wmod).reshape(L0_c.shape[0], 6, 1, -1)
    sa, ca, ga, sb, cb, gb = (mod[:, 0], mod[:, 1], mod[:, 2], mod[:, 3], mod[:, 4], mod[:, 5])
    ga = (2 * (ga >= 0) - 1) * jnp.maximum(jnp.abs(ga), 0.25)
    gb = (2 * (gb >= 0) - 1) * jnp.maximum(jnp.abs(gb), 0.25)
    h = _layernorm(x, axis=-1) * (1 + ca) + sa
    x = x + ga * _L0_attn_ref(h, L0_attn_W_in, L0_attn_W_zxbcdt, L0_attn_conv_w, L0_attn_conv_b, L0_attn_dt_bias, L0_attn_A_log, L0_attn_D_param, L0_attn_norm_pre_w, L0_attn_norm_gated_w, L0_attn_W_out)
    h = _layernorm(x, axis=-1) * (1 + cb) + sb
    x = x + gb * _L0_ffn_ref(h, L0_ffn_w_router, L0_ffn_w1, L0_ffn_b1, L0_ffn_w2, L0_ffn_b2)
    return x

_drawn_inputs = setup_inputs


def setup_inputs(seed=0):
    import zlib

    import numpy as np

    out = dict(_drawn_inputs(seed))
    spreads = {'L0_attn_conv_b': (0.0, 0.1),
     'L0_attn_norm_pre_w': (1.0, 0.6),
     'L0_attn_norm_gated_w': (1.0, 0.6),
     'L0_ffn_b1': (0.0, 0.8),
     'L0_ffn_b2': (0.0, 0.8)}
    factors = {'L0_attn_dt_bias': 42.269, 'L0_attn_A_log': 64.0}
    for name, (base, spread) in spreads.items():
        noise = np.random.default_rng([zlib.crc32(name.encode()), seed]).standard_normal(out[name].shape)
        drawn = base * np.exp(spread * noise) if base else spread * noise
        out[name] = jnp.asarray(drawn.astype(out[name].dtype))
    for name, factor in factors.items():
        out[name] = (out[name] * factor).astype(out[name].dtype)
    return out
```

```python
import numpy as np
import concourse.bass as bass
from concourse import mybir
from contextlib import ExitStack

P = 128
F32 = mybir.dt.float32
ALU = mybir.AluOpType
ACT = mybir.ActivationFunctionType
AX = mybir.AxisListType.X
EPS = 1e-5
BIG = 1.0e30


def wait(eng, sem, value):
    if isinstance(value, int) and value <= 0:
        return
    eng.wait_ge(sem, value)


def slots(eng, n, lag, body):
    for s in range(lag):
        body(s)
    with eng.Fori(lag, n) as s:
        body(s)
    for s in range(n, n + lag):
        body(s)


def inside(i, n):
    return not isinstance(i, int) or 0 <= i < n


def build(nc, x, W_in, W_z, conv_w, conv_b, dt_bias, A_log, D_param, norm_pre_w, norm_gated_w, W_out,
          w_router, w1, b1, w2, b2, c_in, wmod, consts, out):
    NB, T, D = x.shape
    NC = T // P
    NT = NB * NC
    NX = norm_gated_w.shape[0] // P
    DI = NX * P
    NH = A_log.shape[0]
    HD = DI // NH
    NBLK = NX + 2
    KC = conv_w.shape[1]
    NE, _, HID = w1.shape
    NK = HID // P
    ZB, XB0, DT0 = 0, DI, DI + NBLK * P
    assert D == P and T == 512

    with ExitStack() as ctx:
        def sb(name, shape, dt=F32):
            return ctx.enter_context(nc.sbuf_tensor(name, shape, dt))

        def pb(name, shape, dt=F32):
            return ctx.enter_context(nc.psum_tensor(name, shape, dt))

        def sem(name):
            return ctx.enter_context(nc.semaphore(name))

        x_sb = sb("x_sb", [P, NB, NC, P])
        qT = sb("qT", [P, NB, T])
        hT = sb("hT", [P, NB, T])
        w1_sb = sb("w1_sb", [P, NE, HID])
        w2_sb = sb("w2_sb", [P, NE, NK, P])
        cst = sb("cst", [P, 3 * P + 2 * T])
        ident, triS, triI = cst[:, 0:P], cst[:, P:2 * P], cst[:, 2 * P:3 * P]
        ropeC, ropeS = cst[:, 3 * P:3 * P + T], cst[:, 3 * P + T:3 * P + 2 * T]
        ones = sb("ones", [P, P])
        eps = sb("eps", [P, 1])
        rows = sb("rows", [64, P])
        NR = NE * NK + NBLK + NX + 1 + NB
        R_B1, R_CB, R_NG, R_NP, R_C = 0, NE * NK, NE * NK + NBLK, NE * NK + NBLK + NX, NE * NK + NBLK + NX + 1
        cols = sb("cols", [P, NR])
        small = sb("small", [1, 3 * NH])
        hb = sb("hb", [P, 3 * NH])
        negA = sb("negA", [P, NH])
        win = sb("win", [P, P])
        wqT = sb("wqT", [P, P])
        wqrT = sb("wqrT", [P, P])
        wz_nat = sb("wz_nat", [P, NX + NBLK, P])
        wdt_nat = sb("wdt_nat", [NH, P])
        wzT = sb("wzT", [P, DT0 + NH])
        wout_nat = sb("wout_nat", [P, DI])
        wmod_sb = sb("wmod_sb", [P, 6 * P])
        wr_sb = sb("wr_sb", [P, NE])
        b2_row = sb("b2_row", [1, NE, P])
        cw = sb("cw", [P, NBLK, KC])
        cwh = sb("cwh", [P, NBLK, KC])
        cbh = sb("cbh", [P, NBLK])
        siluc = sb("siluc", [P, 3, NB])
        mod = sb("mod", [P, 6, NB])
        gsign = sb("gsign", [P, 2, NB])
        gabs = sb("gabs", [P, 2, NB])
        gad = sb("gad", [P, NB, P])
        gbd = sb("gbd", [P, P])
        woB = sb("woB", [P, NB, NX, P])
        gbB = sb("gbB", [P, NB, P])
        st6 = sb("st6", [P, NT, 6])
        mv = sb("mv", [P, 4, NT])
        lnv = sb("lnv", [P, NT])
        rstd = sb("rstd", [P, NT])
        dtT = sb("dtT", [NH, T])
        dtr = sb("dtr", [P, NT, NH])
        dts = sb("dts", [P, 6, NT * NH])
        dt_ = sb("dt_", [P, NT, NH])
        dtA = sb("dtA", [P, NT, NH])
        dec = sb("dec", [P, 3, NT * NH])
        dtdec = sb("dtdec", [P, NT, NH])
        big = sb("big", [P, 8, T])
        xh, xnT, t1, t2, sq, rb = (big[:, i, :] for i in range(6))
        hq = sb("hq", [P, 2, 2, T])
        xbcT = sb("xbcT", [P, 2, NBLK, T])
        acc = [big[:, 0, :], big[:, 1, :]]
        cth = [big[:, 2, :], big[:, 3, :]]
        rhsL = [big[:, 4, :], big[:, 5, :]]
        E4 = [big[:, 6, :], big[:, 7, :]]
        M4 = [sb("M4a", [P, NH * P]), sb("M4b", [P, NH * P])]
        xB = sb("xB", [P, 2, DI + P])
        Gm = sb("Gm", [P, P])
        xdt = sb("xdt", [P, 2, DI])
        xdec = sb("xdec", [P, 2, DI])
        xD = sb("xD", [P, 2, DI])
        zth = sb("zth", [P, 2, DI])
        zs = sb("zs", [P, 2, DI])
        yo = sb("yo", [P, DI])
        yd = sb("yd", [P, DI])
        ys = sb("ys", [P, DI])
        yz = sb("yz", [P, 2, DI])
        junk = sb("junk", [P, DI])
        ynT = sb("ynT", [P, DI])
        state = sb("state", [P, 2, DI])
        sdec = sb("sdec", [P, DI])
        ss = sb("ss", [P, 2, 1])
        ms = sb("ms", [P, 2, 1])
        rg = sb("rg", [P, 2, 1])
        nhalf = sb("nhalf", [P, 1])
        xo = sb("xo", [P, P])
        lgT = sb("lgT", [NE, T])
        lg = sb("lg", [P, NT, NE])
        rt = xbcT[:, 0, :, :].rearrange("p k (a n) -> p (k a) n", n=NT * NE)
        r1 = sb("r1", [P, 6, NT])
        wexp = sb("wexp", [P, NT, NE])
        desc = sb("desc", [P, NE])

        bank = [pb(f"bank{i}", [P, 512]) for i in range(8)]

        s_cst, s_wts, s_x, s_moe = sem("constants_loaded"), sem("weights_loaded"), [sem(f"x_loaded_{b}") for b in range(NB)], sem("moe_weights_loaded")
        s_one, s_pre, s_prd, s_pra = sem("memsets_done"), sem("prep_pe"), sem("prep_dve"), sem("prep_act")
        s_gd, s_gm, s_ge = sem("gate_diag"), sem("gate_mm"), sem("gate_evac")
        s_ag = sem("stats_batch")
        s_st, s_stc, s_rs, s_rl2 = sem("stats_part"), sem("stats_done"), sem("rstd_ready"), sem("rstd_step")
        a_xh, a_T, a_ev, a_q, a_qr = sem("a_normalised"), sem("a_transposed"), sem("a_modulated"), sem("a_q"), sem("a_q_rot")
        a_t1, a_t2, a_rp, a_sq, a_n = sem("a_t1"), sem("a_t2"), sem("a_roped"), sem("a_squared"), sem("a_meansq")
        a_ln, a_ex, a_h = sem("a_ln"), sem("a_rms"), sem("a_h")
        a_d, a_de, a_dT, a_dc = sem("a_dt"), sem("a_dt_evac"), sem("a_dt_T"), sem("a_dt_done")
        s_da, s_dv, s_dp = sem("dt_act"), sem("dt_dve"), sem("dt_pe")
        s_hq = [sem("hq_even"), sem("hq_odd")]
        b_cv, b_acc, b_tap, b_tp, b_cth, b_cs = (sem("b_conv_proj"), sem("b_conv_first"), sem("b_conv_tap"),
                                                 sem("b_conv_sum"), sem("b_conv_tanh"), sem("b_conv_out"))
        b_T, b_Te, b_rl, b_L, b_E, b_z, b_th, b_zs = (sem("b_T"), sem("b_T_evac"), sem("b_rhsL"), sem("b_L"), sem("b_E"),
                                                      sem("b_z"), sem("b_z_tanh"), sem("b_zs"))
        b_GS, b_Gm, b_M, b_xdt, b_xdec, b_xD = (sem("b_GS"), sem("b_Gm"), sem("b_M"), sem("b_xdt"), sem("b_xdec"), sem("b_xD"))
        b_sd, b_S, b_Y, b_yo, b_yd, b_ys, b_yz, b_ss = (sem("b_sdec"), sem("b_state"), sem("b_Y"), sem("b_yo"), sem("b_yd"),
                                                        sem("b_ysum"), sem("b_yz"), sem("b_ss"))
        b_ms, b_rg, b_yT, b_yTe, b_O, b_xo, b_x2 = (sem("b_ms"), sem("b_rg"), sem("b_yT"), sem("b_yT_evac"), sem("b_out"),
                                                    sem("b_xo"), sem("b_x2"))
        c_xh, c_T, c_ev, c_lg, c_le, c_lT, c_lc = (sem("c_normalised"), sem("c_transposed"), sem("c_modulated"), sem("c_logits"),
                                                   sem("c_logits_evac"), sem("c_logits_T"), sem("c_logits_done"))
        s_rt, s_ra = sem("routing_dve"), sem("routing_act")
        s_rt2, d_t = sem("dve_chain"), sem("d_gated")
        h_bank = [0, 1, 2, 5]
        d_h, d_g, d_o, d_ac, d_x, d_st = (sem("d_hidden"), sem("d_gelu"), sem("d_out"), sem("d_acc"),
                                                            sem("d_x"), sem("d_stored"))

        block = ctx.enter_context(nc.Block())

        def program_b(step):
            for j in range(NBLK):
                step(None, None, None, (0, 0), j, (0, 0, j))

            def batch(b, par, last):
                for c in range(NC):
                    k = NC * b + c
                    step(k, k - 1 if inside(k - 1, NT) else None, k - 2 if inside(k - 2, NT) else None,
                         (b, par), c, None if last else (b + 1, 1 - par, c))
            batch(0, 0, False)
            return batch

        def run_b(eng, step):
            batch = program_b(step)
            with eng.Fori(0, NB // 2 - 1) as j:
                batch(2 * j + 1, 1, False)
                batch(2 * j + 2, 0, False)
            batch(NB - 1, 1, True)
            step(None, NT - 1, NT - 2, (NB, 0), 0, None)
            step(None, None, NT - 1, (NB, 0), 1, None)

        def tokens(ap, b):
            return ap[:, bass.ds(b, 1), :].rearrange("p b t -> p (b t)")

        @block.sync
        def _(sp):
            for dst, src in ((cst[:, :], consts), (rows[R_B1:R_CB, :], b1.rearrange("e (k p) -> (e k) p", p=P)),
                             (rows[R_CB:R_NG, :], conv_b.rearrange("(k p) -> k p", p=P)),
                             (rows[R_NG:R_NP, :], norm_gated_w.rearrange("(k p) -> k p", p=P)),
                             (rows[R_NP:R_C, :], norm_pre_w.rearrange("(k p) -> k p", p=P)),
                             (rows[R_C:NR, :], c_in)):
                sp.dma_start(dst, src).then_inc(s_cst, 16)
            for b in range(NB):
                sp.dma_start(x_sb[:, b, :, :], x[b, :, :].rearrange("(c p) d -> p c d", p=P)).then_inc(s_x[b], 16)
            sp.wait_ge(a_h, NB)

            def fetch(b, par):
                wait(sp, b_O, NC * (b - 1))
                wait(sp, b_z, NC * (b - 1))
                for i, src in enumerate((hT, qT)):
                    sp.dma_start(hq[:, par, i, :], src[:, bass.ds(b, 1), :].rearrange("p b t -> p (b t)")
                                 ).then_inc(s_hq[par], 16)
            for par in range(2):
                fetch(par, par)
            with sp.Fori(1, NB // 2) as j:
                for par in range(2):
                    fetch(2 * j + par, par)
            with sp.Fori(0, NB) as b:
                sp.wait_ge(d_x, b + 1)
                sp.dma_start(out[bass.ds(b, 1), :, :].rearrange("b (c p) d -> p (b c) d", p=P),
                             x_sb[:, bass.ds(b, 1), :, :].rearrange("p b c d -> p (b c) d")).then_inc(d_st, 16)
            sp.wait_ge(d_st, 16 * NB)

        @block.scalar
        def _(act):
            for dst, src in ((win[:, :], W_in[0:P, :]),
                             (wmod_sb[:, :], wmod), (small[:, 0:NH], dt_bias.rearrange("(a h) -> a h", a=1)),
                             (small[:, NH:2 * NH], A_log.rearrange("(a h) -> a h", a=1)),
                             (small[:, 2 * NH:], D_param.rearrange("(a h) -> a h", a=1)),
                             (wz_nat[:, :, :], W_z[0:DT0, :].rearrange("(k p) d -> p k d", p=P)),
                             (wdt_nat[:, :], W_z[DT0:DT0 + NH, :]), (wout_nat[:, :], W_out),
                             (cw[:, :, :], conv_w.rearrange("(k p) t -> p k t", p=P)),
                             (wr_sb[:, :], w_router), (b2_row[:, :, :], b2.rearrange("(a e) d -> a e d", a=1))):
                act.dma_start(dst, src).then_inc(s_wts, 16)
            act.dma_start(w1_sb[:, :, :], w1.rearrange("e d h -> d e h")).then_inc(s_moe, 16)
            act.dma_start(w2_sb[:, :, :, :], w2.rearrange("e (k p) d -> p e k d", p=P)).then_inc(s_moe, 16)
            act.preload_act_table_set("natural_log_exp_and_others")
            act.wait_ge(s_prd, 1)
            nc.scalar.activation(siluc[:, 0, :], cols[:, R_C:NR], ACT.Exp, scale=-1.0).then_inc(s_pra, 1)
            act.wait_ge(s_prd, 2)
            nc.scalar.activation(negA[:, :], hb[:, NH:2 * NH], ACT.Exp).then_inc(s_pra, 1)

            def gates(b):
                act.wait_ge(s_gm, b + 1)
                for k in range(NX):
                    nc.scalar.activation(woB[:, bass.ds(b, 1), k, :].rearrange("p b d -> p (b d)"), bank[5][:, k * P:(k + 1) * P],
                                         ACT.Copy, scale=cols[:, R_NG + k:R_NG + k + 1])
                nc.scalar.activation(gbB[:, bass.ds(b, 1), :].rearrange("p b d -> p (b d)"), bank[5][:, NX * P:(NX + 1) * P],
                                     ACT.Copy).then_inc(s_ge, 1)
            with act.Fori(0, NB) as b:
                gates(b)
            act.wait_ge(s_one, 1)
            act.wait_ge(s_stc, 1)
            nc.scalar.activation(lnv[:, :], mv[:, 1, :], ACT.Ln, bias=eps[:, 0:1]).then_inc(s_rl2, 1)
            act.wait_ge(s_rl2, 1)
            nc.scalar.activation(rstd[:, :], lnv[:, :], ACT.Exp, scale=-0.5).then_inc(s_rs, 1)

            def phase_a(s):
                if inside(s, NB):
                    act.wait_ge(a_T, s + 1)
                    wait(act, a_qr, s)
                    nc.scalar.activation(xnT, bank[0][:, :], ACT.Identity, scale=mod[:, 1, bass.ds(s, 1)],
                                         bias=mod[:, 0, bass.ds(s, 1)]).then_inc(a_ev, 1)
                if inside(s - 2, NB):
                    act.wait_ge(a_rp, s - 1)
                    wait(act, a_n, s - 2)
                    nc.scalar.activation(sq, qT[:, bass.ds(s - 2, 1), :].rearrange("p b t -> p (b t)"), ACT.Square
                                         ).then_inc(a_sq, 1)
                if inside(s - 3, NB):
                    act.wait_ge(a_n, s - 2)
                    wait(act, a_h, s - 3)
                    nc.scalar.activation(rb, bank[3][:, :], ACT.Ln, scale=1.0 / P, bias=eps[:, 0:1]).then_inc(a_ln, 1)
                    act.wait_ge(a_ln, s - 2)
                    nc.scalar.activation(rb, rb, ACT.Exp, scale=-0.5).then_inc(a_ex, 1)
                if inside(s - 4, NB):
                    act.wait_ge(a_d, s - 3)
                    wait(act, a_dT, s - 4)
                    nc.scalar.activation(dtT[:, :], bank[4][0:NH, :], ACT.Copy).then_inc(a_de, 1)
            slots(act, NB, 4, phase_a)
            act.wait_ge(s_dv, 2)
            nc.scalar.activation(dts[:, 2, :], dts[:, 1, :], ACT.Exp, scale=-1.0).then_inc(s_da, 1)
            act.wait_ge(s_dv, 3)
            nc.scalar.activation(dts[:, 4, :], dts[:, 3, :], ACT.Ln).then_inc(s_da, 1)
            act.wait_ge(s_dp, 1)
            nc.scalar.activation(dec[:, :, :].rearrange("p a n -> p (a n)"), bank[5][:, 0:3 * NT * NH], ACT.Exp).then_inc(s_da, 1)

            act.preload_act_table_set("exp_and_others")

            def conv_block(b, par, j):
                n = NBLK * b + j
                act.wait_ge(b_cv, n + 1)
                wait(act, b_cs, n - 1)
                nc.scalar.activation(acc[j % 2], bank[j % 2][:, :], ACT.Identity, scale=cwh[:, j, KC - 1:KC],
                                     bias=cbh[:, j:j + 1]).then_inc(b_acc, 1)

            def conv_tanh(b, par, j):
                n = NBLK * b + j
                act.wait_ge(b_tp, n + 1)
                wait(act, b_cs, n - 1)
                nc.scalar.activation(cth[j % 2], acc[j % 2], ACT.Tanh).then_inc(b_cth, 1)

            def step(k, kq, r, bp, c, conv):
                if r is not None:
                    act.wait_ge(b_yT, r + 1)
                    wait(act, b_O, r)
                    nc.scalar.activation(ynT[:, :], bank[6][:, 0:DI], ACT.Copy).then_inc(b_yTe, 1)
                if k is not None:
                    act.wait_ge(b_T, k + 1)
                    wait(act, b_Y, k - 1)
                    wait(act, b_xD, k - 1)
                    wait(act, b_GS, k)
                    nc.scalar.activation(xB[:, c % 2, :], bank[2][:, 0:DI + P], ACT.Copy).then_inc(b_Te, 1)
                    act.wait_ge(b_L, k + 1)
                    wait(act, b_M, k - 1)
                    nc.scalar.activation(E4[c % 2], bank[3][:, :], ACT.Exp).then_inc(b_E, 1)
                    act.wait_ge(b_z, k + 1)
                    wait(act, b_zs, k - 1)
                    nc.scalar.activation(zth[:, c % 2, :], bank[4][:, 0:DI], ACT.Tanh).then_inc(b_th, 1)
                if conv is not None:
                    conv_block(*conv)
                if kq is not None:
                    act.wait_ge(b_yz, kq + 1)
                    wait(act, b_ss, kq)
                    wait(act, b_ms, kq - 1)
                    nc.scalar.activation(junk[:, :], yz[:, (c + 1) % 2, :], ACT.Square, scale=float(DI) ** -0.5,
                                         accum_out=ss[:, (c + 1) % 2, :]).then_inc(b_ss, 1)
                if conv is not None:
                    conv_tanh(*conv)

            run_b(act, step)

            act.preload_act_table_set("natural_log_exp_and_others")
            act.wait_ge(s_stc, 2)
            nc.scalar.activation(lnv[:, :], mv[:, 1, :], ACT.Ln, bias=eps[:, 0:1]).then_inc(s_rl2, 1)
            act.wait_ge(s_rl2, 2)
            nc.scalar.activation(rstd[:, :], lnv[:, :], ACT.Exp, scale=-0.5).then_inc(s_rs, 1)

            def phase_c(s):
                if inside(s, NB):
                    act.wait_ge(c_T, s + 1)
                    nc.scalar.activation(hT[:, bass.ds(s, 1), :].rearrange("p b t -> p (b t)"), bank[0][:, :], ACT.Identity,
                                         scale=mod[:, 4, bass.ds(s, 1)], bias=mod[:, 3, bass.ds(s, 1)]).then_inc(c_ev, 1)
                if inside(s - 1, NB):
                    act.wait_ge(c_lg, s)
                    wait(act, c_lT, s - 1)
                    nc.scalar.activation(lgT[:, :], bank[1][0:NE, :], ACT.Copy).then_inc(c_le, 1)
            slots(act, NB, 2, phase_c)
            act.wait_ge(s_rt, 2)
            nc.scalar.activation(rt[:, 2, :], rt[:, 1, :], ACT.Exp).then_inc(s_ra, 1)
            act.preload_act_table(ACT.Gelu_apprx_tanh)

            def gelus(b, first):
                for e in range(NE):
                    for k in range(NK):
                        act.wait_ge(d_h, NE * NK * b + NK * e + k + 1)
                        if not (first and e < 2):
                            act.wait_ge(d_o, NE * b + e - 1)
                        nc.scalar.activation(big[:, NK * (e % 2) + k, :], bank[h_bank[k]][:, :], ACT.Gelu_apprx_tanh,
                                             bias=cols[:, R_B1 + NK * e + k:R_B1 + NK * e + k + 1]).then_inc(d_g, 1)
            gelus(0, True)
            with act.Fori(1, NB) as b:
                gelus(b, False)

        @block.gpsimd
        def _(pool):
            nc.gpsimd.memset(ones[:, :], 1.0)
            nc.gpsimd.memset(nhalf[:, :], -0.5)
            for e in range(NE):
                nc.gpsimd.memset(desc[:, e:e + 1], float(NE - e))
            nc.gpsimd.memset(eps[:, :], EPS).then_inc(s_one, 1)

            def phase_a(s):
                if inside(s - 1, NB):
                    pool.wait_ge(a_t2, s)
                    nc.gpsimd.tensor_tensor(qT[:, bass.ds(s - 1, 1), :].rearrange("p b t -> p (b t)"), t1, t2, ALU.add
                                            ).then_inc(a_rp, 1)
                if inside(s - 3, NB):
                    pool.wait_ge(a_ex, s - 2)
                    nc.gpsimd.tensor_tensor(hT[:, bass.ds(s - 3, 1), :].rearrange("p b t -> p (b t)"),
                                            qT[:, bass.ds(s - 3, 1), :].rearrange("p b t -> p (b t)"), rb, ALU.mult
                                            ).then_inc(a_h, 1)
            slots(pool, NB, 3, phase_a)
            pool.wait_ge(s_dv, 6)
            pool.wait_ge(s_prd, 3)

            def step(k, kq, r, bp, c, conv):
                par = c % 2
                if k is not None:
                    wait(pool, b_L, k - 1)
                    nc.gpsimd.tensor_tensor(rhsL[par].rearrange("p (h l) -> p h l", h=NH),
                                            triI.unsqueeze(1).broadcast_to([P, NH, P]),
                                            dtA[:, bass.ds(k, 1), :].rearrange("p a h -> p (a h)").unsqueeze(2)
                                            .broadcast_to([P, NH, P]), ALU.mult).then_inc(b_rl, 1)
                if kq is not None and c != 0:
                    if c != 1:
                        pool.wait_ge(b_S, bp[0] * (NC - 1) + c - 1)
                        nc.gpsimd.tensor_tensor(
                            sdec[:, :].rearrange("p (h q) -> p h q", h=NH),
                            state[:, c % 2, :].rearrange("p (h q) -> p h q", h=NH),
                            dec[:, 2, bass.ds(NH * kq, NH)].unsqueeze(2).broadcast_to([P, NH, HD]), ALU.mult
                        ).then_inc(b_sd, 1)
                if k is not None:
                    xv = xB[:, par, 0:DI].rearrange("p (h q) -> p h q", h=NH)
                    pool.wait_ge(b_Te, k + 1)
                    if c != NC - 1:
                        wait(pool, b_GS, k)
                        nc.gpsimd.tensor_tensor(xdec[:, par, :].rearrange("p (h q) -> p h q", h=NH), xv,
                                                dtdec[:, bass.ds(k, 1), :].rearrange("p a h -> p (a h)").unsqueeze(2)
                                                .broadcast_to([P, NH, HD]), ALU.mult).then_inc(b_xdec, 1)
                    wait(pool, b_yd, k - 1)
                    nc.gpsimd.tensor_tensor(xD[:, par, :].rearrange("p (h q) -> p h q", h=NH), xv,
                                            hb[:, 2 * NH:3 * NH].unsqueeze(2).broadcast_to([P, NH, HD]), ALU.mult
                                            ).then_inc(b_xD, 1)
                if kq is not None:
                    pool.wait_ge(b_yd, kq + 1)
                    wait(pool, b_yz, kq)
                    nc.gpsimd.tensor_tensor(ys[:, :], yo[:, :], yd[:, :], ALU.add).then_inc(b_ys, 1)
                if r is not None:
                    q = c % 2
                    pool.wait_ge(b_ss, r + 1)
                    wait(pool, b_rg, r - 1)
                    nc.gpsimd.tensor_tensor(ms[:, q, :], ss[:, q, :], eps[:, :], ALU.add).then_inc(b_ms, 1)
                    pool.wait_ge(b_ms, r + 1)
                    wait(pool, b_xo, r - 1)
                    nc.gpsimd.tensor_tensor(rg[:, q, :], ms[:, q, :], nhalf[:, :], ALU.pow).then_inc(b_rg, 1)
            run_b(pool, step)

        @block.vector
        def _(dve):
            dve.wait_ge(s_pre, 1)
            nc.vector.tensor_copy(cols[:, :], bank[0][:, 0:NR]).then_inc(s_prd, 1)
            dve.wait_ge(s_pre, 2)
            nc.vector.tensor_copy(hb[:, :], bank[1][:, 0:3 * NH]).then_inc(s_prd, 1)
            dve.wait_ge(s_prd, 2)
            dve.wait_ge(s_wts, 16 * 11)
            dve.wait_ge(s_pra, 2)
            nc.vector.tensor_scalar(negA[:, :], negA[:, :], -1.0, None, ALU.mult)
            nc.vector.tensor_scalar(cwh[:, :, :], cw[:, :, :], 0.5, None, ALU.mult)
            nc.vector.tensor_scalar(cbh[:, :], cols[:, R_CB:R_NG], 0.5, None, ALU.mult)
            nc.vector.tensor_scalar(siluc[:, 1, :], siluc[:, 0, :], 1.0, None, ALU.add).then_inc(s_prd, 1)
            dve.wait_ge(s_prd, 3)
            nc.vector.reciprocal(siluc[:, 2, :], siluc[:, 1, :]).then_inc(s_prd, 1)
            dve.wait_ge(s_prd, 4)
            nc.vector.tensor_tensor(siluc[:, 1, :], siluc[:, 2, :], cols[:, R_C:NR], ALU.mult).then_inc(s_prd, 1)
            dve.wait_ge(s_pre, 3)
            nc.vector.tensor_copy(wqT[:, :], bank[2][:, 0:P])
            sw = bank[2][:, 0:P].rearrange("p (h a i) -> p h a i", a=2, i=4)
            dst = wqrT[:, :].rearrange("p (h a i) -> p h a i", a=2, i=4)
            nc.vector.tensor_copy(dst[:, :, 0, :], sw[:, :, 1, :])
            nc.vector.tensor_copy(dst[:, :, 1, :], sw[:, :, 0, :]).then_inc(s_prd, 1)
            dve.wait_ge(s_pre, 4)
            npw = cols[:, R_NP:R_NP + 1]
            nc.vector.tensor_scalar(wzT[:, 0:DI], bank[3][:, 0:DI], npw, 0.5, ALU.mult, ALU.mult)
            nc.vector.tensor_scalar(wzT[:, DI:4 * P], bank[3][:, DI:4 * P], npw, None, ALU.mult)
            nc.vector.tensor_scalar(wzT[:, 4 * P:DT0 + NH], bank[4][:, 0:DT0 + NH - 4 * P], npw, None, ALU.mult).then_inc(s_prd, 1)
            dve.wait_ge(s_pre, 5)
            nc.vector.tensor_copy(mod[:, :, :].rearrange("p a b -> p (a b)"), bank[1][:, 64:64 + 6 * NB]).then_inc(s_prd, 1)
            dve.wait_ge(s_prd, 8)
            for i, g in enumerate((2, 5)):
                nc.vector.scalar_tensor_tensor(out=gabs[:, i, :], in0=mod[:, g, :], scalar=-1.0, in1=mod[:, g, :],
                                               op0=ALU.mult, op1=ALU.max)
                nc.vector.tensor_scalar(gsign[:, i, :], mod[:, g, :], 0.0, 2.0, ALU.is_ge, ALU.mult).then_inc(s_prd, 1)
            dve.wait_ge(s_prd, 10)
            nc.vector.tensor_scalar(gabs[:, :, :], gabs[:, :, :], 0.25, None, ALU.max)
            nc.vector.tensor_scalar(gsign[:, :, :], gsign[:, :, :], -1.0, None, ALU.add).then_inc(s_prd, 1)
            dve.wait_ge(s_prd, 11)
            for i, g in enumerate((2, 5)):
                nc.vector.tensor_tensor(mod[:, g, :], gabs[:, i, :], gsign[:, i, :], ALU.mult)
            for j in (1, 4):
                nc.vector.tensor_scalar(mod[:, j, :], mod[:, j, :], 1.0, None, ALU.add).then_inc(s_prd, 1)
            dve.wait_ge(s_prd, 13)

            def gates(b):
                wait(dve, s_gm, b)
                nc.vector.tensor_scalar(gad[:, bass.ds(b, 1), :].rearrange("p b d -> p (b d)"), ident,
                                        mod[:, 2, bass.ds(b, 1)], None, ALU.mult)
                nc.vector.tensor_scalar(gbd[:, :], ident, mod[:, 5, bass.ds(b, 1)], None, ALU.mult).then_inc(s_gd, 1)
            gates(0)
            with dve.Fori(1, NB) as b:
                gates(b)

            def stats(b):
                for c in range(NC):
                    ins = nc.vector.bn_stats(st6[:, bass.ds(NC * b + c, 1), :].rearrange("p a m -> p (a m)"),
                                             x_sb[:, bass.ds(b, 1), c, :].rearrange("p b d -> p (b d)"))
                ins.then_inc(s_st, 1)

            def mean_var(n):
                dve.wait_ge(s_st, NB * n)
                me, mo, qe, qo = (st6[:, :, i] for i in (1, 4, 2, 5))
                nc.vector.tensor_tensor(mv[:, 0, :], me, mo, ALU.add)
                nc.vector.tensor_tensor(mv[:, 2, :], me, mo, ALU.subtract)
                nc.vector.tensor_tensor(mv[:, 3, :], qe, qo, ALU.add).then_inc(s_ag, 1)
                dve.wait_ge(s_ag, 2 * n - 1)
                nc.vector.tensor_scalar(mv[:, 0, :], mv[:, 0, :], 0.5, None, ALU.mult)
                nc.vector.scalar_tensor_tensor(out=mv[:, 2, :], in0=mv[:, 2, :], scalar=0.25, in1=mv[:, 2, :],
                                               op0=ALU.mult, op1=ALU.mult).then_inc(s_ag, 1)
                dve.wait_ge(s_ag, 2 * n)
                nc.vector.scalar_tensor_tensor(out=mv[:, 1, :], in0=mv[:, 3, :], scalar=1.0 / P, in1=mv[:, 2, :],
                                               op0=ALU.mult, op1=ALU.add).then_inc(s_stc, 1)
                dve.wait_ge(s_stc, n)

            for b in range(NB):
                dve.wait_ge(s_x[b], 16)
                stats(b)
            mean_var(1)

            def normalise(b):
                for c in range(NC):
                    ins = nc.vector.tensor_scalar(xh[:, c * P:(c + 1) * P],
                                                  x_sb[:, bass.ds(b, 1), c, :].rearrange("p b d -> p (b d)"),
                                                  mv[:, 0, bass.ds(NC * b + c, 1)],
                                                  rstd[:, bass.ds(NC * b + c, 1)], ALU.subtract, ALU.mult)
                return ins

            dve.wait_ge(s_rs, 1)

            def phase_a(s):
                if inside(s, NB):
                    wait(dve, a_T, s)
                    normalise(s).then_inc(a_xh, 1)
                if inside(s - 1, NB):
                    dve.wait_ge(a_q, s)
                    wait(dve, a_rp, s - 1)
                    nc.vector.tensor_tensor(t1, bank[1][:, :], ropeC, ALU.mult).then_inc(a_t1, 1)
                    dve.wait_ge(a_qr, s)
                    nc.vector.tensor_tensor(t2, bank[2][:, :], ropeS, ALU.mult).then_inc(a_t2, 1)
                if inside(s - 5, NB):
                    dve.wait_ge(a_dT, s - 4)
                    nc.vector.tensor_copy(dtr[:, bass.ds(NC * (s - 5), NC), :].rearrange("p c h -> p (c h)"),
                                          bank[5][:, 0:NC * NH]).then_inc(a_dc, 1)
            slots(dve, NB, 5, phase_a)

            dve.wait_ge(a_dc, NB)
            v, av, u, w, lw, tmp = (dts[:, i, :] for i in range(6))
            nc.vector.tensor_tensor(v.rearrange("p (a h) -> p a h", h=NH), dtr[:, :, :],
                                    hb[:, 0:NH].unsqueeze(1).broadcast_to([P, NT, NH]), ALU.add).then_inc(s_dv, 1)
            dve.wait_ge(s_dv, 1)
            nc.vector.scalar_tensor_tensor(out=av, in0=v, scalar=-1.0, in1=v, op0=ALU.mult, op1=ALU.max).then_inc(s_dv, 1)
            dve.wait_ge(s_da, 1)
            nc.vector.tensor_scalar(w, u, 1.0, None, ALU.add).then_inc(s_dv, 1)
            chain = [0]

            def link(ins):
                chain[0] += 1
                ins.then_inc(s_rt2, 1)
                dve.wait_ge(s_rt2, chain[0])
            link(nc.vector.tensor_scalar(tmp, u, -0.25, 1.0 / 3, ALU.mult, ALU.add))
            link(nc.vector.tensor_tensor(tmp, tmp, u, ALU.mult))
            link(nc.vector.tensor_scalar(tmp, tmp, -1.0, 0.5, ALU.mult, ALU.add))
            link(nc.vector.tensor_tensor(tmp, tmp, u, ALU.mult))
            link(nc.vector.tensor_scalar(tmp, tmp, -1.0, 1.0, ALU.mult, ALU.add))
            link(nc.vector.tensor_tensor(tmp, tmp, u, ALU.mult))
            dve.wait_ge(s_da, 2)
            link(nc.vector.tensor_tensor(lw, lw, tmp, ALU.subtract))
            link(nc.vector.scalar_tensor_tensor(out=lw, in0=u, scalar=1.0 / 64, in1=lw, op0=ALU.is_ge, op1=ALU.mult))
            link(nc.vector.tensor_tensor(tmp, tmp, lw, ALU.add))
            dtf = dt_[:, :, :].rearrange("p a h -> p (a h)")
            link(nc.vector.scalar_tensor_tensor(out=dtf, in0=v, scalar=0.0, in1=tmp, op0=ALU.max, op1=ALU.add))
            nc.vector.tensor_tensor(dtA[:, :, :], dt_[:, :, :], negA[:, :].unsqueeze(1).broadcast_to([P, NT, NH]),
                                    ALU.mult).then_inc(s_dv, 1)
            dve.wait_ge(s_da, 3)
            nc.vector.tensor_tensor(dtdec[:, :, :].rearrange("p a h -> p (a h)"), dtf, dec[:, 0, :], ALU.mult).then_inc(s_dv, 1)
            dve.wait_ge(s_dv, 5)
            nc.vector.memset(state[:, :, :], 0.0).then_inc(s_dv, 1)

            def conv_taps(b, par, j):
                n = NBLK * b + j
                dve.wait_ge(b_acc, n + 1)
                for i in range(1, KC):
                    ins = nc.vector.scalar_tensor_tensor(out=acc[j % 2][:, i:T], in0=bank[j % 2][:, 0:T - i],
                                                         scalar=cwh[:, j, KC - 1 - i:KC - i], in1=acc[j % 2][:, i:T],
                                                         op0=ALU.mult, op1=ALU.add)
                    if i < KC - 1:
                        ins.then_inc(b_tap, 1)
                        dve.wait_ge(b_tap, (KC - 2) * n + i)
                ins.then_inc(b_tp, 1)

            def conv_silu(b, par, j):
                n = NBLK * b + j
                dve.wait_ge(b_cth, n + 1)
                if j < NX + 1:
                    wait(dve, b_T, NC * (b - 1))
                wait(dve, b_GS, NC * (b - 1))
                wait(dve, b_Y, NC * (b - 1))
                nc.vector.scalar_tensor_tensor(out=xbcT[:, par, j, :], in0=cth[j % 2], scalar=1.0, in1=acc[j % 2],
                                               op0=ALU.add, op1=ALU.mult).then_inc(b_cs, 1)

            def heads(ap):
                return ap.rearrange("p (h q) -> p h q", h=NH)

            def step(k, kq, r, bp, c, conv):
                par, qar = c % 2, (c + 1) % 2
                if k is not None:
                    dve.wait_ge(b_Te, k + 1)
                    wait(dve, b_Y, k - 1)
                    nc.vector.tensor_tensor(heads(xdt[:, par, :]), heads(xB[:, par, 0:DI]),
                                            dt_[:, bass.ds(k, 1), :].rearrange("p a h -> p (a h)").unsqueeze(2)
                                            .broadcast_to([P, NH, HD]), ALU.mult).then_inc(b_xdt, 1)
                if conv is not None:
                    conv_taps(*conv)
                if k is not None:
                    dve.wait_ge(b_GS, k + 1)
                    nc.vector.tensor_tensor(Gm[:, :], bank[5][:, 0:P], triI, ALU.mult).then_inc(b_Gm, 1)
                if kq is not None:
                    dve.wait_ge(b_Y, kq + 1)
                    if c != 1:
                        nc.vector.tensor_tensor(heads(yo[:, :]), heads(bank[7][:, DI:2 * DI]),
                                                dec[:, 1, bass.ds(NH * kq, NH)].unsqueeze(2).broadcast_to([P, NH, HD]),
                                                ALU.mult)
                    else:
                        nc.vector.memset(yo[:, :], 0.0)
                    dve.wait_ge(b_xD, kq + 1)
                    nc.vector.tensor_tensor(yd[:, :], bank[7][:, 0:DI], xD[:, qar, :], ALU.add).then_inc(b_yd, 1)
                    if c == 1:
                        nc.vector.tensor_copy(state[:, 0, :], bank[5][:, P:P + DI]).then_inc(b_S, 1)
                    elif c != 0:
                        dve.wait_ge(b_sd, (NC - 2) * bp[0] + c - 1)
                        nc.vector.tensor_tensor(state[:, (c + 1) % 2, :], sdec[:, :], bank[5][:, P:P + DI],
                                                ALU.add).then_inc(b_S, 1)
                if k is not None:
                    dve.wait_ge(b_E, k + 1)
                    dve.wait_ge(b_Gm, k + 1)
                    nc.vector.tensor_tensor(M4[par][:, :].rearrange("p (h l) -> p h l", h=NH),
                                            E4[par].rearrange("p (h l) -> p h l", h=NH),
                                            Gm[:, :].unsqueeze(1).broadcast_to([P, NH, P]), ALU.mult).then_inc(b_M, 1)
                    dve.wait_ge(b_th, k + 1)
                    nc.vector.scalar_tensor_tensor(out=zs[:, par, :], in0=zth[:, par, :], scalar=1.0, in1=bank[4][:, 0:DI],
                                                   op0=ALU.add, op1=ALU.mult).then_inc(b_zs, 1)
                if kq is not None:
                    dve.wait_ge(b_ys, kq + 1)
                    dve.wait_ge(b_zs, kq + 1)
                    wait(dve, b_yT, kq - 1)
                    nc.vector.tensor_tensor(yz[:, qar, :], ys[:, :], zs[:, qar, :], ALU.mult).then_inc(b_yz, 1)
                if conv is not None:
                    conv_silu(*conv)
                if r is not None:
                    dve.wait_ge(b_O, r + 1)
                    dve.wait_ge(b_rg, r + 1)
                    xr = x_sb[:, :, :, :].rearrange("p b c d -> p (b c) d")[:, bass.ds(r, 1), :].rearrange("p a d -> p (a d)")
                    nc.vector.scalar_tensor_tensor(out=xo[:, :], in0=bank[6][:, 2 * P:3 * P], scalar=rg[:, par, 0:1], in1=xr,
                                                   op0=ALU.mult, op1=ALU.add).then_inc(b_xo, 1)
                    dve.wait_ge(b_xo, r + 1)
                    nc.vector.tensor_tensor(xr, xo[:, :], bank[6][:, 3 * P:4 * P], ALU.add).then_inc(b_x2, 1)
            run_b(dve, step)

            dve.wait_ge(b_x2, NT)
            with dve.Fori(0, NB) as b:
                stats(b)
            mean_var(2)
            dve.wait_ge(s_rs, 2)

            def phase_c(s):
                if inside(s, NB):
                    wait(dve, c_T, s)
                    normalise(s).then_inc(c_xh, 1)
                if inside(s - 2, NB):
                    dve.wait_ge(c_lT, s - 1)
                    nc.vector.tensor_copy(lg[:, bass.ds(NC * (s - 2), NC), :].rearrange("p c e -> p (c e)"),
                                          bank[2][:, 0:NC * NE]).then_inc(c_lc, 1)
            slots(dve, NB, 2, phase_c)

            dve.wait_ge(c_lc, NB)
            t3 = [rt[:, i, :].rearrange("p (a e) -> p a e", e=NE) for i in range(8)]
            mx1, mx2, pm, z, rz = (r1[:, i, :] for i in range(5))

            def bc(a):
                return a.unsqueeze(2).broadcast_to([P, NT, NE])
            dsc = desc[:, :].unsqueeze(1).broadcast_to([P, NT, NE])
            dve.wait_ge(s_one, 1)
            nc.vector.tensor_reduce(mx1, lg[:, :, :], AX, ALU.max).then_inc(s_rt, 1)
            dve.wait_ge(s_rt, 1)
            nc.vector.tensor_tensor(t3[1], lg[:, :, :], bc(mx1), ALU.subtract).then_inc(s_rt, 1)

            def first_of(src, top, onehot):
                link(nc.vector.tensor_tensor(t3[3], src, bc(top), ALU.is_equal))
                link(nc.vector.tensor_tensor(t3[3], t3[3], dsc, ALU.mult))
                link(nc.vector.tensor_reduce(pm, t3[3], AX, ALU.max))
                link(nc.vector.tensor_tensor(onehot, t3[3], bc(pm), ALU.is_equal))
            first_of(lg[:, :, :], mx1, t3[4])
            link(nc.vector.scalar_tensor_tensor(out=t3[5], in0=t3[4], scalar=-BIG, in1=lg[:, :, :], op0=ALU.mult, op1=ALU.add))
            link(nc.vector.tensor_reduce(mx2, t3[5], AX, ALU.max))
            first_of(t3[5], mx2, t3[6])
            dve.wait_ge(s_ra, 1)
            link(nc.vector.tensor_reduce(z, t3[2], AX, ALU.add))
            link(nc.vector.reciprocal(rz, z))
            link(nc.vector.tensor_tensor(t3[4], t3[4], t3[6], ALU.add))
            link(nc.vector.tensor_tensor(t3[4], t3[4], t3[2], ALU.mult))
            nc.vector.tensor_tensor(wexp[:, :, :], t3[4], bc(rz), ALU.mult).then_inc(s_rt, 1)
            dve.wait_ge(s_rt, 3)

            accm = M4[0]

            def combine(b):
                for e in range(NE):
                    dve.wait_ge(d_o, NE * b + e + 1)
                    wait(dve, d_ac, NE * b + e)
                    for c in range(NC):
                        a, o = accm[:, c * P:(c + 1) * P], bank[3 + e % 2][:, c * P:(c + 1) * P]
                        w = wexp[:, bass.ds(NC * b + c, 1), e]
                        if e == 0:
                            ins = nc.vector.tensor_scalar(a, o, w, None, ALU.mult)
                        else:
                            ins = nc.vector.scalar_tensor_tensor(out=a, in0=o, scalar=w, in1=a, op0=ALU.mult, op1=ALU.add)
                    ins.then_inc(d_ac, 1)
                dve.wait_ge(d_ac, NE * (b + 1))
                gated = M4[1][:, :].rearrange("p (c d) -> p c d", c=NC)
                nc.vector.tensor_tensor(gated, accm[:, :].rearrange("p (c d) -> p c d", c=NC),
                                        gbB[:, bass.ds(b, 1), :].broadcast_to([P, NC, P]), ALU.mult).then_inc(d_t, 1)
                dve.wait_ge(d_t, b + 1)
                xr = x_sb[:, bass.ds(b, 1), :, :].rearrange("p b c d -> p (b c) d")
                nc.vector.tensor_tensor(xr, xr, gated, ALU.add).then_inc(d_x, 1)
            combine(0)
            with dve.Fori(1, NB) as b:
                combine(b)

        @block.tensor
        def _(pe):
            pe.wait_ge(s_cst, 16 * 6)
            nc.tensor.transpose(bank[0][:, 0:NR], rows[0:NR, :], ident[0:NR, 0:NR]).then_inc(s_pre, 1)
            pe.wait_ge(s_wts, 16 * 11)
            pe.wait_ge(s_one, 1)
            nc.tensor.matmul(bank[1][:, 0:3 * NH], ones[0:1, :], small[:, :], start=True, stop=True).then_inc(s_pre, 1)
            nc.tensor.transpose(bank[2][:, 0:P], win[:, :], ident).then_inc(s_pre, 1)
            for j in range(NX + NBLK):
                nc.tensor.transpose(bank[3 + j // 4][:, (j % 4) * P:(j % 4 + 1) * P], wz_nat[:, j, :], ident)
            nc.tensor.transpose(bank[4][:, 2 * P:2 * P + NH], wdt_nat[:, :], ident[0:NH, 0:NH]).then_inc(s_pre, 1)
            pe.wait_ge(s_prd, 5)
            for j in range(6):
                mm = nc.tensor.matmul(bank[1][:, 64 + j * NB:64 + (j + 1) * NB], wmod_sb[:, j * P:(j + 1) * P], siluc[:, 1, :],
                                      start=True, stop=True)
            mm.then_inc(s_pre, 1)

            def gates(b):
                pe.wait_ge(s_gd, b + 1)
                wait(pe, s_ge, b)
                for k in range(NX):
                    nc.tensor.matmul(bank[5][:, k * P:(k + 1) * P], wout_nat[:, k * P:(k + 1) * P],
                                     gad[:, bass.ds(b, 1), :].rearrange("p b d -> p (b d)"), start=True, stop=True)
                nc.tensor.matmul(bank[5][:, NX * P:(NX + 1) * P], ones[:, :], gbd[:, :], start=True, stop=True).then_inc(s_gm, 1)
            gates(0)
            with pe.Fori(1, NB) as b:
                gates(b)
            pe.wait_ge(s_prd, 8)

            def phase_a(s):
                if inside(s, NB):
                    pe.wait_ge(a_xh, s + 1)
                    wait(pe, a_ev, s)
                    for c in range(NC):
                        mm = nc.tensor.transpose(bank[0][:, c * P:(c + 1) * P], xh[:, c * P:(c + 1) * P], ident)
                    mm.then_inc(a_T, 1)
                if inside(s - 1, NB):
                    pe.wait_ge(a_ev, s)
                    wait(pe, a_t1, s - 1)
                    nc.tensor.matmul(bank[1][:, :], wqT[:, :], xnT, start=True, stop=True).then_inc(a_q, 1)
                    wait(pe, a_t2, s - 1)
                    nc.tensor.matmul(bank[2][:, :], wqrT[:, :], xnT, start=True, stop=True).then_inc(a_qr, 1)
                if inside(s - 2, NB):
                    pe.wait_ge(a_sq, s - 1)
                    wait(pe, a_ln, s - 2)
                    nc.tensor.matmul(bank[3][:, :], ones[:, :], sq, start=True, stop=True).then_inc(a_n, 1)
                if inside(s - 4, NB):
                    pe.wait_ge(a_h, s - 3)
                    wait(pe, a_de, s - 4)
                    nc.tensor.matmul(bank[4][0:NH, :], wzT[:, DT0:DT0 + NH],
                                     hT[:, bass.ds(s - 4, 1), :].rearrange("p b t -> p (b t)"), start=True, stop=True
                                     ).then_inc(a_d, 1)
                if inside(s - 5, NB):
                    pe.wait_ge(a_de, s - 4)
                    wait(pe, a_dc, s - 5)
                    for c in range(NC):
                        mm = nc.tensor.matmul(bank[5][:, c * NH:(c + 1) * NH], dtT[:, c * P:(c + 1) * P], ident[0:NH, 0:NH],
                                              start=True, stop=True)
                    mm.then_inc(a_dT, 1)
            pe.wait_ge(s_ge, NB)
            slots(pe, NB, 5, phase_a)
            pe.wait_ge(s_dv, 4)
            dA = dtA[:, :, :].rearrange("p a h -> p (a h)")
            for i, m in enumerate((triS, triI, ones[:, :])):
                mm = nc.tensor.matmul(bank[5][:, i * NT * NH:(i + 1) * NT * NH], m, dA, start=True, stop=True)
            mm.then_inc(s_dp, 1)

            def step(k, kq, r, bp, c, conv):
                par, qar = c % 2, (c + 1) % 2
                if r is not None:
                    pe.wait_ge(b_yz, r + 1)
                    wait(pe, b_x2, r)
                    for i in range(NX):
                        mm = nc.tensor.transpose(bank[6][:, i * P:(i + 1) * P], yz[:, par, i * P:(i + 1) * P], ident)
                    mm.then_inc(b_yT, 1)
                if k is not None:
                    b, bpar = bp
                    tok = slice(c * P, (c + 1) * P)
                    if c == 0:
                        pe.wait_ge(b_cs, NBLK * (b + 1))
                        pe.wait_ge(s_hq[bpar], 16 * b + 32 - 16 * bpar)
                    wait(pe, b_Te, k)
                    for i in range(NX + 1):
                        mm = nc.tensor.transpose(bank[2][:, i * P:(i + 1) * P], xbcT[:, bpar, i, tok], ident)
                    mm.then_inc(b_T, 1)
                    pe.wait_ge(b_rl, k + 1)
                    wait(pe, b_E, k)
                    nc.tensor.matmul(bank[3][:, :], triS, rhsL[par], start=True, stop=True).then_inc(b_L, 1)
                    wait(pe, b_zs, k)
                    nc.tensor.matmul(bank[4][:, 0:DI], hq[:, bpar, 0, tok], wzT[:, 0:DI], start=True, stop=True).then_inc(b_z, 1)
                if conv is not None:
                    cb, _, j = conv
                    wait(pe, b_tp, NBLK * cb + j - 1)
                    nc.tensor.matmul(bank[j % 2][:, :], wzT[:, XB0 + j * P:XB0 + (j + 1) * P],
                                     hT[:, bass.ds(cb, 1), :].rearrange("p b t -> p (b t)"), start=True, stop=True
                                     ).then_inc(b_cv, 1)
                if kq is not None:
                    pe.wait_ge(b_M, kq + 1)
                    pe.wait_ge(b_xdt, kq + 1)
                    wait(pe, b_yd, kq)
                    for h in range(NH):
                        mm = nc.tensor.matmul(bank[7][:, h * HD:(h + 1) * HD], M4[qar][:, h * P:(h + 1) * P],
                                              xdt[:, qar, h * HD:(h + 1) * HD], start=True, stop=True)
                    if c != 1:
                        qb, qbpar, cc = (bp[0], bp[1], c - 1) if c else (bp[0] - 1, 1 - bp[1], NC - 1)
                        pe.wait_ge(b_S, (NC - 1) * qb + cc)
                        mm = nc.tensor.matmul(bank[7][:, DI:2 * DI], xbcT[:, qbpar, NX + 1, cc * P:(cc + 1) * P],
                                              state[:, (cc + 1) % 2, :], start=True, stop=True)
                    mm.then_inc(b_Y, 1)
                if k is not None:
                    wait(pe, b_Gm, k)
                    wait(pe, b_S, (NC - 1) * bp[0] + max(c - 1, 0))
                    if c != 0:
                        pe.wait_ge(b_xdec, (NC - 1) * bp[0] + c)
                        nc.tensor.matmul(bank[5][:, P:P + DI], xB[:, qar, DI:DI + P], xdec[:, qar, :], start=True, stop=True)
                    b, bpar = bp
                    nc.tensor.matmul(bank[5][:, 0:P], xbcT[:, bpar, NX, tok], xbcT[:, bpar, NX + 1, tok],
                                     start=True, stop=True).then_inc(b_GS, 1)
                if r is not None:
                    rb_, rc = (bp[0], c - 2) if c >= 2 else (bp[0] - 1, NC - 2 + c)
                    rpar = bp[1] if c >= 2 else 1 - bp[1]
                    pe.wait_ge(b_yTe, r + 1)
                    for i in range(NX):
                        nc.tensor.matmul(bank[6][:, 2 * P:3 * P], ynT[:, i * P:(i + 1) * P],
                                         woB[:, bass.ds(rb_, 1), i, :].rearrange("p b d -> p (b d)"),
                                         start=(i == 0), stop=(i == NX - 1))
                    nc.tensor.matmul(bank[6][:, 3 * P:4 * P], hq[:, rpar, 1, rc * P:(rc + 1) * P],
                                     gad[:, bass.ds(rb_, 1), :].rearrange("p b d -> p (b d)"), start=True, stop=True
                                     ).then_inc(b_O, 1)
            run_b(pe, step)

            def phase_c(s):
                if inside(s, NB):
                    pe.wait_ge(c_xh, s + 1)
                    wait(pe, c_ev, s)
                    for c in range(NC):
                        mm = nc.tensor.transpose(bank[0][:, c * P:(c + 1) * P], xh[:, c * P:(c + 1) * P], ident)
                    mm.then_inc(c_T, 1)
                if inside(s - 1, NB):
                    pe.wait_ge(c_ev, s)
                    wait(pe, c_le, s - 1)
                    nc.tensor.matmul(bank[1][0:NE, :], wr_sb[:, :], hT[:, bass.ds(s - 1, 1), :].rearrange("p b t -> p (b t)"),
                                     start=True, stop=True).then_inc(c_lg, 1)
                if inside(s - 2, NB):
                    pe.wait_ge(c_le, s - 1)
                    wait(pe, c_lc, s - 2)
                    for c in range(NC):
                        mm = nc.tensor.matmul(bank[2][:, c * NE:(c + 1) * NE], lgT[:, c * P:(c + 1) * P], ident[0:NE, 0:NE],
                                              start=True, stop=True)
                    mm.then_inc(c_lT, 1)
            slots(pe, NB, 2, phase_c)

            pe.wait_ge(s_moe, 32)
            pe.wait_ge(s_rt, 3)

            def hidden(b, e):
                for k in range(NK):
                    wait(pe, d_g, NE * NK * b + NK * e + k - NK + 1)
                    nc.tensor.matmul(bank[h_bank[k]][:, :], w1_sb[:, e, k * P:(k + 1) * P], tokens(hT, b),
                                     start=True, stop=True).then_inc(d_h, 1)

            def down(b, e):
                wait(pe, d_ac, NE * b + e - 1)
                pe.wait_ge(d_g, NE * NK * b + NK * (e + 1))
                for c in range(NC):
                    o = bank[3 + e % 2][:, c * P:(c + 1) * P]
                    nc.tensor.matmul(o, ones[0:1, :], b2_row[:, e, :], start=True, stop=False)
                    for k in range(NK):
                        mm = nc.tensor.matmul(o, big[:, NK * (e % 2) + k, c * P:(c + 1) * P], w2_sb[:, e, k, :],
                                              start=False, stop=(k == NK - 1))
                mm.then_inc(d_o, 1)

            def experts(b):
                for e in range(NE + 1):
                    if e < NE:
                        hidden(b, e)
                    if e > 0:
                        down(b, e - 1)
            experts(0)
            with pe.Fori(1, NB) as b:
                experts(b)


INPUTS = ["x", "W_in", "W_z", "conv_w", "conv_b", "dt_bias", "A_log", "D_param", "norm_pre_w", "norm_gated_w", "W_out",
          "w_router", "w1", "b1", "w2", "b2", "c_in", "wmod"]
NAMES = {"x": "L0_attn_x", "W_in": "L0_attn_W_in", "W_z": "L0_attn_W_zxbcdt", "conv_w": "L0_attn_conv_w",
         "conv_b": "L0_attn_conv_b", "dt_bias": "L0_attn_dt_bias", "A_log": "L0_attn_A_log", "D_param": "L0_attn_D_param",
         "norm_pre_w": "L0_attn_norm_pre_w", "norm_gated_w": "L0_attn_norm_gated_w", "W_out": "L0_attn_W_out",
         "w_router": "L0_ffn_w_router", "w1": "L0_ffn_w1", "b1": "L0_ffn_b1", "w2": "L0_ffn_w2", "b2": "L0_ffn_b2",
         "c_in": "L0_c", "wmod": "L0_wmod"}


def constants(T):
    k, l = np.arange(P)[:, None], np.arange(P)[None, :]
    inv_freq = np.float32(1.0) / np.float32(10000.0) ** (np.arange(0, 8, 2, dtype=np.float32) / np.float32(8))
    ang = (np.arange(T, dtype=np.float32)[None, :] * inv_freq.astype(np.float32)[:, None]).astype(np.float32)
    cos = np.tile(np.cos(ang), (P // 4, 1))
    sin = np.tile(np.concatenate([-np.sin(ang), np.sin(ang)]), (P // 8, 1))
    return np.concatenate([k == l, k > l, k <= l, cos, sin], axis=1).astype(np.float32)


def kernel(**inputs):
    import concourse.bacc as bacc
    from concourse.bass_utils import run_bass_kernel_spmd

    nc = bacc.Bacc("TRN2", target_bir_lowering=False, num_devices=1)
    arrays = {n: np.ascontiguousarray(inputs[NAMES[n]]) for n in INPUTS}
    arrays["consts"] = constants(arrays["x"].shape[1])
    args = {n: nc.dram_tensor(n, a.shape, mybir.dt.from_np(a.dtype), kind="ExternalInput").ap() for n, a in arrays.items()}
    out = nc.dram_tensor("out", arrays["x"].shape, F32, kind="ExternalOutput").ap()
    build(nc, out=out, **args)
    r = run_bass_kernel_spmd(nc, [arrays], core_ids=[0])
    return r.results[0]["out"]
```

```python
import numpy as np
import concourse.bass as bass
from concourse import mybir
from contextlib import ExitStack

P = 128
F32 = mybir.dt.float32
ALU = mybir.AluOpType
ACT = mybir.ActivationFunctionType
AX = mybir.AxisListType.X
EPS = 1e-5
BIG = 1.0e30
TOPK = 2
I32, U32 = mybir.dt.int32, mybir.dt.uint32


def wait(eng, sem, value):
    if isinstance(value, int) and value <= 0:
        return
    eng.wait_ge(sem, value)


def slots(eng, n, lag, body):
    for s in range(lag):
        body(s)
    with eng.Fori(lag, n) as s:
        body(s)
    for s in range(n, n + lag):
        body(s)


def inside(i, n):
    return not isinstance(i, int) or 0 <= i < n


def build(nc, x, W_in, W_z, conv_w, conv_b, dt_bias, A_log, D_param, norm_pre_w, norm_gated_w, W_out,
          w_router, w1, b1, w2, b2, c_in, wmod, consts, out):
    NB, T, D = x.shape
    NC = T // P
    NT = NB * NC
    NX = norm_gated_w.shape[0] // P
    DI = NX * P
    NH = A_log.shape[0]
    HD = DI // NH
    NBLK = NX + 2
    KC = conv_w.shape[1]
    NE, _, HID = w1.shape
    NK = HID // P
    ZB, XB0, DT0 = 0, DI, DI + NBLK * P
    assert D == P and T == 512
    NTOK = NB * T
    REG = NTOK + P
    RING = 8
    TILES = -(-(TOPK * NTOK // P + NE - 1) // RING) * RING
    NDUM = RING
    RW = P + 2
    RID, RWT = P, P + 1
    assert TILES - TOPK * NTOK // P <= NDUM
    C = layout(NB, NC, NE, TILES, NDUM)
    rows_d = nc.dram_tensor("dispatched_rows", [NE * REG + NDUM * P, RW], F32, kind="Internal").ap()
    res_d = nc.dram_tensor("expert_results", [TOPK * NTOK + (NE + NDUM) * P, P], F32, kind="Internal").ap()
    mod_d = nc.dram_tensor("modulation_rows", [2, NB, P], F32, kind="Internal").ap()

    with ExitStack() as ctx:
        def sb(name, shape, dt=F32):
            return ctx.enter_context(nc.sbuf_tensor(name, shape, dt))

        def pb(name, shape, dt=F32):
            return ctx.enter_context(nc.psum_tensor(name, shape, dt))

        def sem(name):
            return ctx.enter_context(nc.semaphore(name))

        x_sb = sb("x_sb", [P, NB, NC, P])
        hold = sb("hold", [P, NB * TOPK * NC * RW])
        qT = hold[:, 0:NB * T].rearrange("p (b t) -> p b t", b=NB)
        hT = hold[:, NB * T:2 * NB * T].rearrange("p (b t) -> p b t", b=NB)
        xrow = hold[:, :].rearrange("p (b k c r) -> p b k c r", k=TOPK, c=NC, r=RW)
        res = hold[:, 0:2 * NB * T].rearrange("p (b k c d) -> p b k c d", k=TOPK, c=NC, d=P)
        w1_sb = sb("w1_sb", [P, NE, HID])
        w2_sb = sb("w2_sb", [P, NE, NK, P])
        cst = sb("cst", [P, C["all"].stop])
        ident, triS, triI = cst[:, 0:P], cst[:, P:2 * P], cst[:, 2 * P:3 * P]
        ropeC, ropeS = cst[:, 3 * P:3 * P + T], cst[:, 3 * P + T:3 * P + 2 * T]
        ones = sb("ones", [P, P])
        eps = sb("eps", [P, 1])
        rows = sb("rows", [64, P])
        NR = NE * NK + NBLK + NX + 1 + NB
        R_B1, R_CB, R_NG, R_NP, R_C = 0, NE * NK, NE * NK + NBLK, NE * NK + NBLK + NX, NE * NK + NBLK + NX + 1
        cols = sb("cols", [P, NR])
        small = sb("small", [1, 3 * NH])
        hb = sb("hb", [P, 3 * NH])
        negA = sb("negA", [P, NH])
        win = sb("win", [P, P])
        wqT = sb("wqT", [P, P])
        wqrT = sb("wqrT", [P, P])
        wdt_nat = sb("wdt_nat", [NH, P])
        wzT = sb("wzT", [P, DT0 + NH])
        wr_sb = sb("wr_sb", [P, NE])
        b2B = sb("b2B", [P, NE, P])
        modrow = sb("modrow", [NB, 2, P])
        cw = sb("cw", [P, NBLK, KC])
        cwh = sb("cwh", [P, NBLK, KC])
        cbh = sb("cbh", [P, NBLK])
        siluc = sb("siluc", [P, 3, NB])
        mod = sb("mod", [P, 6, NB])
        gsign = sb("gsign", [P, 2, NB])
        gabs = sb("gabs", [P, 2, NB])
        gad = sb("gad", [P, NB, P])
        gbd = sb("gbd", [P, P])
        woB = sb("woB", [P, NB, NX, P])
        gbB = sb("gbB", [P, NB, P])
        st6 = sb("st6", [P, NT, 6])
        mv = sb("mv", [P, 4, NT])
        lnv = sb("lnv", [P, NT])
        rstd = sb("rstd", [P, NT])
        dtr = sb("dtr", [P, NT, NH])
        dt_ = sb("dt_", [P, NT, NH])
        dtA = sb("dtA", [P, NT, NH])
        dec = sb("dec", [P, 3, NT * NH])
        dtdec = sb("dtdec", [P, NT, NH])
        big = sb("big", [P, 8, T])
        xh, xnT, t1, t2, sq, rb = (big[:, i, :] for i in range(6))
        hq = sb("hq", [P, 2, 2, T])
        xbcT = sb("xbcT", [P, 2, NBLK, T])
        wz_nat = xbcT[:, 0, 0:2, :].rearrange("p k (a d) -> p (k a) d", d=P)[:, 0:NX + NBLK, :]
        wmod_sb = xbcT[:, 1, 0:2, :].rearrange("p k t -> p (k t)")[:, 0:6 * P]
        acc = [big[:, j, :] for j in range(4)]
        cth = [sb("cth_a", [P, T])[:, :], sb("cth_b", [P, T])[:, :]]
        rhsL = [big[:, 4, :], big[:, 5, :]]
        E4 = [big[:, 6, :], big[:, 7, :]]
        M4 = [sb("M4a", [P, NH * P]), sb("M4b", [P, NH * P])]
        xB = sb("xB", [P, NC, DI + P])
        Gm = sb("Gm", [P, P])
        xdt = sb("xdt", [P, 2, DI])
        xdec = sb("xdec", [P, 2, DI])
        xD = sb("xD", [P, 2, DI])
        zth = sb("zth", [P, 2, DI])
        zs = sb("zs", [P, 2, DI])
        yo = sb("yo", [P, DI])
        yd = sb("yd", [P, DI])
        ys = sb("ys", [P, DI])
        yz = sb("yz", [P, 2, DI])
        junk = sb("junk", [P, DI])
        ynT = sb("ynT", [P, 2, DI])
        wout_nat = zs[:, 0, :]
        dtT = cth[1][0:NH, :]
        dts = xB[:, 0:2, :].rearrange("p c d -> p (c d)").rearrange("p (i n) -> p i n", i=6)
        state = sb("state", [P, 2, DI])
        sdec = sb("sdec", [P, DI])
        ss = sb("ss", [P, 2, 1])
        ms = sb("ms", [P, 2, 1])
        rg = sb("rg", [P, 2, 1])
        nhalf = sb("nhalf", [P, 1])
        xo = sb("xo", [P, P])
        xm, h2T = big[:, 1, :], big[:, 2, :]
        shB, scB = (xbcT[:, 0, 2 * i:2 * i + 2, :].rearrange("p k (a d) -> p (k a) d", d=P) for i in range(2))
        lg = sb("lg", [P, NC, NE])
        eq = sb("eq", [P, NC, NE])
        rest = sb("rest", [P, NC, NE])
        oh = sb("oh", [P, TOPK, NC, NE])
        top = sb("top", [P, TOPK, NC])
        pick = sb("pick", [P, TOPK, NC])
        ex = sb("ex", [P, NC, NE + 1])
        zsum = sb("zsum", [P, 2, NC])
        chosen = sb("chosen", [P, NC, NE])
        chosum = sb("chosum", [P, NE])
        before = sb("before", [P, NE])
        place = sb("place", [P, NC, NE])
        where = sb("where", [P, TOPK, NC, NE])
        posf = sb("posf", [P, TOPK, NC])
        pos = sb("pos", [P, NB, TOPK * NC], U32)
        tick = sb("tick", [P, 1])
        desc = sb("desc", [P, NE])
        count = sb("count", [P, NE])
        cmp_ = xB[0:1, 0:2, :].rearrange("p c d -> p (c d)")
        tiles_e = sb("tiles_e", [1, NE])
        ends_e = sb("ends_e", [1, NE])
        tl = cth[0][0:1, 0:4 * TILES].rearrange("p (i n) -> p i n", i=4)
        t_base = sb("t_base", [1, TILES], I32)
        t_exp = sb("t_exp", [1, TILES], I32)
        padpos = sb("padpos", [P, NE], U32)
        xt = sb("xt", [P, RING, RW])
        w1c = big[:, 0:2, :]
        w2c = big[:, 2:6, :]
        gT = big[:, 6:8, :]
        xtT = yz[:, 0, :].rearrange("p (i d) -> p i d", i=2)
        b1c = sb("b1c", [P, 4, NK])
        b2c = M4[0][:, :].rearrange("p (i d) -> p i d", i=4)
        yt = M4[1][:, :].rearrange("p (i d) -> p i d", i=4)
        idt = [sb(f"idt{i}", [P, 1], U32) for i in range(4)]

        bank = [pb(f"bank{i}", [P, 512]) for i in range(8)]

        s_cst, s_wts, s_x, s_moe = sem("constants_loaded"), sem("weights_loaded"), [sem(f"x_loaded_{b}") for b in range(NB)], sem("moe_weights_loaded")
        s_one, s_pre, s_prd, s_pra = sem("memsets_done"), sem("prep_pe"), sem("prep_dve"), sem("prep_act")
        s_gd, s_gm, s_ge = sem("gate_diag"), sem("gate_mm"), sem("gate_evac")
        s_ag = sem("stats_batch")
        s_st, s_stc, s_rs, s_rl2 = sem("stats_part"), sem("stats_done"), sem("rstd_ready"), sem("rstd_step")
        a_xh, a_T, a_ev, a_q, a_qr = sem("a_normalised"), sem("a_transposed"), sem("a_modulated"), sem("a_q"), sem("a_q_rot")
        a_t1, a_t2, a_rp, a_sq, a_n = sem("a_t1"), sem("a_t2"), sem("a_roped"), sem("a_squared"), sem("a_meansq")
        a_ln, a_ex, a_h = sem("a_ln"), sem("a_rms"), sem("a_h")
        a_d, a_de, a_dT, a_dc = sem("a_dt"), sem("a_dt_evac"), sem("a_dt_T"), sem("a_dt_done")
        s_da, s_dv, s_dp = sem("dt_act"), sem("dt_dve"), sem("dt_pe")
        s_hq = [sem("hq_even"), sem("hq_odd")]
        b_cv, b_acc, b_tap, b_tp, b_cth, b_cs = (sem("b_conv_proj"), sem("b_conv_first"), sem("b_conv_tap"),
                                                 sem("b_conv_sum"), sem("b_conv_tanh"), sem("b_conv_out"))
        b_T, b_Te, b_rl, b_L, b_E, b_z, b_th, b_zs = (sem("b_T"), sem("b_T_evac"), sem("b_rhsL"), sem("b_L"), sem("b_E"),
                                                      sem("b_z"), sem("b_z_tanh"), sem("b_zs"))
        b_St = sem("b_St")
        b_GS, b_Gm, b_M, b_xdt, b_xdec, b_xD = (sem("b_GS"), sem("b_Gm"), sem("b_M"), sem("b_xdt"), sem("b_xdec"), sem("b_xD"))
        b_sd, b_S, b_Y, b_yo, b_yd, b_ys, b_yz, b_ss = (sem("b_sdec"), sem("b_state"), sem("b_Y"), sem("b_yo"), sem("b_yd"),
                                                        sem("b_ysum"), sem("b_yz"), sem("b_ss"))
        b_ms, b_rg, b_yT, b_yTe, b_O, b_xo, b_x2 = (sem("b_ms"), sem("b_rg"), sem("b_yT"), sem("b_yT_evac"), sem("b_out"),
                                                    sem("b_xo"), sem("b_x2"))
        c_xh, c_T, c_ev, c_lg, c_le = (sem("c_normalised"), sem("c_transposed"), sem("c_columns"), sem("c_logits"),
                                       sem("c_logits_read"))
        s_link = sem("softplus_link")
        s_mr2 = sem("mod_rows_product")
        s_mr, s_md, s_mb = sem("mod_rows"), sem("mod_rows_stored"), sem("mod_rows_spread")
        s_dd, s_pd = sem("padding_ids"), sem("padding_tiles_stored")
        c_row, c_link, c_exi, c_exp, c_cho, c_rk, c_pos = (sem("c_rows"), sem("c_link"), sem("c_exp_in"), sem("c_exp"),
            sem("c_chosen"), sem("c_ranks"), sem("c_positions"))
        c_xm = sem("c_values")
        c_sc = sem("c_scattered")
        t_cnt, t_pad, t_tab, t_link, t_psc = (sem("t_counts"), sem("t_pad_ready"), sem("t_table"), sem("t_link"),
                                              sem("t_padding_scattered"))
        e_ld = [sem(f"e_loaded_{i}") for i in range(RING)]
        e_T, e_Te, e_w, e_h, e_g, e_o, e_y, e_id = (sem("e_transposed"), sem("e_columns"), sem("e_weights"), sem("e_hidden"),
                                                    sem("e_gelu"), sem("e_out"), sem("e_weighted"), sem("e_ids"))
        e_tk = sem("e_tick")
        e_sc = [sem(f"e_scattered_{i}") for i in range(4)]
        f_ld, f_x, f_link, d_st = [sem(f"f_loaded_{b}") for b in range(NB)], sem("f_x"), sem("f_link"), sem("stored")

        block = ctx.enter_context(nc.Block())

        LAG_Y, LAG_T, LAG_O = 2, 3, 4
        CONV0, CONV1, CONV2 = -6, -5, -4

        def at(b, par, c, lag):
            db, cc = (c - lag) // NC, (c - lag) % NC
            b2 = b + db
            if not inside(b2, NB):
                return None
            return NC * b2 + cc, b2, (par + db) % 2, cc

        def run_b(slot):
            def batch(b, par):
                for c in range(NC):
                    slot(b, par, c)
            for c in (NC - 2, NC - 1):
                slot(-2, 0, c)
            for b in (-1, 0, 1):
                batch(b, b % 2)
            yield batch
            for b in range(NB - 2, NB + 1):
                batch(b, b % 2)
            slot(NB + 1, (NB + 1) % 2, 0)

        def phase_b(eng, slot):
            for batch in run_b(slot):
                with eng.Fori(1, NB // 2 - 1) as j:
                    batch(2 * j, 0)
                    batch(2 * j + 1, 1)

        def tiles(eng, stage):
            for u in range(-RING, RING):
                stage(u, u % RING)
            with eng.Fori(1, TILES // RING - 1) as j:
                for u in range(RING):
                    stage(RING * j + u, u)
            for t in range(TILES - RING, TILES + RING):
                stage(t, t % RING)

        def tile(t, u, lag):
            return (t - lag, (u - lag) % RING) if inside(t - lag, TILES) else None

        def nth(t, u, ring):
            return t // ring if isinstance(t, int) else (t - u) * (RING // ring) // RING + u // ring

        LINKS = 19

        def by_head(ap):
            return ap.rearrange("p (h q) -> p h q", h=NH)

        def per_head(ap, n):
            return ap.unsqueeze(2).broadcast_to([P, NH, n])

        def tokens(ap, b):
            return ap[:, bass.ds(b, 1), :].rearrange("p b t -> p (b t)")

        @block.sync
        def _(sp):
            for dst, src in ((cst[:, :], consts), (rows[R_B1:R_CB, :], b1.rearrange("e (k p) -> (e k) p", p=P)),
                             (rows[R_CB:R_NG, :], conv_b.rearrange("(k p) -> k p", p=P)),
                             (rows[R_NG:R_NP, :], norm_gated_w.rearrange("(k p) -> k p", p=P)),
                             (rows[R_NP:R_C, :], norm_pre_w.rearrange("(k p) -> k p", p=P)),
                             (rows[R_C:NR, :], c_in)):
                sp.dma_start(dst, src).then_inc(s_cst, 16)
            for b in range(NB):
                sp.dma_start(x_sb[:, b, :, :], x[b, :, :].rearrange("(c p) d -> p c d", p=P)).then_inc(s_x[b], 16)
            sp.wait_ge(a_h, NB)

            def fetch(b, par):
                wait(sp, b_z, NC * (b - 1))
                wait(sp, b_O, NC * (b - 1))
                for i, src in enumerate((hT, qT)):
                    sp.dma_start(hq[:, par, i, :], tokens(src, b)).then_inc(s_hq[par], 16)
            for par in range(2):
                fetch(par, par)
            with sp.Fori(1, NB // 2) as j:
                for par in range(2):
                    fetch(2 * j + par, par)
            sp.wait_ge(s_md, 16)
            sp.wait_ge(b_Y, NC * (NB - 1))
            for i, dst in enumerate((shB, scB)):
                sp.dma_start(dst, mod_d[i:i + 1, :, :].broadcast_to([P, NB, P])).then_inc(s_mb, 16)

            sp.wait_ge(t_tab, 1)
            sp.wait_ge(c_sc, 16 * TOPK * NC * NB)
            sp.wait_ge(t_psc, 16 * NE)
            sp.wait_ge(s_pd, 16)

            def load(t, u):
                if i := tile(t, u, 0):
                    t, u = i
                    base = sp.value_load(t_base[0:1, bass.ds(t, 1)], min_val=0, max_val=NE * REG + (NDUM - 1) * P)
                    wait(sp, e_y, t - RING + 1)
                    sp.dma_start(xt[:, u, :], rows_d[bass.ds(base, P), :]).then_inc(e_ld[u], 16)
            tiles(sp, load)

            for i in range(4):
                sp.wait_ge(e_sc[i], 16 * TILES // 4)
            for b in range(NB):
                for k in range(TOPK):
                    sp.dma_start(res[:, b, k, :, :], res_d[k * NTOK + b * T:k * NTOK + (b + 1) * T, :].rearrange(
                        "(c p) d -> p c d", p=P)).then_inc(f_ld[b], 16)
            with sp.Fori(0, NB) as b:
                sp.wait_ge(f_x, b + 1)
                sp.dma_start(out[bass.ds(b, 1), :, :].rearrange("b (c p) d -> p (b c) d", p=P),
                             x_sb[:, bass.ds(b, 1), :, :].rearrange("p b c d -> p (b c) d")).then_inc(d_st, 16)
            sp.wait_ge(d_st, 16 * NB)

        @block.scalar
        def _(act):
            for dst, src in ((win[:, :], W_in[0:P, :]),
                             (wmod_sb[:, :], wmod), (small[:, 0:NH], dt_bias.rearrange("(a h) -> a h", a=1)),
                             (small[:, NH:2 * NH], A_log.rearrange("(a h) -> a h", a=1)),
                             (small[:, 2 * NH:], D_param.rearrange("(a h) -> a h", a=1)),
                             (wz_nat[:, :, :], W_z[0:DT0, :].rearrange("(k p) d -> p k d", p=P)),
                             (wdt_nat[:, :], W_z[DT0:DT0 + NH, :]), (wout_nat, W_out),
                             (cw[:, :, :], conv_w.rearrange("(k p) t -> p k t", p=P)),
                             (wr_sb[:, :], w_router), (b2B[:, :, :], b2.rearrange("(a e) d -> a e d", a=1).broadcast_to([P, NE, P]))):
                act.dma_start(dst, src).then_inc(s_wts, 16)
            act.dma_start(w1_sb[:, :, :], w1.rearrange("e d h -> d e h")).then_inc(s_moe, 16)
            act.dma_start(w2_sb[:, :, :, :], w2.rearrange("e (k p) d -> p e k d", p=P)).then_inc(s_moe, 16)
            act.preload_act_table_set("natural_log_exp_and_others")
            act.wait_ge(s_prd, 1)
            nc.scalar.activation(siluc[:, 0, :], cols[:, R_C:NR], ACT.Exp, scale=-1.0).then_inc(s_pra, 1)
            act.wait_ge(s_prd, 2)
            nc.scalar.activation(negA[:, :], hb[:, NH:2 * NH], ACT.Exp).then_inc(s_pra, 1)

            def gates(b):
                act.wait_ge(s_gm, b + 1)
                for k in range(NX):
                    nc.scalar.activation(woB[:, bass.ds(b, 1), k, :].rearrange("p b d -> p (b d)"), bank[5][:, k * P:(k + 1) * P],
                                         ACT.Copy, scale=cols[:, R_NG + k:R_NG + k + 1])
                nc.scalar.activation(gbB[:, bass.ds(b, 1), :].rearrange("p b d -> p (b d)"), bank[5][:, NX * P:(NX + 1) * P],
                                     ACT.Copy).then_inc(s_ge, 1)
            with act.Fori(0, NB) as b:
                gates(b)
            act.wait_ge(s_mr, 1)
            act.dma_start(mod_d.rearrange("i b d -> b i d"), modrow[:, :, :]).then_inc(s_md, 16)
            act.wait_ge(s_dd, 1)
            act.dma_start(rows_d[NE * REG:NE * REG + NDUM * P, :].rearrange("(n p) r -> p n r", p=P), xt[:, :, :]
                          ).then_inc(s_pd, 16)
            act.wait_ge(s_one, 1)
            act.wait_ge(s_stc, 1)
            nc.scalar.activation(lnv[:, :], mv[:, 1, :], ACT.Ln, bias=eps[:, 0:1]).then_inc(s_rl2, 1)
            act.wait_ge(s_rl2, 1)
            nc.scalar.activation(rstd[:, :], lnv[:, :], ACT.Exp, scale=-0.5).then_inc(s_rs, 1)

            def phase_a(s):
                if inside(s, NB):
                    act.wait_ge(a_T, s + 1)
                    wait(act, a_qr, s)
                    nc.scalar.activation(xnT, bank[0][:, :], ACT.Identity, scale=mod[:, 1, bass.ds(s, 1)],
                                         bias=mod[:, 0, bass.ds(s, 1)]).then_inc(a_ev, 1)
                if inside(s - 2, NB):
                    act.wait_ge(a_rp, s - 1)
                    wait(act, a_n, s - 2)
                    nc.scalar.activation(sq, qT[:, bass.ds(s - 2, 1), :].rearrange("p b t -> p (b t)"), ACT.Square
                                         ).then_inc(a_sq, 1)
                if inside(s - 3, NB):
                    act.wait_ge(a_n, s - 2)
                    wait(act, a_h, s - 3)
                    nc.scalar.activation(rb, bank[3][:, :], ACT.Ln, scale=1.0 / P, bias=eps[:, 0:1]).then_inc(a_ln, 1)
                    act.wait_ge(a_ln, s - 2)
                    nc.scalar.activation(rb, rb, ACT.Exp, scale=-0.5).then_inc(a_ex, 1)
                if inside(s - 4, NB):
                    act.wait_ge(a_d, s - 3)
                    wait(act, a_dT, s - 4)
                    nc.scalar.activation(dtT, bank[4][0:NH, :], ACT.Copy).then_inc(a_de, 1)
            slots(act, NB, 4, phase_a)
            act.wait_ge(s_dv, 2)
            nc.scalar.activation(dts[:, 2, :], dts[:, 1, :], ACT.Exp, scale=-1.0).then_inc(s_da, 1)
            act.wait_ge(s_dv, 3)
            nc.scalar.activation(dts[:, 4, :], dts[:, 3, :], ACT.Ln).then_inc(s_da, 1)
            act.wait_ge(s_dp, 1)
            nc.scalar.activation(dec[:, :, :].rearrange("p a n -> p (a n)"), bank[5][:, 0:3 * NT * NH], ACT.Exp).then_inc(s_da, 1)

            act.preload_act_table_set("exp_and_others")

            def slot(b, par, c):
                if i := at(b, par, c, 0):
                    k, _, _, cc = i
                    act.wait_ge(b_T, k + 1)
                    wait(act, b_xD, k - 3)
                    wait(act, b_St, k - 3)
                    nc.scalar.activation(xB[:, cc, :], bank[2][:, 0:DI + P], ACT.Copy).then_inc(b_Te, 1)
                if i := at(b, par, c, LAG_T):
                    k, _, _, cc = i
                    act.wait_ge(b_yT, k + 1)
                    wait(act, b_O, k - 1)
                    nc.scalar.activation(ynT[:, cc % 2, :], bank[6][:, 0:DI], ACT.Copy).then_inc(b_yTe, 1)
                    wait(act, b_ms, k - 1)
                    nc.scalar.activation(junk[:, :], yz[:, cc % 2, :], ACT.Square, scale=float(DI) ** -0.5,
                                         accum_out=ss[:, cc % 2, :]).then_inc(b_ss, 1)
                if i := at(b, par, c, 0):
                    k, _, _, cc = i
                    act.wait_ge(b_L, k + 1)
                    wait(act, b_M, k - 1)
                    nc.scalar.activation(E4[cc % 2], bank[3][:, :], ACT.Exp).then_inc(b_E, 1)
                    act.wait_ge(b_z, k + 1)
                    wait(act, b_zs, k - 1)
                    nc.scalar.activation(zth[:, cc % 2, :], bank[4][:, 0:DI], ACT.Tanh).then_inc(b_th, 1)
                if i := at(b, par, c, CONV0):
                    n, _, _, j = i
                    act.wait_ge(b_cv, n + 1)
                    wait(act, b_cs, n - 3)
                    nc.scalar.activation(acc[j], bank[j % 2][:, :], ACT.Identity, scale=cwh[:, j, KC - 1:KC],
                                         bias=cbh[:, j:j + 1]).then_inc(b_acc, 1)
                if i := at(b, par, c, CONV1):
                    n, _, _, j = i
                    act.wait_ge(b_tp, n + 1)
                    wait(act, b_cs, n - 1)
                    nc.scalar.activation(cth[j % 2], acc[j], ACT.Tanh).then_inc(b_cth, 1)
            phase_b(act, slot)

            act.preload_act_table_set("natural_log_exp_and_others")
            act.wait_ge(s_stc, 2)
            nc.scalar.activation(lnv[:, :], mv[:, 1, :], ACT.Ln, bias=eps[:, 0:1]).then_inc(s_rl2, 1)
            act.wait_ge(s_rl2, 2)
            nc.scalar.activation(rstd[:, :], lnv[:, :], ACT.Exp, scale=-0.5).then_inc(s_rs, 1)

            def phase_c(s):
                if inside(s, NB):
                    act.wait_ge(c_T, s + 1)
                    wait(act, c_lg, s)
                    nc.scalar.activation(h2T, bank[0][:, :], ACT.Copy).then_inc(c_ev, 1)
                    act.wait_ge(c_xm, s + 1)
                    nc.scalar.activation(xrow[:, bass.ds(s, 1), :, :, 0:P].rearrange("p b k c d -> p (b k) c d"),
                                         xm.rearrange("p (a c d) -> p a c d", a=1, c=NC).broadcast_to([P, TOPK, NC, P]),
                                         ACT.Copy).then_inc(c_row, 1)
                if inside(s - 1, NB):
                    act.wait_ge(c_exi, s)
                    nc.scalar.activation(ex[:, :, :], ex[:, :, :], ACT.Exp).then_inc(c_exp, 1)
            slots(act, NB, 1, phase_c)
            act.preload_act_table(ACT.Gelu_apprx_tanh)

            def gelus(t, u):
                if i := tile(t, u, 0):
                    t, u = i
                    act.wait_ge(e_h, t + 1)
                    wait(act, e_o, t - 1)
                    for k in range(NK):
                        ins = nc.scalar.activation(gT[:, u % 2, k * P:(k + 1) * P], bank[u % 2][:, k * P:(k + 1) * P],
                                                   ACT.Gelu_apprx_tanh, bias=b1c[:, u % 4, k:k + 1])
                    ins.then_inc(e_g, 1)
            tiles(act, gelus)

        @block.gpsimd
        def _(pool):
            nc.gpsimd.memset(ones[:, :], 1.0)
            nc.gpsimd.memset(before[:, :], 0.0)
            nc.gpsimd.memset(xt[:, :, :], 0.0)
            nc.gpsimd.memset(nhalf[:, :], -0.5)
            for e in range(NE):
                nc.gpsimd.memset(desc[:, e:e + 1], float(NE - e))
            nc.gpsimd.memset(eps[:, :], EPS).then_inc(s_one, 1)

            def phase_a(s):
                if inside(s - 1, NB):
                    pool.wait_ge(a_t2, s)
                    nc.gpsimd.tensor_tensor(qT[:, bass.ds(s - 1, 1), :].rearrange("p b t -> p (b t)"), t1, t2, ALU.add
                                            ).then_inc(a_rp, 1)
                if inside(s - 3, NB):
                    pool.wait_ge(a_ex, s - 2)
                    nc.gpsimd.tensor_tensor(hT[:, bass.ds(s - 3, 1), :].rearrange("p b t -> p (b t)"),
                                            qT[:, bass.ds(s - 3, 1), :].rearrange("p b t -> p (b t)"), rb, ALU.mult
                                            ).then_inc(a_h, 1)
            slots(pool, NB, 3, phase_a)
            pool.wait_ge(s_dv, 6)
            pool.wait_ge(s_prd, 3)

            def slot(b, par, c):
                if i := at(b, par, c, 0):
                    k, _, _, cc = i
                    wait(pool, b_L, k - 1)
                    nc.gpsimd.tensor_tensor(by_head(rhsL[cc % 2]), triI.unsqueeze(1).broadcast_to([P, NH, P]),
                                            per_head(dtA[:, bass.ds(k, 1), :].rearrange("p a h -> p (a h)"), P),
                                            ALU.mult).then_inc(b_rl, 1)
                if i := at(b, par, c, 1):
                    k, kb, _, cc = i
                    xv = by_head(xB[:, cc, 0:DI])
                    pool.wait_ge(b_Te, k + 1)
                    wait(pool, b_Y, k - 1)
                    nc.gpsimd.tensor_tensor(by_head(xdt[:, cc % 2, :]), xv,
                                            per_head(dt_[:, bass.ds(k, 1), :].rearrange("p a h -> p (a h)"), HD),
                                            ALU.mult).then_inc(b_xdt, 1)
                    if cc != NC - 1:
                        wait(pool, b_St, k - 1)
                        nc.gpsimd.tensor_tensor(by_head(xdec[:, cc % 2, :]), xv,
                                                per_head(dtdec[:, bass.ds(k, 1), :].rearrange("p a h -> p (a h)"), HD),
                                                ALU.mult).then_inc(b_xdec, 1)
                    wait(pool, b_yd, k - 1)
                    nc.gpsimd.tensor_tensor(by_head(xD[:, cc % 2, :]), xv, per_head(hb[:, 2 * NH:3 * NH], HD), ALU.mult
                                            ).then_inc(b_xD, 1)
                if i := at(b, par, c, LAG_Y):
                    k, kb, _, cc = i
                    if cc in (1, 2):
                        pool.wait_ge(b_S, (NC - 1) * kb + cc)
                        nc.gpsimd.tensor_tensor(by_head(sdec[:, :]), by_head(state[:, (cc + 1) % 2, :]),
                                                per_head(dec[:, 2, bass.ds(NH * k, NH)], HD), ALU.mult).then_inc(b_sd, 1)
                if i := at(b, par, c, LAG_T):
                    k, _, _, cc = i
                    q = cc % 2
                    pool.wait_ge(b_ss, k + 1)
                    wait(pool, b_rg, k - 1)
                    nc.gpsimd.tensor_tensor(ms[:, q, :], ss[:, q, :], eps[:, :], ALU.add).then_inc(b_ms, 1)
                    pool.wait_ge(b_ms, k + 1)
                    wait(pool, b_xo, k - 1)
                    nc.gpsimd.tensor_tensor(rg[:, q, :], ms[:, q, :], nhalf[:, :], ALU.pow).then_inc(b_rg, 1)
                if i := at(b, par, c, LAG_Y):
                    k, _, _, cc = i
                    pool.wait_ge(b_yd, k + 1)
                    wait(pool, b_yz, k)
                    nc.gpsimd.tensor_tensor(ys[:, :], yo[:, :], yd[:, :], ALU.add).then_inc(b_ys, 1)
            phase_b(pool, slot)

            for b in range(NB):
                pool.wait_ge(c_pos, b + 1)
                pool.wait_ge(c_row, b + 1)
                for n in range(TOPK * NC):
                    nc.gpsimd.indirect_dma_start(rows_d, bass.IndirectOffsetOnAxis(pos[:, b, n:n + 1], 0),
                                                 xrow[:, b, n // NC, n % NC, :], None).then_inc(c_sc, 16)
            pool.wait_ge(t_pad, 1)
            for e in range(NE):
                nc.gpsimd.indirect_dma_start(rows_d, bass.IndirectOffsetOnAxis(padpos[:, e:e + 1], 0), xt[:, e, :], None
                                             ).then_inc(t_psc, 16)

            def store(t, u):
                if i := tile(t, u, 1):
                    n, v = i
                    pool.wait_ge(e_id, n + 1)
                    pool.wait_ge(e_y, n + 1)
                    wait(pool, e_tk, n)
                    nc.gpsimd.tensor_tensor(tick[:, :], nhalf[:, :], nhalf[:, :], ALU.add).then_inc(e_tk, 1)
                    nc.gpsimd.indirect_dma_start(res_d, bass.IndirectOffsetOnAxis(idt[v % 4][:, 0:1], 0), yt[:, v % 4, :], None
                                                 ).then_inc(e_sc[v % 4], 16)
            tiles(pool, store)

        @block.vector
        def _(dve):
            dve.wait_ge(s_pre, 1)
            nc.vector.tensor_copy(cols[:, :], bank[0][:, 0:NR]).then_inc(s_prd, 1)
            dve.wait_ge(s_pre, 2)
            nc.vector.tensor_copy(hb[:, :], bank[1][:, 0:3 * NH]).then_inc(s_prd, 1)
            dve.wait_ge(s_prd, 2)
            dve.wait_ge(s_wts, 16 * 11)
            dve.wait_ge(s_pra, 2)
            nc.vector.tensor_scalar(negA[:, :], negA[:, :], -1.0, None, ALU.mult)
            nc.vector.tensor_scalar(cwh[:, :, :], cw[:, :, :], 0.5, None, ALU.mult)
            nc.vector.tensor_scalar(cbh[:, :], cols[:, R_CB:R_NG], 0.5, None, ALU.mult)
            nc.vector.tensor_scalar(siluc[:, 1, :], siluc[:, 0, :], 1.0, None, ALU.add).then_inc(s_prd, 1)
            dve.wait_ge(s_prd, 3)
            nc.vector.reciprocal(siluc[:, 2, :], siluc[:, 1, :]).then_inc(s_prd, 1)
            dve.wait_ge(s_prd, 4)
            nc.vector.tensor_tensor(siluc[:, 1, :], siluc[:, 2, :], cols[:, R_C:NR], ALU.mult).then_inc(s_prd, 1)
            dve.wait_ge(s_pre, 3)
            nc.vector.tensor_copy(wqT[:, :], bank[2][:, 0:P])
            sw = bank[2][:, 0:P].rearrange("p (h a i) -> p h a i", a=2, i=4)
            dst = wqrT[:, :].rearrange("p (h a i) -> p h a i", a=2, i=4)
            nc.vector.tensor_copy(dst[:, :, 0, :], sw[:, :, 1, :])
            nc.vector.tensor_copy(dst[:, :, 1, :], sw[:, :, 0, :]).then_inc(s_prd, 1)
            dve.wait_ge(s_pre, 4)
            npw = cols[:, R_NP:R_NP + 1]
            nc.vector.tensor_scalar(wzT[:, 0:DI], bank[3][:, 0:DI], npw, 0.5, ALU.mult, ALU.mult)
            nc.vector.tensor_scalar(wzT[:, DI:4 * P], bank[3][:, DI:4 * P], npw, None, ALU.mult)
            nc.vector.tensor_scalar(wzT[:, 4 * P:DT0 + NH], bank[4][:, 0:DT0 + NH - 4 * P], npw, None, ALU.mult).then_inc(s_prd, 1)
            dve.wait_ge(s_pre, 5)
            nc.vector.tensor_copy(mod[:, :, :].rearrange("p a b -> p (a b)"), bank[1][:, 64:64 + 6 * NB]).then_inc(s_prd, 1)
            dve.wait_ge(s_prd, 8)
            for i, g in enumerate((2, 5)):
                nc.vector.scalar_tensor_tensor(out=gabs[:, i, :], in0=mod[:, g, :], scalar=-1.0, in1=mod[:, g, :],
                                               op0=ALU.mult, op1=ALU.max)
                nc.vector.tensor_scalar(gsign[:, i, :], mod[:, g, :], 0.0, 2.0, ALU.is_ge, ALU.mult).then_inc(s_prd, 1)
            dve.wait_ge(s_prd, 10)
            nc.vector.tensor_scalar(gabs[:, :, :], gabs[:, :, :], 0.25, None, ALU.max)
            nc.vector.tensor_scalar(gsign[:, :, :], gsign[:, :, :], -1.0, None, ALU.add).then_inc(s_prd, 1)
            dve.wait_ge(s_prd, 11)
            for i, g in enumerate((2, 5)):
                nc.vector.tensor_tensor(mod[:, g, :], gabs[:, i, :], gsign[:, i, :], ALU.mult)
            for j in (1, 4):
                nc.vector.tensor_scalar(mod[:, j, :], mod[:, j, :], 1.0, None, ALU.add).then_inc(s_prd, 1)
            dve.wait_ge(s_prd, 13)

            dve.wait_ge(s_mr2, 1)
            nc.vector.tensor_copy(modrow[:, 0, :], bank[6][0:NB, 0:P])
            nc.vector.tensor_scalar(modrow[:, 1, :], bank[6][0:NB, P:2 * P], 1.0, None, ALU.add).then_inc(s_mr, 1)
            dve.wait_ge(s_one, 1)
            nc.vector.tensor_copy(xt[:, :, RID], cst[:, C["dumid"]]).then_inc(s_dd, 1)

            def gates(b):
                wait(dve, s_gm, b)
                nc.vector.tensor_scalar(gad[:, bass.ds(b, 1), :].rearrange("p b d -> p (b d)"), ident,
                                        mod[:, 2, bass.ds(b, 1)], None, ALU.mult)
                nc.vector.tensor_scalar(gbd[:, :], ident, mod[:, 5, bass.ds(b, 1)], None, ALU.mult).then_inc(s_gd, 1)
            gates(0)
            with dve.Fori(1, NB) as b:
                gates(b)

            def stats(b):
                for c in range(NC):
                    ins = nc.vector.bn_stats(st6[:, bass.ds(NC * b + c, 1), :].rearrange("p a m -> p (a m)"),
                                             x_sb[:, bass.ds(b, 1), c, :].rearrange("p b d -> p (b d)"))
                ins.then_inc(s_st, 1)

            def mean_var(n):
                dve.wait_ge(s_st, NB + (NT if n == 2 else 0))
                me, mo, qe, qo = (st6[:, :, i] for i in (1, 4, 2, 5))
                nc.vector.tensor_tensor(mv[:, 0, :], me, mo, ALU.add)
                nc.vector.tensor_tensor(mv[:, 2, :], me, mo, ALU.subtract)
                nc.vector.tensor_tensor(mv[:, 3, :], qe, qo, ALU.add).then_inc(s_ag, 1)
                dve.wait_ge(s_ag, 2 * n - 1)
                nc.vector.tensor_scalar(mv[:, 0, :], mv[:, 0, :], 0.5, None, ALU.mult)
                nc.vector.scalar_tensor_tensor(out=mv[:, 2, :], in0=mv[:, 2, :], scalar=0.25, in1=mv[:, 2, :],
                                               op0=ALU.mult, op1=ALU.mult).then_inc(s_ag, 1)
                dve.wait_ge(s_ag, 2 * n)
                nc.vector.scalar_tensor_tensor(out=mv[:, 1, :], in0=mv[:, 3, :], scalar=1.0 / P, in1=mv[:, 2, :],
                                               op0=ALU.mult, op1=ALU.add).then_inc(s_stc, 1)
                dve.wait_ge(s_stc, n)

            for b in range(NB):
                dve.wait_ge(s_x[b], 16)
                stats(b)
            mean_var(1)

            def normalise(b):
                for c in range(NC):
                    ins = nc.vector.tensor_scalar(xh[:, c * P:(c + 1) * P],
                                                  x_sb[:, bass.ds(b, 1), c, :].rearrange("p b d -> p (b d)"),
                                                  mv[:, 0, bass.ds(NC * b + c, 1)],
                                                  rstd[:, bass.ds(NC * b + c, 1)], ALU.subtract, ALU.mult)
                return ins

            dve.wait_ge(s_rs, 1)

            def phase_a(s):
                if inside(s, NB):
                    wait(dve, a_T, s)
                    normalise(s).then_inc(a_xh, 1)
                if inside(s - 1, NB):
                    dve.wait_ge(a_q, s)
                    wait(dve, a_rp, s - 1)
                    nc.vector.tensor_tensor(t1, bank[1][:, :], ropeC, ALU.mult).then_inc(a_t1, 1)
                    dve.wait_ge(a_qr, s)
                    nc.vector.tensor_tensor(t2, bank[2][:, :], ropeS, ALU.mult).then_inc(a_t2, 1)
                if inside(s - 5, NB):
                    dve.wait_ge(a_dT, s - 4)
                    nc.vector.tensor_copy(dtr[:, bass.ds(NC * (s - 5), NC), :].rearrange("p c h -> p (c h)"),
                                          bank[5][:, 0:NC * NH]).then_inc(a_dc, 1)
            slots(dve, NB, 5, phase_a)

            dve.wait_ge(a_dc, NB)
            v, av, u, w, lw, tmp = (dts[:, i, :] for i in range(6))
            nc.vector.tensor_tensor(v.rearrange("p (a h) -> p a h", h=NH), dtr[:, :, :],
                                    hb[:, 0:NH].unsqueeze(1).broadcast_to([P, NT, NH]), ALU.add).then_inc(s_dv, 1)
            dve.wait_ge(s_dv, 1)
            nc.vector.scalar_tensor_tensor(out=av, in0=v, scalar=-1.0, in1=v, op0=ALU.mult, op1=ALU.max).then_inc(s_dv, 1)
            dve.wait_ge(s_da, 1)
            nc.vector.tensor_scalar(w, u, 1.0, None, ALU.add).then_inc(s_dv, 1)
            chain = [0]

            def link(ins):
                chain[0] += 1
                ins.then_inc(s_link, 1)
                dve.wait_ge(s_link, chain[0])
            link(nc.vector.tensor_scalar(tmp, u, -0.25, 1.0 / 3, ALU.mult, ALU.add))
            link(nc.vector.tensor_tensor(tmp, tmp, u, ALU.mult))
            link(nc.vector.tensor_scalar(tmp, tmp, -1.0, 0.5, ALU.mult, ALU.add))
            link(nc.vector.tensor_tensor(tmp, tmp, u, ALU.mult))
            link(nc.vector.tensor_scalar(tmp, tmp, -1.0, 1.0, ALU.mult, ALU.add))
            link(nc.vector.tensor_tensor(tmp, tmp, u, ALU.mult))
            dve.wait_ge(s_da, 2)
            link(nc.vector.tensor_tensor(lw, lw, tmp, ALU.subtract))
            link(nc.vector.scalar_tensor_tensor(out=lw, in0=u, scalar=1.0 / 64, in1=lw, op0=ALU.is_ge, op1=ALU.mult))
            link(nc.vector.tensor_tensor(tmp, tmp, lw, ALU.add))
            dtf = dt_[:, :, :].rearrange("p a h -> p (a h)")
            link(nc.vector.scalar_tensor_tensor(out=dtf, in0=v, scalar=0.0, in1=tmp, op0=ALU.max, op1=ALU.add))
            nc.vector.tensor_tensor(dtA[:, :, :], dt_[:, :, :], negA[:, :].unsqueeze(1).broadcast_to([P, NT, NH]),
                                    ALU.mult).then_inc(s_dv, 1)
            dve.wait_ge(s_da, 3)
            nc.vector.tensor_tensor(dtdec[:, :, :].rearrange("p a h -> p (a h)"), dtf, dec[:, 0, :], ALU.mult).then_inc(s_dv, 1)
            dve.wait_ge(s_dv, 5)
            nc.vector.memset(state[:, :, :], 0.0).then_inc(s_dv, 1)

            def slot(b, par, c):
                if i := at(b, par, c, CONV2):
                    n, bw, wpar, j = i
                    dve.wait_ge(b_cth, n + 1)
                    wait(dve, b_T if j < NX else b_GS, NC * (bw - 1))
                    if j == NX + 1:
                        wait(dve, b_Y, NC * (bw - 1))
                    nc.vector.scalar_tensor_tensor(out=xbcT[:, wpar, j, :], in0=cth[j % 2], scalar=1.0, in1=acc[j],
                                                   op0=ALU.add, op1=ALU.mult).then_inc(b_cs, 1)
                if i := at(b, par, c, 1):
                    k, _, _, cc = i
                    dve.wait_ge(b_GS, k + 1)
                    nc.vector.tensor_tensor(Gm[:, :], bank[5][:, 0:P], triI, ALU.mult).then_inc(b_Gm, 1)
                if i := at(b, par, c, 1):
                    k, _, _, cc = i
                    q = cc % 2
                    dve.wait_ge(b_th, k + 1)
                    wait(dve, b_yz, k - 1)
                    nc.vector.scalar_tensor_tensor(out=zs[:, q, :], in0=zth[:, q, :], scalar=1.0, in1=bank[4][:, 0:DI],
                                                   op0=ALU.add, op1=ALU.mult).then_inc(b_zs, 1)
                    dve.wait_ge(b_E, k + 1)
                    dve.wait_ge(b_Gm, k + 1)
                    wait(dve, b_Y, k - 1)
                    nc.vector.tensor_tensor(by_head(M4[q][:, :]), by_head(E4[q]),
                                            Gm[:, :].unsqueeze(1).broadcast_to([P, NH, P]), ALU.mult).then_inc(b_M, 1)
                if i := at(b, par, c, LAG_Y):
                    k, kb, _, cc = i
                    dve.wait_ge(b_Y, k + 1)
                    wait(dve, b_ys, k)
                    if cc:
                        nc.vector.tensor_tensor(by_head(yo[:, :]), by_head(bank[7][:, DI:2 * DI]),
                                                per_head(dec[:, 1, bass.ds(NH * k, NH)], HD), ALU.mult)
                    else:
                        nc.vector.memset(yo[:, :], 0.0)
                    dve.wait_ge(b_xD, k + 1)
                    nc.vector.tensor_tensor(yd[:, :], bank[7][:, 0:DI], xD[:, cc % 2, :], ALU.add).then_inc(b_yd, 1)
                    if cc != NC - 1:
                        dve.wait_ge(b_St, k + 1)
                    if cc == 0:
                        nc.vector.tensor_copy(state[:, 0, :], bank[5][:, P:P + DI]).then_inc(b_S, 1)
                    elif cc != NC - 1:
                        dve.wait_ge(b_sd, (NC - 2) * kb + cc)
                        nc.vector.tensor_tensor(state[:, cc % 2, :], sdec[:, :], bank[5][:, P:P + DI], ALU.add).then_inc(b_S, 1)
                if i := at(b, par, c, CONV1):
                    n, _, _, j = i
                    dve.wait_ge(b_acc, n + 1)
                    for t in range(1, KC):
                        ins = nc.vector.scalar_tensor_tensor(out=acc[j][:, t:T], in0=bank[j % 2][:, 0:T - t],
                                                             scalar=cwh[:, j, KC - 1 - t:KC - t], in1=acc[j][:, t:T],
                                                             op0=ALU.mult, op1=ALU.add)
                        if t < KC - 1:
                            ins.then_inc(b_tap, 1)
                            dve.wait_ge(b_tap, (KC - 2) * n + t)
                    ins.then_inc(b_tp, 1)
                if i := at(b, par, c, LAG_Y):
                    k, _, _, cc = i
                    q = cc % 2
                    dve.wait_ge(b_ys, k + 1)
                    wait(dve, b_yT, k - 1)
                    wait(dve, b_ss, k - 1)
                    nc.vector.tensor_tensor(yz[:, q, :], ys[:, :], zs[:, q, :], ALU.mult).then_inc(b_yz, 1)
                if i := at(b, par, c, LAG_O):
                    k, _, _, cc = i
                    dve.wait_ge(b_O, k + 1)
                    dve.wait_ge(b_rg, k + 1)
                    xr = x_sb[:, :, :, :].rearrange("p b c d -> p (b c) d")[:, bass.ds(k, 1), :].rearrange("p a d -> p (a d)")
                    nc.vector.scalar_tensor_tensor(out=xo[:, :], in0=bank[6][:, 2 * P:3 * P], scalar=rg[:, cc % 2, 0:1],
                                                   in1=xr, op0=ALU.mult, op1=ALU.add).then_inc(b_xo, 1)
                    dve.wait_ge(b_xo, k + 1)
                    nc.vector.tensor_tensor(xr, xo[:, :], bank[6][:, 3 * P:4 * P], ALU.add).then_inc(b_x2, 1)
                if i := at(b, par, c, LAG_O + 1):
                    k, _, _, cc = i
                    dve.wait_ge(b_x2, k + 1)
                    nc.vector.bn_stats(st6[:, bass.ds(k, 1), :].rearrange("p a m -> p (a m)"),
                                       x_sb[:, :, :, :].rearrange("p b c d -> p (b c) d")[:, bass.ds(k, 1), :].rearrange(
                                           "p a d -> p (a d)")).then_inc(s_st, 1)
            phase_b(dve, slot)

            mean_var(2)
            dve.wait_ge(s_rs, 2)
            dve.wait_ge(s_mb, 32)

            def route(b):
                n = [0]

                def link(ins):
                    n[0] += 1
                    ins.then_inc(c_link, 1)
                    dve.wait_ge(c_link, LINKS * b + n[0])

                def bc(a):
                    return a.unsqueeze(2).broadcast_to([P, NC, NE])
                dsc = desc[:, :].unsqueeze(1).broadcast_to([P, NC, NE])

                def first_of(src, i):
                    link(nc.vector.tensor_reduce(top[:, i, :], src, AX, ALU.max))
                    link(nc.vector.tensor_tensor(eq[:, :, :], src, bc(top[:, i, :]), ALU.is_equal))
                    link(nc.vector.tensor_tensor(eq[:, :, :], eq[:, :, :], dsc, ALU.mult))
                    link(nc.vector.tensor_reduce(pick[:, i, :], eq[:, :, :], AX, ALU.max))
                    link(nc.vector.tensor_tensor(oh[:, i, :, :], eq[:, :, :], bc(pick[:, i, :]), ALU.is_equal))
                dve.wait_ge(c_lg, b + 1)
                nc.vector.tensor_copy(lg[:, :, :].rearrange("p c e -> p (c e)"), bank[1][:, 0:NC * NE]).then_inc(c_le, 1)
                dve.wait_ge(c_le, b + 1)
                first_of(lg[:, :, :], 0)
                link(nc.vector.scalar_tensor_tensor(out=rest[:, :, :], in0=oh[:, 0, :, :], scalar=-BIG, in1=lg[:, :, :],
                                                    op0=ALU.mult, op1=ALU.add))
                first_of(rest[:, :, :], 1)
                nc.vector.tensor_tensor(chosen[:, :, :], oh[:, 0, :, :], oh[:, 1, :, :], ALU.add).then_inc(c_cho, 1)
                nc.vector.tensor_tensor(ex[:, :, NE], top[:, 1, :], top[:, 0, :], ALU.subtract)
                nc.vector.tensor_tensor(ex[:, :, 0:NE], lg[:, :, :], bc(top[:, 0, :]), ALU.subtract).then_inc(c_exi, 1)
                dve.wait_ge(c_cho, b + 1)
                link(nc.vector.tensor_reduce(chosum[:, :], chosen[:, :, :].rearrange("p c e -> p e c"), AX, ALU.add))
                dve.wait_ge(c_exp, b + 1)
                link(nc.vector.tensor_reduce(zsum[:, 0, :], ex[:, :, 0:NE], AX, ALU.add))
                link(nc.vector.reciprocal(zsum[:, 1, :], zsum[:, 0, :]))

                def column(k, i):
                    return xrow[:, bass.ds(b, 1), k, :, i].rearrange("p b c -> p (b c)")
                nc.vector.tensor_copy(column(0, RWT), zsum[:, 1, :])
                nc.vector.tensor_tensor(column(1, RWT), ex[:, :, NE], zsum[:, 1, :], ALU.mult)
                for k in range(TOPK):
                    ins = nc.vector.tensor_copy(column(k, RID), cst[:, C["ids"]].rearrange("p (b n) -> p b n", b=NB)[
                        :, bass.ds(b, 1), k * NC:(k + 1) * NC].rearrange("p b c -> p (b c)"))
                link(ins)
                dve.wait_ge(c_rk, b + 1)
                link(nc.vector.tensor_tensor(before[:, :], before[:, :], chosum[:, :], ALU.add))
                link(nc.vector.tensor_tensor(place[:, :, :], bank[2][:, 0:NC * NE].rearrange("p (c e) -> p c e", e=NE),
                                             cst[:, C["region"]].unsqueeze(1).broadcast_to([P, NC, NE]), ALU.add))
                for k in range(TOPK):
                    ins = nc.vector.tensor_tensor(where[:, k, :, :], oh[:, k, :, :], place[:, :, :], ALU.mult)
                link(ins)
                nc.vector.tensor_reduce(posf[:, :, :].rearrange("p k c -> p (k c)"),
                                        where[:, :, :, :].rearrange("p k c e -> p (k c) e"), AX, ALU.add).then_inc(c_link, 1)
                n[0] += 1
                assert n[0] == LINKS, n[0]
                dve.wait_ge(c_link, LINKS * (b + 1))
                nc.vector.tensor_copy(pos[:, bass.ds(b, 1), :].rearrange("p b n -> p (b n)"),
                                      posf[:, :, :].rearrange("p k c -> p (k c)")).then_inc(c_pos, 1)

            def phase_c(s):
                if inside(s, NB):
                    wait(dve, c_T, s)
                    wait(dve, c_row, s)
                    normalise(s).then_inc(c_xh, 1)
                    dve.wait_ge(c_xh, 2 * s + 1)
                    x3, m3 = (a.rearrange("p (c d) -> p c d", c=NC) for a in (xh, xm))
                    nc.vector.tensor_tensor(x3, x3, scB[:, bass.ds(s, 1), :].broadcast_to([P, NC, P]), ALU.mult
                                            ).then_inc(c_xh, 1)
                    dve.wait_ge(c_xh, 2 * s + 2)
                    nc.vector.tensor_tensor(m3, x3, shB[:, bass.ds(s, 1), :].broadcast_to([P, NC, P]), ALU.add
                                            ).then_inc(c_xm, 1)
                    wait(dve, c_xm, s + 1)
                if inside(s - 1, NB):
                    route(s - 1)
            slots(dve, NB, 1, phase_c)

            nlink = [0]

            def link(ins):
                nlink[0] += 1
                ins.then_inc(t_link, 1)
                dve.wait_ge(t_link, nlink[0])
            dve.wait_ge(t_cnt, 1)
            link(nc.vector.tensor_copy(count[:, :], bank[2][:, 64:64 + NE]))
            nc.vector.tensor_tensor(padpos[:, :], count[:, :], cst[:, C["padpos"]], ALU.add)
            dve.wait_ge(s_pd, 16)
            nc.vector.tensor_copy(xt[:, :, RID], cst[:, C["padid"]]).then_inc(t_pad, 1)

            def wide(ap, n, e):
                return ap.unsqueeze(1).broadcast_to([1, n, e])

            def long(ap, n, e):
                return ap.unsqueeze(2).broadcast_to([1, n, e])

            def cells(n, e):
                return cmp_[0:1, 0:n * e].rearrange("p (n e) -> p n e", e=e)
            tile_no, E_, start, base = cst[0:1, C["tile"]], tl[:, 0, :], tl[:, 1, :], tl[:, 2, :]
            link(nc.vector.tensor_tensor(cells(NE, NT), long(count[0:1, :], NE, NT), wide(cst[0:1, C["steps"]], NE, NT), ALU.is_gt))
            link(nc.vector.tensor_reduce(tiles_e[:, :], cells(NE, NT), AX, ALU.add))
            link(nc.vector.tensor_tensor(cells(NE, NE), cst[0:1, C["upto"]].rearrange("p (n e) -> p n e", e=NE),
                                         wide(tiles_e[:, :], NE, NE), ALU.mult))
            link(nc.vector.tensor_reduce(ends_e[:, :], cells(NE, NE), AX, ALU.add))
            link(nc.vector.tensor_tensor(cells(TILES, NE), long(tile_no, TILES, NE), wide(ends_e[:, :], TILES, NE), ALU.is_ge))
            link(nc.vector.tensor_reduce(E_, cells(TILES, NE), AX, ALU.add))
            link(nc.vector.tensor_tensor(cells(TILES, NE), cells(TILES, NE), wide(tiles_e[:, :], TILES, NE), ALU.mult))
            link(nc.vector.tensor_reduce(start, cells(TILES, NE), AX, ALU.add))
            link(nc.vector.tensor_tensor(base, tile_no, start, ALU.subtract))
            link(nc.vector.tensor_scalar(base, base, float(P), None, ALU.mult))
            link(nc.vector.scalar_tensor_tensor(out=base, in0=E_, scalar=float(REG), in1=base, op0=ALU.mult, op1=ALU.add))
            nc.vector.tensor_copy(t_base[:, :], base)
            link(nc.vector.tensor_scalar(E_, E_, float(NE - 1), None, ALU.min))
            nc.vector.tensor_copy(t_exp[:, :], E_).then_inc(t_tab, 1)
            dve.wait_ge(t_tab, 1)

            def experts(t, u):
                if i := tile(t, u, -1):
                    n, v = i
                    e = dve.value_load(t_exp[0:1, bass.ds(n, 1)], min_val=0, max_val=NE - 1)
                    wait(dve, e_h, n - 1)
                    nc.vector.tensor_copy(w1c[:, v % 2, :], w1_sb[:, bass.ds(e, 1), :].rearrange("p e h -> p (e h)"))
                    wait(dve, e_o, n - 3)
                    nc.vector.tensor_copy(w2c[:, v % 4, :], w2_sb[:, bass.ds(e, 1), :, :].rearrange("p e k d -> p (e k d)"))
                    nc.vector.tensor_copy(b1c[:, v % 4, :], cols[:, bass.ds(NK * e + R_B1, NK)]).then_inc(e_w, 1)
                    dve.wait_ge(e_ld[v], 16 * (nth(n, v, RING) + 1))
                    wait(dve, e_y, n - 3)
                    nc.vector.tensor_scalar(b2c[:, v % 4, :], b2B[:, bass.ds(e, 1), :].rearrange("p e d -> p (e d)"),
                                            xt[:, v, RWT:RWT + 1], None, ALU.mult)
                    wait(dve, e_sc[v % 4], 16 * nth(n, v, 4))
                    nc.vector.tensor_copy(idt[v % 4][:, :], xt[:, v, RID:RID + 1]).then_inc(e_id, 1)
                    dve.wait_ge(e_T, n + 1)
                    nc.vector.tensor_copy(xtT[:, v % 2, :], bank[2 + v % 2][:, 0:P]).then_inc(e_Te, 1)
                if i := tile(t, u, 1):
                    n, v = i
                    dve.wait_ge(e_o, n + 1)
                    dve.wait_ge(e_Te, n + 1)
                    wait(dve, e_sc[v % 4], 16 * nth(n, v, 4))
                    nc.vector.scalar_tensor_tensor(out=yt[:, v % 4, :], in0=bank[4 + v % 2][:, 0:P], scalar=xt[:, v, RWT:RWT + 1],
                                                   in1=b2c[:, v % 4, :], op0=ALU.mult, op1=ALU.add).then_inc(e_y, 1)
            tiles(dve, experts)

            for b in range(NB):
                dve.wait_ge(f_ld[b], 16 * TOPK)
                r0, r1 = res[:, b, 0, :, :], res[:, b, 1, :, :]
                nc.vector.tensor_tensor(r0, r0, r1, ALU.add).then_inc(f_link, 1)
                dve.wait_ge(f_link, 2 * b + 1)
                nc.vector.tensor_tensor(r1, r0, gbB[:, b:b + 1, :].broadcast_to([P, NC, P]), ALU.mult).then_inc(f_link, 1)
                dve.wait_ge(f_link, 2 * b + 2)
                nc.vector.tensor_tensor(x_sb[:, b, :, :], x_sb[:, b, :, :], r1, ALU.add).then_inc(f_x, 1)

        @block.tensor
        def _(pe):
            pe.wait_ge(s_cst, 16 * 6)
            nc.tensor.transpose(bank[0][:, 0:NR], rows[0:NR, :], ident[0:NR, 0:NR]).then_inc(s_pre, 1)
            pe.wait_ge(s_wts, 16 * 11)
            pe.wait_ge(s_one, 1)
            nc.tensor.matmul(bank[1][:, 0:3 * NH], ones[0:1, :], small[:, :], start=True, stop=True).then_inc(s_pre, 1)
            nc.tensor.transpose(bank[2][:, 0:P], win[:, :], ident).then_inc(s_pre, 1)
            for j in range(NX + NBLK):
                nc.tensor.transpose(bank[3 + j // 4][:, (j % 4) * P:(j % 4 + 1) * P], wz_nat[:, j, :], ident)
            nc.tensor.transpose(bank[4][:, 2 * P:2 * P + NH], wdt_nat[:, :], ident[0:NH, 0:NH]).then_inc(s_pre, 1)
            pe.wait_ge(s_prd, 5)
            for j in range(6):
                mm = nc.tensor.matmul(bank[1][:, 64 + j * NB:64 + (j + 1) * NB], wmod_sb[:, j * P:(j + 1) * P], siluc[:, 1, :],
                                      start=True, stop=True)
            mm.then_inc(s_pre, 1)
            nc.tensor.matmul(bank[6][0:NB, 0:2 * P], siluc[:, 1, :], wmod_sb[:, 3 * P:5 * P], start=True, stop=True
                             ).then_inc(s_mr2, 1)

            def gates(b):
                pe.wait_ge(s_gd, b + 1)
                wait(pe, s_ge, b)
                for k in range(NX):
                    nc.tensor.matmul(bank[5][:, k * P:(k + 1) * P], wout_nat[:, k * P:(k + 1) * P],
                                     gad[:, bass.ds(b, 1), :].rearrange("p b d -> p (b d)"), start=True, stop=True)
                nc.tensor.matmul(bank[5][:, NX * P:(NX + 1) * P], ones[:, :], gbd[:, :], start=True, stop=True).then_inc(s_gm, 1)
            gates(0)
            with pe.Fori(1, NB) as b:
                gates(b)
            pe.wait_ge(s_prd, 8)

            def phase_a(s):
                if inside(s, NB):
                    pe.wait_ge(a_xh, s + 1)
                    wait(pe, a_ev, s)
                    for c in range(NC):
                        mm = nc.tensor.transpose(bank[0][:, c * P:(c + 1) * P], xh[:, c * P:(c + 1) * P], ident)
                    mm.then_inc(a_T, 1)
                if inside(s - 1, NB):
                    pe.wait_ge(a_ev, s)
                    wait(pe, a_t1, s - 1)
                    nc.tensor.matmul(bank[1][:, :], wqT[:, :], xnT, start=True, stop=True).then_inc(a_q, 1)
                    wait(pe, a_t2, s - 1)
                    nc.tensor.matmul(bank[2][:, :], wqrT[:, :], xnT, start=True, stop=True).then_inc(a_qr, 1)
                if inside(s - 2, NB):
                    pe.wait_ge(a_sq, s - 1)
                    wait(pe, a_ln, s - 2)
                    nc.tensor.matmul(bank[3][:, :], ones[:, :], sq, start=True, stop=True).then_inc(a_n, 1)
                if inside(s - 4, NB):
                    pe.wait_ge(a_h, s - 3)
                    wait(pe, a_de, s - 4)
                    nc.tensor.matmul(bank[4][0:NH, :], wzT[:, DT0:DT0 + NH],
                                     hT[:, bass.ds(s - 4, 1), :].rearrange("p b t -> p (b t)"), start=True, stop=True
                                     ).then_inc(a_d, 1)
                if inside(s - 5, NB):
                    pe.wait_ge(a_de, s - 4)
                    wait(pe, a_dc, s - 5)
                    for c in range(NC):
                        mm = nc.tensor.matmul(bank[5][:, c * NH:(c + 1) * NH], dtT[:, c * P:(c + 1) * P], ident[0:NH, 0:NH],
                                              start=True, stop=True)
                    mm.then_inc(a_dT, 1)
            pe.wait_ge(s_ge, NB)
            slots(pe, NB, 5, phase_a)
            pe.wait_ge(s_dv, 4)
            dA = dtA[:, :, :].rearrange("p a h -> p (a h)")
            for i, m in enumerate((triS, triI, ones[:, :])):
                mm = nc.tensor.matmul(bank[5][:, i * NT * NH:(i + 1) * NT * NH], m, dA, start=True, stop=True)
            mm.then_inc(s_dp, 1)

            def slot(b, par, c):
                if i := at(b, par, c, LAG_Y):
                    k, kb, kpar, cc = i
                    q = cc % 2
                    pe.wait_ge(b_M, k + 1)
                    pe.wait_ge(b_xdt, k + 1)
                    wait(pe, b_yd, k)
                    for h in range(NH):
                        mm = nc.tensor.matmul(bank[7][:, h * HD:(h + 1) * HD], M4[q][:, h * P:(h + 1) * P],
                                              xdt[:, q, h * HD:(h + 1) * HD], start=True, stop=True)
                    if cc:
                        pe.wait_ge(b_S, (NC - 1) * kb + cc)
                        mm = nc.tensor.matmul(bank[7][:, DI:2 * DI], xbcT[:, kpar, NX + 1, cc * P:(cc + 1) * P],
                                              state[:, (cc + 1) % 2, :], start=True, stop=True)
                    mm.then_inc(b_Y, 1)
                    wait(pe, b_Gm, k + 1)
                    wait(pe, b_S, (NC - 1) * kb + cc)
                    if cc != NC - 1:
                        pe.wait_ge(b_xdec, (NC - 1) * kb + cc + 1)
                        mm = nc.tensor.matmul(bank[5][:, P:P + DI], xB[:, cc, DI:DI + P], xdec[:, q, :], start=True, stop=True)
                        mm.then_inc(b_St, 1)
                    else:
                        pe.sem_inc(b_St, 1)
                if i := at(b, par, c, 1):
                    k, kb, kpar, cc = i
                    wait(pe, b_Gm, k)
                    tok = slice(cc * P, (cc + 1) * P)
                    nc.tensor.matmul(bank[5][:, 0:P], xbcT[:, kpar, NX, tok], xbcT[:, kpar, NX + 1, tok],
                                     start=True, stop=True).then_inc(b_GS, 1)
                if i := at(b, par, c, 0):
                    k, kb, kpar, cc = i
                    tok = slice(cc * P, (cc + 1) * P)
                    if cc == 0:
                        pe.wait_ge(b_cs, NBLK * (kb + 1))
                    wait(pe, b_Te, k)
                    for i in range(NX + 1):
                        mm = nc.tensor.transpose(bank[2][:, i * P:(i + 1) * P], xbcT[:, kpar, i, tok], ident)
                    mm.then_inc(b_T, 1)
                if i := at(b, par, c, LAG_T):
                    k, _, _, cc = i
                    pe.wait_ge(b_yz, k + 1)
                    wait(pe, b_x2, k - 1)
                    for i in range(NX):
                        mm = nc.tensor.transpose(bank[6][:, i * P:(i + 1) * P], yz[:, cc % 2, i * P:(i + 1) * P], ident)
                    mm.then_inc(b_yT, 1)
                if i := at(b, par, c, 0):
                    k, kb, kpar, cc = i
                    tok = slice(cc * P, (cc + 1) * P)
                    pe.wait_ge(b_rl, k + 1)
                    wait(pe, b_E, k)
                    nc.tensor.matmul(bank[3][:, :], triS, rhsL[cc % 2], start=True, stop=True).then_inc(b_L, 1)
                    if cc == 0:
                        pe.wait_ge(s_hq[kpar], 16 * kb + 32 - 16 * kpar)
                    wait(pe, b_zs, k)
                    nc.tensor.matmul(bank[4][:, 0:DI], hq[:, kpar, 0, tok], wzT[:, 0:DI], start=True, stop=True).then_inc(b_z, 1)
                if i := at(b, par, c, CONV0):
                    n, nb, _, j = i
                    wait(pe, b_tp, n - 1)
                    nc.tensor.matmul(bank[j % 2][:, :], wzT[:, XB0 + j * P:XB0 + (j + 1) * P], tokens(hT, nb),
                                     start=True, stop=True).then_inc(b_cv, 1)
                if i := at(b, par, c, LAG_O):
                    k, kb, kpar, cc = i
                    nxt = at(b, par, c, LAG_T)
                    pe.wait_ge(b_yTe, k + 2 if nxt else k + 1)
                    if not nxt:
                        wait(pe, b_x2, k)
                    for i in range(NX):
                        nc.tensor.matmul(bank[6][:, 2 * P:3 * P], ynT[:, cc % 2, i * P:(i + 1) * P],
                                         woB[:, bass.ds(kb, 1), i, :].rearrange("p b d -> p (b d)"),
                                         start=(i == 0), stop=(i == NX - 1))
                    nc.tensor.matmul(bank[6][:, 3 * P:4 * P], hq[:, kpar, 1, cc * P:(cc + 1) * P], tokens(gad, kb),
                                     start=True, stop=True).then_inc(b_O, 1)
            phase_b(pe, slot)

            def phase_c(s):
                if inside(s, NB):
                    pe.wait_ge(c_xm, s + 1)
                    wait(pe, c_ev, s)
                    for c in range(NC):
                        mm = nc.tensor.transpose(bank[0][:, c * P:(c + 1) * P], xm[:, c * P:(c + 1) * P], ident)
                    mm.then_inc(c_T, 1)
                    pe.wait_ge(c_ev, s + 1)
                    wait(pe, c_le, s)
                    for c in range(NC):
                        mm = nc.tensor.matmul(bank[1][:, c * NE:(c + 1) * NE], h2T[:, c * P:(c + 1) * P], wr_sb[:, :],
                                              start=True, stop=True)
                    mm.then_inc(c_lg, 1)
                if inside(s - 1, NB):
                    pe.wait_ge(c_cho, s)
                    wait(pe, c_link, LINKS * (s - 1))
                    for c in range(NC):
                        o = bank[2][:, c * NE:(c + 1) * NE]
                        nc.tensor.matmul(o, ones[:, :], before[:, :], start=True, stop=False)
                        for i in range(c):
                            nc.tensor.matmul(o, ones[:, :], chosen[:, i, :], start=False, stop=False)
                        mm = nc.tensor.matmul(o, triI, chosen[:, c, :], start=False, stop=True)
                    mm.then_inc(c_rk, 1)
            slots(pe, NB, 1, phase_c)
            pe.wait_ge(c_pos, NB)
            nc.tensor.matmul(bank[2][:, 64:64 + NE], ones[:, :], before[:, :], start=True, stop=True).then_inc(t_cnt, 1)

            pe.wait_ge(s_moe, 32)

            def experts(t, u):
                if i := tile(t, u, -1):
                    n, v = i
                    pe.wait_ge(e_ld[v], 16 * (nth(n, v, RING) + 1))
                    wait(pe, e_Te, n - 1)
                    nc.tensor.transpose(bank[2 + v % 2][:, 0:P], xt[:, v, 0:P], ident).then_inc(e_T, 1)
                if i := tile(t, u, 0):
                    n, v = i
                    pe.wait_ge(e_Te, n + 1)
                    pe.wait_ge(e_w, n + 1)
                    wait(pe, e_g, n - 1)
                    for k in range(NK):
                        mm = nc.tensor.matmul(bank[v % 2][:, k * P:(k + 1) * P], w1c[:, v % 2, k * P:(k + 1) * P], xtT[:, v % 2, :],
                                              start=True, stop=True)
                    mm.then_inc(e_h, 1)
                if i := tile(t, u, 1):
                    n, v = i
                    pe.wait_ge(e_g, n + 1)
                    wait(pe, e_y, n - 1)
                    for k in range(NK):
                        mm = nc.tensor.matmul(bank[4 + v % 2][:, 0:P], gT[:, v % 2, k * P:(k + 1) * P],
                                              w2c[:, v % 4, k * P:(k + 1) * P], start=(k == 0), stop=(k == NK - 1))
                    mm.then_inc(e_o, 1)
            tiles(pe, experts)


INPUTS = ["x", "W_in", "W_z", "conv_w", "conv_b", "dt_bias", "A_log", "D_param", "norm_pre_w", "norm_gated_w", "W_out",
          "w_router", "w1", "b1", "w2", "b2", "c_in", "wmod"]
NAMES = {"x": "L0_attn_x", "W_in": "L0_attn_W_in", "W_z": "L0_attn_W_zxbcdt", "conv_w": "L0_attn_conv_w",
         "conv_b": "L0_attn_conv_b", "dt_bias": "L0_attn_dt_bias", "A_log": "L0_attn_A_log", "D_param": "L0_attn_D_param",
         "norm_pre_w": "L0_attn_norm_pre_w", "norm_gated_w": "L0_attn_norm_gated_w", "W_out": "L0_attn_W_out",
         "w_router": "L0_ffn_w_router", "w1": "L0_ffn_w1", "b1": "L0_ffn_b1", "w2": "L0_ffn_w2", "b2": "L0_ffn_b2",
         "c_in": "L0_c", "wmod": "L0_wmod"}


def layout(NB, NC, NE, TILES, NDUM):
    T, parts, at = NC * P, {}, 3 * P
    for name, n in (("cos", T), ("sin", T), ("ids", NB * TOPK * NC), ("region", NE), ("padpos", NE), ("padid", NE),
                    ("dumid", NDUM), ("tile", TILES), ("steps", NB * NC), ("upto", NE * NE)):
        parts[name] = slice(at, at + n)
        at += n
    parts["all"] = slice(0, at)
    return parts


def constants(NB, T, NE):
    NC, NTOK = T // P, NB * T
    NT, REG = NB * NC, NTOK + P
    NDUM = 8
    TILES = -(-(TOPK * NT + NE - 1) // 8) * 8
    k, l = np.arange(P)[:, None], np.arange(P)[None, :]
    inv_freq = np.float32(1.0) / np.float32(10000.0) ** (np.arange(0, 8, 2, dtype=np.float32) / np.float32(8))
    ang = (np.arange(T, dtype=np.float32)[None, :] * inv_freq.astype(np.float32)[:, None]).astype(np.float32)
    cos = np.tile(np.cos(ang), (P // 4, 1))
    sin = np.tile(np.concatenate([-np.sin(ang), np.sin(ang)]), (P // 8, 1))
    b, h, c = (a.reshape(1, -1) for a in np.meshgrid(np.arange(NB), np.arange(TOPK), np.arange(NC), indexing="ij"))
    e = np.arange(NE)[None, :]

    def rows(a):
        return np.broadcast_to(a, (P, a.shape[-1]))
    parts = [k == l, k > l, k <= l, cos, sin,
             h * NTOK + b * T + c * P + k,
             rows(e * REG - 1),
             e * REG + k,
             TOPK * NTOK + e * P + k,
             TOPK * NTOK + NE * P + np.arange(NDUM)[None, :] * P + k,
             rows(np.arange(TILES)[None, :]), rows(P * np.arange(NT)[None, :]),
             rows((e[0][None, :] <= e[0][:, None]).reshape(1, -1))]
    return np.concatenate(parts, axis=1).astype(np.float32)


def kernel(**inputs):
    import concourse.bacc as bacc
    from concourse.bass_utils import run_bass_kernel_spmd

    nc = bacc.Bacc("TRN2", target_bir_lowering=False, num_devices=1)
    arrays = {n: np.ascontiguousarray(inputs[NAMES[n]]) for n in INPUTS}
    arrays["consts"] = constants(*arrays["x"].shape[:2], arrays["w1"].shape[0])
    args = {n: nc.dram_tensor(n, a.shape, mybir.dt.from_np(a.dtype), kind="ExternalInput").ap() for n, a in arrays.items()}
    out = nc.dram_tensor("out", arrays["x"].shape, F32, kind="ExternalOutput").ap()
    build(nc, out=out, **args)
    r = run_bass_kernel_spmd(nc, [arrays], core_ids=[0])
    return r.results[0]["out"]
```

```python
import numpy as np
import concourse.bass as bass
from concourse import mybir
from contextlib import ExitStack

P = 128
F32 = mybir.dt.float32
ALU = mybir.AluOpType
ACT = mybir.ActivationFunctionType
AX = mybir.AxisListType.X
EPS = 1e-5
BIG = 1.0e30
WHOLE = 12582912.0
TOPK = 2
I32, U32 = mybir.dt.int32, mybir.dt.uint32


def wait(eng, sem, value):
    if isinstance(value, int) and value <= 0:
        return
    eng.wait_ge(sem, value)


def few_slots(n, ahead, lag, body):
    for s in range(-ahead, n + lag):
        body(s, s % 2)


def inside(i, n):
    return not isinstance(i, int) or 0 <= i < n


def build(nc, x, W_in, W_z, conv_w, conv_b, dt_bias, A_log, D_param, norm_pre_w, norm_gated_w, W_out,
          w_router, w1, b1, w2, b2, c_in, wmod, consts, out):
    NB, T, D = x.shape
    NC = T // P
    NT = NB * NC
    NX = norm_gated_w.shape[0] // P
    DI = NX * P
    NH = A_log.shape[0]
    HD = DI // NH
    NBLK = NX + 2
    KC = conv_w.shape[1]
    NE, _, HID = w1.shape
    NK = HID // P
    XB0, DT0 = DI, DI + NBLK * P
    assert D == P and T == 512
    NTOK = NB * T
    RING = 8
    TILES = TOPK * NT + NE - 1
    C = layout(NB, NC, NE, TILES)
    h2_d = nc.dram_tensor("second_layernorm_rows", [NTOK, P], F32, kind="Internal").ap()
    res_d = nc.dram_tensor("expert_results", [TOPK * NTOK + TILES * P, P], F32, kind="Internal").ap()
    mod_d = nc.dram_tensor("modulation_rows", [2, NB, P], F32, kind="Internal").ap()

    with ExitStack() as ctx:
        def sb(name, shape, dt=F32):
            return ctx.enter_context(nc.sbuf_tensor(name, shape, dt))

        def pb(name, shape, dt=F32):
            return ctx.enter_context(nc.psum_tensor(name, shape, dt))

        def sem(name):
            return ctx.enter_context(nc.semaphore(name))

        x_sb = sb("x_sb", [P, NB, NC, P])
        hold = sb("hold", [P, 2 * NB * T])
        qT = hold[:, 0:NB * T].rearrange("p (b t) -> p b t", b=NB)
        hT = hold[:, NB * T:2 * NB * T].rearrange("p (b t) -> p b t", b=NB)
        res = hold[:, 0:2 * NB * T].rearrange("p (b k c d) -> p b k c d", k=TOPK, c=NC, d=P)
        w1_sb = sb("w1_sb", [P, NE, HID])
        w2_sb = sb("w2_sb", [P, NE, NK, P])
        cst = sb("cst", [P, C["all"].stop])
        ident, triS, triI = cst[:, 0:P], cst[:, P:2 * P], cst[:, 2 * P:3 * P]
        ropeC, ropeS = cst[:, 3 * P:3 * P + T], cst[:, 3 * P + T:3 * P + 2 * T]
        ones = sb("ones", [P, P])
        eps = sb("eps", [P, 1])
        rows = sb("rows", [64, P])
        NR = NE * NK + NBLK + NX + 1 + NB
        R_B1, R_CB, R_NG, R_NP, R_C = 0, NE * NK, NE * NK + NBLK, NE * NK + NBLK + NX, NE * NK + NBLK + NX + 1
        cols = sb("cols", [P, NR])
        small = sb("small", [1, 3 * NH])
        hb = sb("hb", [P, 3 * NH])
        negA = sb("negA", [P, NH])
        win = sb("win", [P, P])
        wqT = sb("wqT", [P, P])
        wqrT = sb("wqrT", [P, P])
        wdt_nat = sb("wdt_nat", [NH, P])
        wzT = sb("wzT", [P, DT0])
        wdtz = sb("wdtz", [P, 2 * NB * NH])
        wrz = sb("wrz", [P, 2 * NB * NE])
        b2B = sb("b2B", [P, NE, P])
        modrow = sb("modrow", [NB, 2, P])
        cw = sb("cw", [P, NBLK, KC])
        cwh = sb("cwh", [P, NBLK, KC])
        cbh = sb("cbh", [P, NBLK])
        siluc = sb("siluc", [P, 3, NB])
        mod = sb("mod", [P, 6, NB])
        gsign = sb("gsign", [P, 2, NB])
        gabs = sb("gabs", [P, 2, NB])
        gad = sb("gad", [P, NB, P])
        woB = sb("woB", [P, NB, NX, P])
        gbB = sb("gbB", [P, NB, P])
        st6 = sb("st6", [P, NT, 6])
        mv = sb("mv", [P, 4, NT])
        lnv = sb("lnv", [P, NT])
        rstd = sb("rstd", [P, NT])
        dtr = sb("dtr", [P, NT, NH])
        dt_ = sb("dt_", [P, NT, NH])
        dtA = sb("dtA", [P, NT, NH])
        dec = sb("dec", [P, 3, NT * NH])
        dtdec = sb("dtdec", [P, NT, NH])
        big = sb("big", [P, 8, T])
        xh, xnT = (big[:, 2 * i:2 * i + 2, :] for i in range(2))
        t1, t2, sq, rb = (big[:, i, :] for i in range(4, 8))
        hq = sb("hq", [P, 2, 2, T])
        xbcT = sb("xbcT", [P, 2, NBLK, T])
        wz_nat = xbcT[:, 0, 0:2, :].rearrange("p k (a d) -> p (k a) d", d=P)[:, 0:NX + NBLK, :]
        wmod_sb = xbcT[:, 1, 0:2, :].rearrange("p k t -> p (k t)")[:, 0:6 * P]
        acc = [big[:, j, :] for j in range(4)]
        cth = [sb("cth_a", [P, T])[:, :], sb("cth_b", [P, T])[:, :]]
        rhsL = [big[:, 4, :], big[:, 5, :]]
        E4 = [big[:, 6, :], big[:, 7, :]]
        M4 = [sb("M4a", [P, NH * P]), sb("M4b", [P, NH * P])]
        xB = sb("xB", [P, NC, DI + P])
        Gm = sb("Gm", [P, P])
        xdt = sb("xdt", [P, 2, DI])
        xdec = sb("xdec", [P, 2, DI])
        xD = sb("xD", [P, 2, DI])
        zth = sb("zth", [P, 2, DI])
        zs = sb("zs", [P, 2, DI])
        yo = sb("yo", [P, DI])
        yd = sb("yd", [P, DI])
        ys = sb("ys", [P, DI])
        yz = sb("yz", [P, 2, DI])
        junk = sb("junk", [P, DI])
        ynT = sb("ynT", [P, 2, DI])
        gbd = hq[:, 0, :, :].rearrange("p a (b d) -> p (a b) d", d=P)
        wout_nat = zs[:, 0, :]
        dtT = zth[0:NB * NH, :, :].rearrange("p i d -> p (i d)")
        dts = xB[:, 0:2, :].rearrange("p c d -> p (c d)").rearrange("p (i n) -> p i n", i=6)
        state = sb("state", [P, 2, DI])
        sdec = sb("sdec", [P, DI])
        ss = sb("ss", [P, 2, 1])
        ms = sb("ms", [P, 2, 1])
        rg = sb("rg", [P, 2, 1])
        nhalf = sb("nhalf", [P, 1])
        xo = sb("xo", [P, P])
        xh2 = [big[:, 2 * i:2 * i + 2, :].rearrange("p b t -> p (b t)") for i in range(2)]
        xm = [big[:, 4 + 2 * i:6 + 2 * i, :].rearrange("p b t -> p (b t)") for i in range(2)]
        h2T = M4
        shB, scB = (xbcT[:, 0, 2 * i:2 * i + 2, :].rearrange("p k (a d) -> p (k a) d", d=P) for i in range(2))
        NP = 2 * NC
        NA = NT * NE

        def routed(i):
            return hold[:, i * NA:(i + 1) * NA].rearrange("p (a e) -> p a e", e=NE)
        lg, eq, rest, chosen, place = (routed(i) for i in range(5))
        oh, where = (hold[:, i * NA:(i + 2) * NA].rearrange("p (k a e) -> p k a e", k=TOPK, e=NE) for i in (5, 7))
        lgT = hold[0:NB * NE, 28 * NA:28 * NA + T]
        scan = [routed(9), routed(10), hold[:, 11 * NA:12 * NA + NE].rearrange("p (a e) -> p a e", e=NE)]
        ex = hold[:, 13 * NA:14 * NA + NT].rearrange("p (a e) -> p a e", e=NE + 1)
        cells = hold[:, 15 * NA:15 * NA + TILES * NE]
        isplace = hold[:, 18 * NA:18 * NA + 16 * P].rearrange("p (i d) -> p i d", d=P)
        istile = hold[:, 26 * NA:26 * NA + 16 * TILES].rearrange("p (i n) -> p i n", n=TILES)
        top = sb("top", [P, TOPK, NT])
        pick = sb("pick", [P, NT])
        zsum = sb("zsum", [P, NT])
        wts = sb("wts", [P, TOPK, NT])
        posf = sb("posf", [P, TOPK * NT])
        plo = sb("plo", [P, TOPK * NT])
        phi = sb("phi", [P, TOPK * NT])
        desc = sb("desc", [P, NE])
        tiles_e = sb("tiles_e", [P, NE])
        ends_e = sb("ends_e", [P, NE])
        first_e = sb("first_e", [P, NE])
        E_ = cth[0][:, 0:TILES]
        tb, tsel = (cth[1][:, i * TILES:(i + 1) * TILES] for i in range(2))
        tbT = cth[1][0:TILES, 2 * TILES:2 * TILES + P]
        t_exp = sb("t_exp", [1, TILES], I32)
        src_ix = sb("src_ix", [P, TILES], U32)
        dst_ix = sb("dst_ix", [P, TILES], U32)
        xt = sb("xt", [P, RING, P])
        w1c = big[:, 0:2, :]
        w2c = big[:, 2:6, :]
        gT = big[:, 6:8, :]
        xtT = yz[:, 0, :].rearrange("p (i d) -> p i d", i=2)
        b1c = sb("b1c", [P, 4, NK])
        b2c = M4[0][:, :].rearrange("p (i d) -> p i d", i=4)
        yt = M4[1][:, :].rearrange("p (i d) -> p i d", i=4)

        bank = [pb(f"bank{i}", [P, 512]) for i in range(8)]

        s_cst, s_wts, s_moe = sem("constants_loaded"), sem("weights_loaded"), sem("moe_weights_loaded")
        s_x = [sem(f"x_loaded_{b}") for b in range(NB)]
        s_cst2 = sem("tables_loaded")
        s_one, s_pre, s_prd, s_pra = sem("memsets_done"), sem("prep_pe"), sem("prep_dve"), sem("prep_act")
        s_gd, s_gm, s_ge = sem("gate_diag"), sem("gate_mm"), sem("gate_evac")
        s_ag = sem("stats_combined")
        s_st, s_stc, s_rs, s_rl2 = sem("stats_part"), sem("stats_done"), sem("rstd_ready"), sem("rstf_step")
        a_xh, a_T, a_ev, a_q, a_qr = sem("a_normalised"), sem("a_transposed"), sem("a_modulated"), sem("a_q"), sem("a_q_rot")
        a_t1, a_t2, a_rp, a_sq, a_n = sem("a_t1"), sem("a_t2"), sem("a_roped"), sem("a_squared"), sem("a_meansq")
        a_ln, a_ex, a_h = sem("a_ln"), sem("a_rms"), sem("a_h")
        a_d, a_de, a_dT, a_dc = sem("a_dt"), sem("a_dt_evac"), sem("a_dt_T"), sem("a_dt_done")
        s_da, s_dv, s_dp = sem("dt_act"), sem("dt_dve"), sem("dt_pe")
        s_hq = [sem("hq_even"), sem("hq_odd")]
        b_cv, b_acc, b_tap, b_tp, b_cth, b_cs = (sem("b_conv_proj"), sem("b_conv_first"), sem("b_conv_tap"),
                                                 sem("b_conv_sum"), sem("b_conv_tanh"), sem("b_conv_out"))
        b_T, b_Te, b_rl, b_L, b_E, b_z, b_th, b_zs = (sem("b_T"), sem("b_T_evac"), sem("b_rhsL"), sem("b_L"), sem("b_E"),
                                                      sem("b_z"), sem("b_z_tanh"), sem("b_zs"))
        b_St = sem("b_St")
        b_GS, b_Gm, b_M, b_xdt, b_xdec, b_xD = (sem("b_GS"), sem("b_Gm"), sem("b_M"), sem("b_xdt"), sem("b_xdec"), sem("b_xD"))
        b_sd, b_S, b_Y, b_yo, b_yd, b_ys, b_yz, b_ss = (sem("b_sdec"), sem("b_state"), sem("b_Y"), sem("b_yo"), sem("b_yd"),
                                                        sem("b_ysum"), sem("b_yz"), sem("b_ss"))
        b_ms, b_rg, b_yT, b_yTe, b_O, b_xo, b_x2 = (sem("b_ms"), sem("b_rg"), sem("b_yT"), sem("b_yT_evac"), sem("b_out"),
                                                    sem("b_xo"), sem("b_x2"))
        s_link = sem("softplus_link")
        s_mr2 = sem("mod_rows_product")
        s_mr, s_md, s_mb = sem("mod_rows"), sem("mod_rows_stored"), sem("mod_rows_spread")
        c_xh, c_sx, c_xm, c_T, c_ev, c_lg, c_h2 = (sem("c_normalised"), sem("c_scaled"), sem("c_shifted"), sem("c_transposed"),
                                                   sem("c_columns"), sem("c_logits"),
                                                   [sem(f"c_rows_stored_{g}") for g in range(NB // 2)])
        c_le, c_lT = sem("c_logits_read"), sem("c_logits_turned")
        c_link, c_exi, c_exp, c_scan, c_rk = (sem("c_link"), sem("c_exp_in"), sem("c_exp"), sem("c_scanned"), sem("c_ranks"))
        t_pos, t_tile, t_num, t_hot = (sem("t_positions"), sem("t_tile_one_hots"), sem("t_tiles_numbered"),
                                       sem("t_place_one_hots"))
        t_mm, t_flat, t_turn, t_src, t_tab = (sem("t_table_product"), sem("t_table_read"), sem("t_table_turned"),
                                              sem("t_indices"), sem("t_experts"))
        e_ld = [sem(f"e_loaded_{i}") for i in range(RING)]
        e_T, e_Te, e_w, e_h, e_g, e_o, e_y, e_b = (sem("e_transposed"), sem("e_columns"), sem("e_weights"), sem("e_hidden"),
                                                    sem("e_gelu"), sem("e_out"), sem("e_result"), sem("e_bias"))
        e_sc = [sem(f"e_scattered_{i}") for i in range(4)]
        f_ld = [sem(f"f_loaded_{b}") for b in range(NB)]
        f_w, f_sum, f_gb, f_x, f_st = sem("f_weighted"), sem("f_summed"), sem("f_gated"), sem("f_x"), sem("f_stored")

        g_bank = (5, 7)
        block = ctx.enter_context(nc.Block())

        LAG_Y, LAG_T, LAG_O = 2, 3, 4
        CONV0, CONV1, CONV_T, CONV2 = -7, -6, -5, -4

        def at(b, par, c, lag):
            db, cc = (c - lag) // NC, (c - lag) % NC
            b2 = b + db
            if not inside(b2, NB):
                return None
            return NC * b2 + cc, b2, (par + db) % 2, cc

        EARLY = NBLK

        def late(i):
            return None if i is None or (isinstance(i[0], int) and i[0] < EARLY) else i

        def run_b(slot, drain):
            def batch(b, par):
                for c in range(NC):
                    slot(b, par, c)
            for c in range(1, NC):
                slot(-2, 0, c)
            for b in (-1, 0, 1):
                batch(b, b % 2)
            yield batch
            for b in (NB - 2, NB - 1):
                batch(b, b % 2)
            for c in range(NC + 1):
                slot(NB + c // NC, (NB + c // NC) % 2, c % NC)
                drain(c)

        def phase_b(eng, slot, drain):
            for batch in run_b(slot, drain):
                with eng.Fori(1, NB // 2 - 1) as j:
                    batch(2 * j, 0)
                    batch(2 * j + 1, 1)

        def tiles(eng, stage):
            for u in range(-RING, RING):
                stage(u, u % RING)
            rounds = TILES // RING - 1
            with eng.Fori(1, rounds) as j:
                for u in range(RING):
                    stage(RING * j + u, u)
            for t in range(RING * rounds, TILES + RING):
                stage(t, t % RING)

        def tile(t, u, lag):
            return (t - lag, (u - lag) % RING) if inside(t - lag, TILES) else None

        def nth(t, u, ring):
            return t // ring if isinstance(t, int) else (t - u) * (RING // ring) // RING + u // ring

        def by_head(ap):
            return ap.rearrange("p (h q) -> p h q", h=NH)

        def per_head(ap, n):
            return ap.unsqueeze(2).broadcast_to([P, NH, n])

        def tokens(ap, b):
            return ap[:, bass.ds(b, 1), :].rearrange("p b t -> p (b t)")

        def chunk(ap, k):
            return ap[:, :, :, :].rearrange("p b c d -> p (b c) d")[:, bass.ds(k, 1), :].rearrange("p a d -> p (a d)")

        @block.sync
        def _(sp):
            for dst, src in ((cst[:, 0:3 * P], consts[:, 0:3 * P]), (rows[R_B1:R_CB, :], b1.rearrange("e (k p) -> (e k) p", p=P)),
                             (rows[R_CB:R_NG, :], conv_b.rearrange("(k p) -> k p", p=P)),
                             (rows[R_NG:R_NP, :], norm_gated_w.rearrange("(k p) -> k p", p=P)),
                             (rows[R_NP:R_C, :], norm_pre_w.rearrange("(k p) -> k p", p=P)),
                             (rows[R_C:NR, :], c_in)):
                sp.dma_start(dst, src).then_inc(s_cst, 16)
            for b in range(NB):
                sp.dma_start(x_sb[:, b, :, :], x[b, :, :].rearrange("(c p) d -> p c d", p=P)).then_inc(s_x[b], 16)
            sp.dma_start(cst[:, 3 * P:], consts[:, 3 * P:]).then_inc(s_cst2, 16)
            sp.wait_ge(s_x[NB - 1], 16)
            sp.dma_start(w1_sb[:, :, :], w1.rearrange("e d h -> d e h")).then_inc(s_moe, 16)
            sp.dma_start(w2_sb[:, :, :, :], w2.rearrange("e (k p) d -> p e k d", p=P)).then_inc(s_moe, 16)
            sp.dma_start(b2B[:, :, :], b2.rearrange("(a e) d -> a e d", a=1).broadcast_to([P, NE, P])).then_inc(s_moe, 16)
            sp.wait_ge(s_one, 1)
            sp.dma_start(wrz[:, NB * NE:(NB + 1) * NE], w_router).then_inc(s_moe, 16)
            sp.wait_ge(a_h, NB)
            sp.wait_ge(s_ge, NB)

            def fetch(b, par):
                wait(sp, b_z, NC * (b - 1))
                wait(sp, b_O, NC * (b - 1))
                for i, src in enumerate((hT, qT)):
                    sp.dma_start(hq[:, par, i, :], tokens(src, b)).then_inc(s_hq[par], 16)
            for par in range(2):
                fetch(par, par)
            with sp.Fori(1, NB // 2) as j:
                for par in range(2):
                    fetch(2 * j + par, par)
            sp.wait_ge(s_md, 16)
            sp.wait_ge(b_Y, NC * (NB - 1))
            for i, dst in enumerate((shB, scB)):
                sp.dma_start(dst, mod_d[i:i + 1, :, :].broadcast_to([P, NB, P])).then_inc(s_mb, 16)

            for g in range(NB // 2):
                sp.wait_ge(c_xm, 2 * g + 2)
                sp.dma_start(h2_d[g * NP * P:(g + 1) * NP * P, :].rearrange("(b p c) d -> p b (c d)", b=2, c=NC),
                             xm[g % 2].rearrange("p (b n) -> p b n", b=2)).then_inc(c_h2[g], 16)

            for i in range(4):
                sp.wait_ge(e_sc[i], 16 * ((TILES - 1 - i) // 4 + 1))
            for b in range(NB):
                for k in range(TOPK):
                    sp.dma_start(res[:, b, k, :, :], res_d[k * NTOK + b * T:k * NTOK + (b + 1) * T, :].rearrange(
                        "(p c) d -> p c d", p=P)).then_inc(f_ld[b], 16)
            with sp.Fori(0, NB) as b:
                sp.wait_ge(f_x, b + 1)
                sp.dma_start(out[bass.ds(b, 1), :, :].rearrange("b (c p) d -> p (b c) d", p=P),
                             x_sb[:, bass.ds(b, 1), :, :].rearrange("p b c d -> p (b c) d")).then_inc(f_st, 16)
            sp.wait_ge(f_st, 16 * NB)

        @block.scalar
        def _(act):
            act.preload_act_table_set("natural_log_exp_and_others")
            for dst, src in ((win[:, :], W_in[0:P, :]),
                             (wmod_sb[:, :], wmod), (small[:, 0:NH], dt_bias.rearrange("(a h) -> a h", a=1)),
                             (small[:, NH:2 * NH], A_log.rearrange("(a h) -> a h", a=1)),
                             (small[:, 2 * NH:], D_param.rearrange("(a h) -> a h", a=1)),
                             (wz_nat[:, :, :], W_z[0:DT0, :].rearrange("(k p) d -> p k d", p=P)),
                             (wdt_nat[:, :], W_z[DT0:DT0 + NH, :]), (wout_nat, W_out),
                             (cw[:, :, :], conv_w.rearrange("(k p) t -> p k t", p=P))):
                act.dma_start(dst, src).then_inc(s_wts, 16)
            act.wait_ge(s_prd, 1)
            nc.scalar.activation(siluc[:, 0, :], cols[:, R_C:NR], ACT.Exp, scale=-1.0).then_inc(s_pra, 1)
            act.wait_ge(s_prd, 2)
            nc.scalar.activation(negA[:, :], hb[:, NH:2 * NH], ACT.Exp).then_inc(s_pra, 1)

            act.wait_ge(s_mr, 1)
            act.dma_start(mod_d.rearrange("i b d -> b i d"), modrow[:, :, :]).then_inc(s_md, 16)
            act.wait_ge(s_one, 1)
            act.wait_ge(s_stc, 1)
            nc.scalar.activation(lnv[:, :], mv[:, 1, :], ACT.Ln, bias=eps[:, 0:1]).then_inc(s_rl2, 1)
            act.wait_ge(s_rl2, 1)
            nc.scalar.activation(rstd[:, :], lnv[:, :], ACT.Exp, scale=-0.5).then_inc(s_rs, 1)

            def conv_first(n, j):
                act.wait_ge(b_cv, n + 1)
                wait(act, b_cs, n - 3)
                nc.scalar.activation(acc[j], bank[j % 2][:, :], ACT.Identity, scale=cwh[:, j, KC - 1:KC],
                                     bias=cbh[:, j:j + 1]).then_inc(b_acc, 1)

            def gates(b):
                act.wait_ge(s_gm, b + 1)
                o = bank[g_bank[b % 2]]
                for k in range(NX):
                    nc.scalar.activation(woB[:, b, k, :], o[:, k * P:(k + 1) * P], ACT.Copy,
                                         scale=cols[:, R_NG + k:R_NG + k + 1])
                nc.scalar.activation(gbB[:, b, :], o[:, NX * P:(NX + 1) * P], ACT.Copy).then_inc(s_ge, 1)

            def phase_a(s, par):
                if inside(s - 2, NB):
                    act.wait_ge(a_rp, s - 1)
                    wait(act, a_n, s - 2)
                    nc.scalar.activation(sq, tokens(qT, s - 2), ACT.Square).then_inc(a_sq, 1)
                if inside(s - 3, NB):
                    act.wait_ge(a_n, s - 2)
                    wait(act, a_h, s - 3)
                    nc.scalar.activation(rb, bank[3][:, :], ACT.Ln, scale=1.0 / P, bias=eps[:, 0:1]).then_inc(a_ln, 1)
                    act.wait_ge(a_ln, s - 2)
                    nc.scalar.activation(rb, rb, ACT.Exp, scale=-0.5).then_inc(a_ex, 1)
                if inside(s, NB):
                    act.wait_ge(a_T, s + 1)
                    wait(act, a_qr, s - 1)
                    nc.scalar.activation(xnT[:, par, :], bank[0][:, :], ACT.Identity, scale=mod[:, 1, bass.ds(s, 1)],
                                         bias=mod[:, 0, bass.ds(s, 1)]).then_inc(a_ev, 1)
                if inside(s - 1, NB):
                    gates(s - 1)
                if inside(s - NB, EARLY):
                    conv_first(s - NB, s - NB)
            few_slots(NB, 1, 4, phase_a)
            act.wait_ge(a_d, NB)
            nc.scalar.activation(dtT, bank[4][0:NB * NH, :], ACT.Copy).then_inc(a_de, 1)
            act.wait_ge(s_dv, 2)
            nc.scalar.activation(dts[:, 2, :], dts[:, 1, :], ACT.Exp, scale=-1.0).then_inc(s_da, 1)
            act.wait_ge(s_dv, 3)
            nc.scalar.activation(dts[:, 4, :], dts[:, 3, :], ACT.Ln).then_inc(s_da, 1)
            act.wait_ge(s_dp, 1)
            nc.scalar.activation(dec[:, :, :].rearrange("p a n -> p (a n)"), bank[5][:, 0:3 * NT * NH], ACT.Exp).then_inc(s_da, 1)

            act.preload_act_table_set("exp_and_others")

            def slot(b, par, c):
                if i := at(b, par, c, LAG_Y):
                    k, _, _, cc = i
                    act.wait_ge(b_Y, k + 1)
                    wait(act, b_ys, k)
                    for h in range(NH):
                        head = slice(h * HD, (h + 1) * HD)
                        if cc:
                            ins = nc.scalar.activation(yo[:, head], bank[7][:, DI + h * HD:DI + (h + 1) * HD], ACT.Copy,
                                                       scale=dec[:, 1, bass.ds(NH * k + h, 1)])
                        elif h == 0:
                            ins = nc.scalar.activation(yo[:, :], xB[:, 0, 0:DI], ACT.Copy, scale=0.0)
                    ins.then_inc(b_yo, 1)
                if i := at(b, par, c, 0):
                    k, _, _, cc = i
                    act.wait_ge(b_T, k + 1)
                    wait(act, b_xD, k - 3)
                    wait(act, b_St, k - 3)
                    nc.scalar.activation(xB[:, cc, :], bank[2][:, 0:DI + P], ACT.Copy).then_inc(b_Te, 1)
                if i := at(b, par, c, LAG_T):
                    k, _, _, cc = i
                    act.wait_ge(b_yT, k + 1)
                    wait(act, b_O, k - 1)
                    nc.scalar.activation(ynT[:, cc % 2, :], bank[6][:, 0:DI], ACT.Copy).then_inc(b_yTe, 1)
                    wait(act, b_ms, k - 1)
                    nc.scalar.activation(junk[:, :], yz[:, cc % 2, :], ACT.Square, scale=float(DI) ** -0.5,
                                         accum_out=ss[:, cc % 2, :]).then_inc(b_ss, 1)
                if i := at(b, par, c, 0):
                    k, _, _, cc = i
                    act.wait_ge(b_L, k + 1)
                    wait(act, b_M, k - 1)
                    nc.scalar.activation(E4[cc % 2], bank[3][:, :], ACT.Exp).then_inc(b_E, 1)
                    act.wait_ge(b_z, k + 1)
                    wait(act, b_zs, k - 1)
                    nc.scalar.activation(zth[:, cc % 2, :], bank[4][:, 0:DI], ACT.Tanh).then_inc(b_th, 1)
                if i := at(b, par, c, -1):
                    k, _, _, cc = i
                    wait(act, b_L, k - 1)
                    for h in range(NH):
                        ins = nc.scalar.activation(rhsL[cc % 2][:, h * P:(h + 1) * P], triI, ACT.Copy,
                                                   scale=dtA[:, bass.ds(k, 1), h])
                    ins.then_inc(b_rl, 1)
                if i := at(b, par, c, CONV_T):
                    n, _, _, j = i
                    act.wait_ge(b_tp, n + 1)
                    wait(act, b_cs, n - 1)
                    nc.scalar.activation(cth[j % 2], acc[j], ACT.Tanh).then_inc(b_cth, 1)
                if i := late(at(b, par, c, CONV0)):
                    conv_first(i[0], i[3])
            act.wait_ge(s_dv, 4)

            def second_rstd(n, part):
                act.wait_ge(s_stc, n)
                nc.scalar.activation(lnv[:, part], mv[:, 1, part], ACT.Ln, bias=eps[:, 0:1]).then_inc(s_rl2, 1)
                act.wait_ge(s_rl2, n)
                nc.scalar.activation(rstd[:, part], lnv[:, part], ACT.Exp, scale=-0.5).then_inc(s_rs, 1)

            def columns(g):
                for i in range(2):
                    act.wait_ge(c_T, 2 * g + i + 1)
                    wait(act, c_lg, 2 * g + i - 1)
                    nc.scalar.activation(h2T[i][:, :], bank[i][:, :], ACT.Copy).then_inc(c_ev, 1)

            def drain(i):
                if i == 0:
                    act.preload_act_table_set("natural_log_exp_and_others")
                if i == 1:
                    second_rstd(2, slice(0, NT - NP))
            phase_b(act, slot, drain)
            columns(0)
            second_rstd(3, slice(NT - NP, NT))
            for g in range(1, NB // 2):
                columns(g)
            act.wait_ge(c_lg, NB)
            nc.scalar.activation(lgT[:, :], bank[2][0:NB * NE, :], ACT.Copy).then_inc(c_le, 1)
            act.wait_ge(c_exi, 2)
            nc.scalar.activation(ex, ex, ACT.Exp).then_inc(c_exp, 1)
            act.preload_act_table(ACT.Gelu_apprx_tanh)

            def gelus(t, u):
                if i := tile(t, u, -1):
                    n, v = i
                    act.wait_ge(e_T, n + 1)
                    wait(act, e_h, n - 1)
                    nc.scalar.activation(xtT[:, v % 2, :], bank[2 + v % 2][:, 0:P], ACT.Copy).then_inc(e_Te, 1)
                if i := tile(t, u, 0):
                    t, u = i
                    act.wait_ge(e_h, t + 1)
                    wait(act, e_o, t - 1)
                    for k in range(NK):
                        ins = nc.scalar.activation(gT[:, u % 2, k * P:(k + 1) * P], bank[u % 2][:, k * P:(k + 1) * P],
                                                   ACT.Gelu_apprx_tanh, bias=b1c[:, u % 4, k:k + 1])
                    ins.then_inc(e_g, 1)
            tiles(act, gelus)

            for b in range(NB):
                act.wait_ge(f_ld[b], 16 * TOPK)
                for c in range(NC):
                    ins = nc.scalar.activation(res[:, b, 0, c, :], res[:, b, 0, c, :], ACT.Copy,
                                               scale=wts[:, 0, NC * b + c:NC * b + c + 1])
                ins.then_inc(f_w, 1)

        @block.gpsimd
        def _(pool):
            nc.gpsimd.memset(ones[:, :], 1.0)
            nc.gpsimd.memset(nhalf[:, :], -0.5)
            nc.gpsimd.memset(wdtz[:, :], 0.0)
            nc.gpsimd.memset(wrz[:, 0:NB * NE], 0.0)
            nc.gpsimd.memset(wrz[:, (NB + 1) * NE:], 0.0)
            for e in range(NE):
                nc.gpsimd.memset(desc[:, e:e + 1], float(NE - e))
            nc.gpsimd.memset(eps[:, :], EPS).then_inc(s_one, 1)

            pool.wait_ge(s_prd, 13)
            for dst, g in ((gad, 2), (gbd, 5)):
                ins = nc.gpsimd.tensor_tensor(dst[:, :, :], ident.unsqueeze(1).broadcast_to([P, NB, P]),
                                              mod[:, g, :].unsqueeze(2).broadcast_to([P, NB, P]), ALU.mult)
            ins.then_inc(s_gd, 1)

            def phase_a(s, par):
                if inside(s - 3, NB):
                    pool.wait_ge(a_ex, s - 2)
                    nc.gpsimd.tensor_tensor(tokens(hT, s - 3), tokens(qT, s - 3), rb, ALU.mult).then_inc(a_h, 1)
                if inside(s - 1, NB):
                    pool.wait_ge(a_t2, s)
                    nc.gpsimd.tensor_tensor(tokens(qT, s - 1), t1, t2, ALU.add).then_inc(a_rp, 1)
            few_slots(NB, 1, 4, phase_a)
            pool.wait_ge(s_dv, 5)
            pool.wait_ge(s_prd, 3)

            def slot(b, par, c):
                if i := at(b, par, c, LAG_Y):
                    k, kb, _, cc = i
                    if cc in (1, 2):
                        pool.wait_ge(b_S, (NC - 1) * kb + cc)
                        nc.gpsimd.tensor_tensor(by_head(sdec[:, :]), by_head(state[:, (cc + 1) % 2, :]),
                                                per_head(dec[:, 2, bass.ds(NH * k, NH)], HD), ALU.mult).then_inc(b_sd, 1)
                if i := at(b, par, c, 1):
                    k, kb, _, cc = i
                    xv = by_head(xB[:, cc, 0:DI])
                    pool.wait_ge(b_Te, k + 1)
                    wait(pool, b_Y, k - 1)
                    nc.gpsimd.tensor_tensor(by_head(xdt[:, cc % 2, :]), xv,
                                            per_head(dt_[:, bass.ds(k, 1), :].rearrange("p a h -> p (a h)"), HD),
                                            ALU.mult).then_inc(b_xdt, 1)
                    if cc != NC - 1:
                        wait(pool, b_St, k - 1)
                        nc.gpsimd.tensor_tensor(by_head(xdec[:, cc % 2, :]), xv,
                                                per_head(dtdec[:, bass.ds(k, 1), :].rearrange("p a h -> p (a h)"), HD),
                                                ALU.mult).then_inc(b_xdec, 1)
                    wait(pool, b_yd, k - 1)
                    nc.gpsimd.tensor_tensor(by_head(xD[:, cc % 2, :]), xv, per_head(hb[:, 2 * NH:3 * NH], HD), ALU.mult
                                            ).then_inc(b_xD, 1)
                if i := at(b, par, c, 1):
                    k, _, _, cc = i
                    q = cc % 2
                    pool.wait_ge(b_E, k + 1)
                    pool.wait_ge(b_Gm, k + 1)
                    wait(pool, b_Y, k - 1)
                    nc.gpsimd.tensor_tensor(by_head(M4[q][:, :]), by_head(E4[q]),
                                            Gm[:, :].unsqueeze(1).broadcast_to([P, NH, P]), ALU.mult).then_inc(b_M, 1)
                if i := at(b, par, c, LAG_T):
                    k, _, _, cc = i
                    q = cc % 2
                    pool.wait_ge(b_ss, k + 1)
                    wait(pool, b_rg, k - 1)
                    nc.gpsimd.tensor_tensor(ms[:, q, :], ss[:, q, :], eps[:, :], ALU.add).then_inc(b_ms, 1)
                    pool.wait_ge(b_ms, k + 1)
                    wait(pool, b_xo, k - 1)
                    nc.gpsimd.tensor_tensor(rg[:, q, :], ms[:, q, :], nhalf[:, :], ALU.pow).then_inc(b_rg, 1)
                if i := at(b, par, c, LAG_Y):
                    k, _, _, cc = i
                    pool.wait_ge(b_yd, k + 1)
                    wait(pool, b_yz, k)
                    nc.gpsimd.tensor_tensor(ys[:, :], yo[:, :], yd[:, :], ALU.add).then_inc(b_ys, 1)

            def scale(g):
                for i in range(2):
                    pool.wait_ge(c_xh, 2 * g + i + 1)
                    x3 = xh2[g % 2][:, i * T:(i + 1) * T].rearrange("p (c d) -> p c d", d=P)
                    nc.gpsimd.tensor_tensor(x3, x3, scB[:, 2 * g + i:2 * g + i + 1, :].broadcast_to([P, NC, P]), ALU.mult
                                            ).then_inc(c_sx, 1)

            def drain(i):
                if i == 2:
                    pool.wait_ge(s_mb, 32)
                if i in (2, 3):
                    scale(i - 2)
            phase_b(pool, slot, drain)
            scale(NB // 2 - 2)
            scale(NB // 2 - 1)

            pool.wait_ge(s_cst2, 16)
            for g in range(TOPK * NT // 8):
                half = slice(8 * (g % 2), 8 * (g % 2) + 8)
                pool.wait_ge(t_tile, g + 1)
                nc.gpsimd.tensor_tensor(istile[:, half, :], istile[:, half, :],
                                        cst[:, C["ids"]][:, 8 * g:8 * g + 8].unsqueeze(2).broadcast_to([P, 8, TILES]), ALU.mult
                                        ).then_inc(t_num, 1)

            for g in range(NB // 2):
                pool.wait_ge(c_h2[g], 16)
            pool.wait_ge(t_src, 1)
            AHEAD = 4
            for t in range(TILES + AHEAD):
                if t < TILES:
                    wait(pool, e_T, t - RING + 1)
                    nc.gpsimd.indirect_dma_start(xt[:, t % RING, :], None, h2_d,
                                                 bass.IndirectOffsetOnAxis(src_ix[:, t:t + 1], 0)).then_inc(e_ld[t % RING], 16)
                if t >= AHEAD:
                    n = t - AHEAD
                    pool.wait_ge(e_y, n + 1)
                    nc.gpsimd.indirect_dma_start(res_d, bass.IndirectOffsetOnAxis(dst_ix[:, n:n + 1], 0), yt[:, n % 4, :], None
                                                 ).then_inc(e_sc[n % 4], 16)

            for b in range(NB):
                pool.wait_ge(f_sum, b + 1)
                nc.gpsimd.tensor_tensor(res[:, b, 1, :, :], res[:, b, 0, :, :], gbB[:, b:b + 1, :].broadcast_to([P, NC, P]),
                                        ALU.mult).then_inc(f_gb, 1)

        @block.vector
        def _(dve):
            X_FIRST = NB // 2 + 1
            dve.wait_ge(s_pre, 1)
            nc.vector.tensor_copy(cols[:, :], bank[0][:, 0:NR]).then_inc(s_prd, 1)
            def stats(b):
                for c in range(NC):
                    ins = nc.vector.bn_stats(st6[:, bass.ds(NC * b + c, 1), :].rearrange("p a m -> p (a m)"),
                                             x_sb[:, bass.ds(b, 1), c, :].rearrange("p b d -> p (b d)"))
                ins.then_inc(s_st, 1)

            for b in range(X_FIRST):
                dve.wait_ge(s_x[b], 16)
                stats(b)
            dve.wait_ge(s_pre, 2)
            nc.vector.tensor_copy(hb[:, :], bank[1][:, 0:3 * NH]).then_inc(s_prd, 1)
            dve.wait_ge(s_prd, 2)
            dve.wait_ge(s_wts, 16 * 9)
            dve.wait_ge(s_pra, 2)
            nc.vector.tensor_scalar(negA[:, :], negA[:, :], -1.0, None, ALU.mult)
            nc.vector.tensor_scalar(cwh[:, :, :], cw[:, :, :], 0.5, None, ALU.mult)
            nc.vector.tensor_scalar(cbh[:, :], cols[:, R_CB:R_NG], 0.5, None, ALU.mult)
            nc.vector.tensor_scalar(siluc[:, 1, :], siluc[:, 0, :], 1.0, None, ALU.add).then_inc(s_prd, 1)
            dve.wait_ge(s_prd, 3)
            nc.vector.reciprocal(siluc[:, 2, :], siluc[:, 1, :]).then_inc(s_prd, 1)
            dve.wait_ge(s_prd, 4)
            nc.vector.tensor_tensor(siluc[:, 1, :], siluc[:, 2, :], cols[:, R_C:NR], ALU.mult).then_inc(s_prd, 1)
            dve.wait_ge(s_pre, 3)
            nc.vector.tensor_copy(wqT[:, :], bank[2][:, 0:P])
            sw = bank[2][:, 0:P].rearrange("p (h a i) -> p h a i", a=2, i=4)
            dst = wqrT[:, :].rearrange("p (h a i) -> p h a i", a=2, i=4)
            nc.vector.tensor_copy(dst[:, :, 0, :], sw[:, :, 1, :])
            nc.vector.tensor_copy(dst[:, :, 1, :], sw[:, :, 0, :]).then_inc(s_prd, 1)
            dve.wait_ge(s_pre, 4)
            npw = cols[:, R_NP:R_NP + 1]
            nc.vector.tensor_scalar(wzT[:, 0:DI], bank[3][:, 0:DI], npw, 0.5, ALU.mult, ALU.mult)
            nc.vector.tensor_scalar(wzT[:, DI:4 * P], bank[3][:, DI:4 * P], npw, None, ALU.mult)
            nc.vector.tensor_scalar(wzT[:, 4 * P:DT0], bank[4][:, 0:DT0 - 4 * P], npw, None, ALU.mult)
            dve.wait_ge(s_one, 1)
            nc.vector.tensor_scalar(wdtz[:, NB * NH:(NB + 1) * NH], bank[4][:, DT0 - 4 * P:DT0 - 4 * P + NH], npw, None, ALU.mult
                                    ).then_inc(s_prd, 1)
            dve.wait_ge(s_pre, 5)
            nc.vector.tensor_copy(mod[:, :, :].rearrange("p a b -> p (a b)"), bank[1][:, 64:64 + 6 * NB]).then_inc(s_prd, 1)
            dve.wait_ge(s_prd, 8)
            for i, g in enumerate((2, 5)):
                nc.vector.scalar_tensor_tensor(out=gabs[:, i, :], in0=mod[:, g, :], scalar=-1.0, in1=mod[:, g, :],
                                               op0=ALU.mult, op1=ALU.max)
                nc.vector.tensor_scalar(gsign[:, i, :], mod[:, g, :], 0.0, 2.0, ALU.is_ge, ALU.mult).then_inc(s_prd, 1)
            dve.wait_ge(s_prd, 10)
            nc.vector.tensor_scalar(gabs[:, :, :], gabs[:, :, :], 0.25, None, ALU.max)
            nc.vector.tensor_scalar(gsign[:, :, :], gsign[:, :, :], -1.0, None, ALU.add).then_inc(s_prd, 1)
            dve.wait_ge(s_prd, 11)
            for i, g in enumerate((2, 5)):
                nc.vector.tensor_tensor(mod[:, g, :], gabs[:, i, :], gsign[:, i, :], ALU.mult)
            for j in (1, 4):
                nc.vector.tensor_scalar(mod[:, j, :], mod[:, j, :], 1.0, None, ALU.add).then_inc(s_prd, 1)
            dve.wait_ge(s_prd, 13)

            dve.wait_ge(s_mr2, 1)
            nc.vector.tensor_copy(modrow[:, 0, :], bank[6][0:NB, 0:P])
            nc.vector.tensor_scalar(modrow[:, 1, :], bank[6][0:NB, P:2 * P], 1.0, None, ALU.add).then_inc(s_mr, 1)
            def mean_var(n, part, counted):
                dve.wait_ge(s_st, counted)
                me, mo, qe, qo = (st6[:, part, i] for i in (1, 4, 2, 5))
                mean, var, diff, q = (mv[:, i, part] for i in range(4))
                nc.vector.tensor_tensor(mean, me, mo, ALU.add)
                nc.vector.tensor_tensor(diff, me, mo, ALU.subtract)
                nc.vector.tensor_tensor(q, qe, qo, ALU.add).then_inc(s_ag, 1)
                dve.wait_ge(s_ag, 2 * n - 1)
                nc.vector.tensor_scalar(mean, mean, 0.5, None, ALU.mult)
                nc.vector.scalar_tensor_tensor(out=diff, in0=diff, scalar=0.25, in1=diff, op0=ALU.mult, op1=ALU.mult
                                               ).then_inc(s_ag, 1)
                dve.wait_ge(s_ag, 2 * n)
                nc.vector.scalar_tensor_tensor(out=var, in0=q, scalar=1.0 / P, in1=diff, op0=ALU.mult, op1=ALU.add
                                               ).then_inc(s_stc, 1)
                dve.wait_ge(s_stc, n)

            for b in range(X_FIRST, NB):
                dve.wait_ge(s_x[b], 16)
                stats(b)
            mean_var(1, slice(0, NT), NB)
            def normalise(b, xh):
                for c in range(NC):
                    ins = nc.vector.tensor_scalar(xh[:, c * P:(c + 1) * P],
                                                  x_sb[:, bass.ds(b, 1), c, :].rearrange("p b d -> p (b d)"),
                                                  mv[:, 0, bass.ds(NC * b + c, 1)],
                                                  rstd[:, bass.ds(NC * b + c, 1)], ALU.subtract, ALU.mult)
                return ins

            dve.wait_ge(s_rs, 1)

            def conv_taps(n, j):
                dve.wait_ge(b_acc, n + 1)
                for t in range(1, KC):
                    ins = nc.vector.scalar_tensor_tensor(out=acc[j][:, t:T], in0=bank[j % 2][:, 0:T - t],
                                                         scalar=cwh[:, j, KC - 1 - t:KC - t], in1=acc[j][:, t:T],
                                                         op0=ALU.mult, op1=ALU.add)
                    if t < KC - 1:
                        ins.then_inc(b_tap, 1)
                        dve.wait_ge(b_tap, (KC - 2) * n + t)
                ins.then_inc(b_tp, 1)

            dve.wait_ge(s_cst2, 16)

            def phase_a(s, par):
                if inside(s + 1, NB):
                    wait(dve, a_T, s)
                    normalise(s + 1, xh[:, 1 - par, :]).then_inc(a_xh, 1)
                if inside(s - 1, NB):
                    dve.wait_ge(a_q, s)
                    wait(dve, a_rp, s - 1)
                    nc.vector.tensor_tensor(t1, bank[1][:, :], ropeC, ALU.mult).then_inc(a_t1, 1)
                    dve.wait_ge(a_qr, s)
                    nc.vector.tensor_tensor(t2, bank[2][:, :], ropeS, ALU.mult).then_inc(a_t2, 1)
                if inside(s - NB - 1, EARLY):
                    conv_taps(s - NB - 1, s - NB - 1)
            few_slots(NB, 1, 4, phase_a)

            conv_taps(EARLY - 1, EARLY - 1)
            dve.wait_ge(a_dT, 1)
            nc.vector.tensor_copy(dtr[:, :, :].rearrange("p (b c) h -> p b c h", b=NB),
                                  bank[5][:, 0:NT * NH].rearrange("p (c b h) -> p b c h", b=NB, h=NH)).then_inc(a_dc, 1)
            dve.wait_ge(a_dc, 1)
            v, av, u, w, lw, tmp = (dts[:, i, :] for i in range(6))
            nc.vector.tensor_tensor(v.rearrange("p (a h) -> p a h", h=NH), dtr[:, :, :],
                                    hb[:, 0:NH].unsqueeze(1).broadcast_to([P, NT, NH]), ALU.add).then_inc(s_dv, 1)
            dve.wait_ge(s_dv, 1)
            nc.vector.scalar_tensor_tensor(out=av, in0=v, scalar=-1.0, in1=v, op0=ALU.mult, op1=ALU.max).then_inc(s_dv, 1)
            dve.wait_ge(s_da, 1)
            nc.vector.tensor_scalar(w, u, 1.0, None, ALU.add).then_inc(s_dv, 1)
            chain = [0]

            def link(ins):
                chain[0] += 1
                ins.then_inc(s_link, 1)
                dve.wait_ge(s_link, chain[0])
            link(nc.vector.tensor_scalar(tmp, u, -0.25, 1.0 / 3, ALU.mult, ALU.add))
            link(nc.vector.tensor_tensor(tmp, tmp, u, ALU.mult))
            link(nc.vector.tensor_scalar(tmp, tmp, -1.0, 0.5, ALU.mult, ALU.add))
            link(nc.vector.tensor_tensor(tmp, tmp, u, ALU.mult))
            link(nc.vector.tensor_scalar(tmp, tmp, -1.0, 1.0, ALU.mult, ALU.add))
            link(nc.vector.tensor_tensor(tmp, tmp, u, ALU.mult))
            dve.wait_ge(s_da, 2)
            link(nc.vector.tensor_tensor(lw, lw, tmp, ALU.subtract))
            link(nc.vector.scalar_tensor_tensor(out=lw, in0=u, scalar=1.0 / 64, in1=lw, op0=ALU.is_ge, op1=ALU.mult))
            link(nc.vector.tensor_tensor(tmp, tmp, lw, ALU.add))
            dtf = dt_[:, :, :].rearrange("p a h -> p (a h)")
            link(nc.vector.scalar_tensor_tensor(out=dtf, in0=v, scalar=0.0, in1=tmp, op0=ALU.max, op1=ALU.add))
            nc.vector.tensor_tensor(dtA[:, :, :], dt_[:, :, :], negA[:, :].unsqueeze(1).broadcast_to([P, NT, NH]),
                                    ALU.mult).then_inc(s_dv, 1)
            dve.wait_ge(s_da, 3)
            nc.vector.tensor_tensor(dtdec[:, :, :].rearrange("p a h -> p (a h)"), dtf, dec[:, 0, :], ALU.mult).then_inc(s_dv, 1)
            dve.wait_ge(s_dv, 5)

            def slot(b, par, c):
                if i := at(b, par, c, CONV2):
                    n, bw, wpar, j = i
                    dve.wait_ge(b_cth, n + 1)
                    wait(dve, b_T if j < NX else b_GS, NC * (bw - 1))
                    if j == NX + 1:
                        wait(dve, b_Y, NC * (bw - 1))
                    nc.vector.scalar_tensor_tensor(out=xbcT[:, wpar, j, :], in0=cth[j % 2], scalar=1.0, in1=acc[j],
                                                   op0=ALU.add, op1=ALU.mult).then_inc(b_cs, 1)
                if i := at(b, par, c, 1):
                    k, _, _, cc = i
                    dve.wait_ge(b_GS, k + 1)
                    wait(dve, b_M, k)
                    nc.vector.tensor_tensor(Gm[:, :], bank[5][:, 0:P], triI, ALU.mult).then_inc(b_Gm, 1)
                if i := at(b, par, c, 1):
                    k, _, _, cc = i
                    q = cc % 2
                    dve.wait_ge(b_th, k + 1)
                    wait(dve, b_yz, k - 1)
                    nc.vector.scalar_tensor_tensor(out=zs[:, q, :], in0=zth[:, q, :], scalar=1.0, in1=bank[4][:, 0:DI],
                                                   op0=ALU.add, op1=ALU.mult).then_inc(b_zs, 1)
                if i := at(b, par, c, LAG_Y):
                    k, kb, _, cc = i
                    dve.wait_ge(b_Y, k + 1)
                    wait(dve, b_ys, k)
                    dve.wait_ge(b_xD, k + 1)
                    dve.wait_ge(b_yo, k + 1)
                    nc.vector.tensor_tensor(yd[:, :], bank[7][:, 0:DI], xD[:, cc % 2, :], ALU.add).then_inc(b_yd, 1)
                    if cc != NC - 1:
                        dve.wait_ge(b_St, k + 1)
                    if cc == 0:
                        nc.vector.tensor_copy(state[:, 0, :], bank[5][:, P:P + DI]).then_inc(b_S, 1)
                    elif cc != NC - 1:
                        dve.wait_ge(b_sd, (NC - 2) * kb + cc)
                        nc.vector.tensor_tensor(state[:, cc % 2, :], sdec[:, :], bank[5][:, P:P + DI], ALU.add).then_inc(b_S, 1)
                if i := late(at(b, par, c, CONV1)):
                    conv_taps(i[0], i[3])
                if i := at(b, par, c, LAG_Y):
                    k, _, _, cc = i
                    q = cc % 2
                    dve.wait_ge(b_ys, k + 1)
                    wait(dve, b_yT, k - 1)
                    wait(dve, b_ss, k - 1)
                    nc.vector.tensor_tensor(yz[:, q, :], ys[:, :], zs[:, q, :], ALU.mult).then_inc(b_yz, 1)
                if i := at(b, par, c, LAG_O):
                    k, _, _, cc = i
                    dve.wait_ge(b_O, k + 1)
                    dve.wait_ge(b_rg, k + 1)
                    xr = x_sb[:, :, :, :].rearrange("p b c d -> p (b c) d")[:, bass.ds(k, 1), :].rearrange("p a d -> p (a d)")
                    nc.vector.scalar_tensor_tensor(out=xo[:, :], in0=bank[6][:, 2 * P:3 * P], scalar=rg[:, cc % 2, 0:1],
                                                   in1=xr, op0=ALU.mult, op1=ALU.add).then_inc(b_xo, 1)
                    dve.wait_ge(b_xo, k + 1)
                    nc.vector.tensor_tensor(xr, xo[:, :], bank[6][:, 3 * P:4 * P], ALU.add).then_inc(b_x2, 1)
                if i := at(b, par, c, LAG_O + 1):
                    k, _, _, cc = i
                    dve.wait_ge(b_x2, k + 1)
                    nc.vector.bn_stats(st6[:, bass.ds(k, 1), :].rearrange("p a m -> p (a m)"),
                                       chunk(x_sb, k)).then_inc(s_st, 1)

            def norm(g):
                wait(dve, c_xm, 2 * g - 2)
                for i in range(2):
                    normalise(2 * g + i, xh2[g % 2][:, i * T:(i + 1) * T]).then_inc(c_xh, 1)

            def shift(g):
                for i in range(2):
                    b, part = 2 * g + i, slice(i * T, (i + 1) * T)
                    dve.wait_ge(c_sx, b + 1)
                    wait(dve, c_T, b - 3)
                    if g > 1:
                        dve.wait_ge(c_h2[g - 2], 16)
                    nc.vector.tensor_tensor(xm[g % 2][:, part].rearrange("p (c d) -> p c d", d=P),
                                            xh2[g % 2][:, part].rearrange("p (c d) -> p c d", d=P),
                                            shB[:, b:b + 1, :].broadcast_to([P, NC, P]), ALU.add).then_inc(c_xm, 1)

            def drain(i):
                if i == 0:
                    mean_var(2, slice(0, NT - NP), NB + NT - NP)
                if i == 2:
                    dve.wait_ge(s_rs, 2)
                    norm(0)
                if i == 3:
                    norm(1)
                    dve.wait_ge(s_mb, 32)
                    shift(0)
            phase_b(dve, slot, drain)
            mean_var(3, slice(NT - NP, NT), NB + NT)
            shift(1)
            norm(NB // 2 - 2)
            dve.wait_ge(s_rs, 3)
            norm(NB // 2 - 1)
            shift(NB // 2 - 2)
            shift(NB // 2 - 1)

            nlink = [0]

            def link(ins):
                nlink[0] += 1
                ins.then_inc(c_link, 1)
                dve.wait_ge(c_link, nlink[0])

            def bc(a):
                return a.unsqueeze(2).broadcast_to([P, a.shape[1], NE])

            def per_expert(a, n):
                return a.unsqueeze(1).broadcast_to([P, n, NE])

            def first_of(src, i):
                link(nc.vector.tensor_reduce(top[:, i, :], src, AX, ALU.max))
                link(nc.vector.tensor_tensor(eq, src, bc(top[:, i, :]), ALU.is_equal))
                link(nc.vector.tensor_tensor(eq, eq, per_expert(desc[:, :], NT), ALU.mult))
                link(nc.vector.tensor_reduce(pick[:, :], eq, AX, ALU.max))
                link(nc.vector.tensor_tensor(oh[:, i, :, :], eq, bc(pick[:, :]), ALU.is_equal))
            dve.wait_ge(c_lT, 1)
            link(nc.vector.tensor_copy(hold[:, 0:NA].rearrange("p (b c e) -> p b c e", b=NB, e=NE),
                                       bank[4][:, 0:NA].rearrange("p (c b e) -> p b c e", b=NB, e=NE)))
            first_of(lg, 0)
            nc.vector.tensor_tensor(ex[:, :, 0:NE], lg, bc(top[:, 0, :]), ALU.subtract).then_inc(c_exi, 1)
            link(nc.vector.scalar_tensor_tensor(out=rest, in0=oh[:, 0, :, :], scalar=-BIG, in1=lg, op0=ALU.mult, op1=ALU.add))
            first_of(rest, 1)
            nc.vector.tensor_tensor(ex[:, :, NE], top[:, 1, :], top[:, 0, :], ALU.subtract).then_inc(c_exi, 1)
            link(nc.vector.tensor_tensor(chosen, oh[:, 0, :, :], oh[:, 1, :, :], ALU.add))
            src, reach, step = chosen, 1, 0
            while reach < NT:
                dst = scan[2][:, 1:, :] if 2 * reach >= NT else scan[step % 2]
                nc.vector.tensor_copy(dst[:, 0:reach, :], src[:, 0:reach, :])
                if 2 * reach >= NT:
                    nc.vector.memset(scan[2][:, 0:1, :], 0.0)
                ins = nc.vector.tensor_tensor(dst[:, reach:, :], src[:, reach:, :], src[:, 0:NT - reach, :], ALU.add)
                if 2 * reach >= NT:
                    ins.then_inc(c_scan, 1)
                else:
                    link(ins)
                src, reach, step = dst, 2 * reach, step + 1
            dve.wait_ge(c_exp, 1)
            link(nc.vector.tensor_reduce(zsum[:, :], ex[:, :, 0:NE], AX, ALU.add))
            link(nc.vector.reciprocal(wts[:, 0, :], zsum[:, :]))
            nc.vector.tensor_tensor(wts[:, 1, :], ex[:, :, NE], wts[:, 0, :], ALU.mult)
            dve.wait_ge(c_rk, 1)
            steps = cells[:, 0:NE * NT].rearrange("p (e n) -> p e n", n=NT)
            upto = cells[:, 0:NE * NE].rearrange("p (n e) -> p n e", e=NE)
            link(nc.vector.tensor_copy(first_e[:, :], bank[3][:, NA:NA + NE]))
            link(nc.vector.tensor_tensor(steps, first_e[:, :].unsqueeze(2).broadcast_to([P, NE, NT]),
                                         cst[:, C["steps"]].unsqueeze(1).broadcast_to([P, NE, NT]), ALU.is_gt))
            link(nc.vector.tensor_reduce(tiles_e[:, :], steps, AX, ALU.add))
            link(nc.vector.tensor_tensor(upto, cst[:, C["upto"]].rearrange("p (n e) -> p n e", e=NE),
                                         per_expert(tiles_e[:, :], NE), ALU.mult))
            link(nc.vector.tensor_reduce(ends_e[:, :], upto, AX, ALU.add))
            link(nc.vector.tensor_tensor(first_e[:, :], ends_e[:, :], tiles_e[:, :], ALU.subtract))
            link(nc.vector.tensor_scalar(first_e[:, :], first_e[:, :], float(P), -1.0, ALU.mult, ALU.add))
            link(nc.vector.tensor_tensor(place, bank[3][:, 0:NA].rearrange("p (a e) -> p a e", e=NE),
                                         per_expert(first_e[:, :], NT), ALU.add))
            for k in range(TOPK):
                ins = nc.vector.tensor_tensor(where[:, k, :, :], oh[:, k, :, :], place, ALU.mult)
            link(ins)
            link(nc.vector.tensor_reduce(posf[:, :], where[:, :, :, :].rearrange("p k a e -> p (k a) e"), AX, ALU.add))
            link(nc.vector.tensor_scalar(phi[:, :], posf[:, :], -(P - 1) / 2.0, 1.0 / P, ALU.add, ALU.mult))
            link(nc.vector.tensor_scalar(phi[:, :], phi[:, :], WHOLE, None, ALU.add))
            link(nc.vector.tensor_scalar(phi[:, :], phi[:, :], -WHOLE, None, ALU.add))
            nc.vector.scalar_tensor_tensor(out=plo[:, :], in0=phi[:, :], scalar=-float(P), in1=posf[:, :], op0=ALU.mult,
                                           op1=ALU.add).then_inc(t_pos, 1)
            dve.wait_ge(t_pos, 1)

            for g in range(TOPK * NT // 8):
                some = slice(8 * g, 8 * g + 8)
                half = slice(8 * (g % 2), 8 * (g % 2) + 8)
                wait(dve, t_mm, g - 1)
                nc.vector.tensor_tensor(istile[:, half, :], cst[:, C["tile"]].unsqueeze(1).broadcast_to([P, 8, TILES]),
                                        phi[:, some].unsqueeze(2).broadcast_to([P, 8, TILES]), ALU.is_equal).then_inc(t_tile, 1)
                nc.vector.tensor_tensor(isplace[:, half, :], cst[:, C["lane"]].unsqueeze(1).broadcast_to([P, 8, P]),
                                        plo[:, some].unsqueeze(2).broadcast_to([P, 8, P]), ALU.is_equal).then_inc(t_hot, 1)
            spans = cells.rearrange("p (n e) -> p n e", e=NE)
            link(nc.vector.tensor_tensor(spans, bc(cst[:, C["tile"]]), per_expert(ends_e[:, :], TILES), ALU.is_ge))
            link(nc.vector.tensor_reduce(E_, spans, AX, ALU.add))
            nc.vector.tensor_scalar(t_exp[:, :], E_[0:1, :], float(NE - 1), None, ALU.min).then_inc(t_tab, 1)
            dve.wait_ge(t_mm, TOPK * NT // 8)
            nc.vector.tensor_copy(tbT, bank[4][0:TILES, 0:P]).then_inc(t_flat, 1)
            dve.wait_ge(t_turn, 1)
            link(nc.vector.tensor_copy(tb, bank[5][:, 0:TILES]))
            link(nc.vector.scalar_tensor_tensor(out=tsel, in0=tb, scalar=0.0, in1=cst[:, C["nobody"]], op0=ALU.is_equal, op1=ALU.mult))
            link(nc.vector.scalar_tensor_tensor(out=tsel, in0=tb, scalar=-1.0, in1=tsel, op0=ALU.add, op1=ALU.add))
            link(nc.vector.tensor_copy(dst_ix[:, :], tsel))
            link(nc.vector.tensor_scalar(tsel, tb, NTOK + 0.5, -float(NTOK), ALU.is_ge, ALU.mult))
            link(nc.vector.scalar_tensor_tensor(out=tsel, in0=tb, scalar=-1.0, in1=tsel, op0=ALU.add, op1=ALU.add))
            nc.vector.tensor_scalar(src_ix[:, :], tsel, 0.0, None, ALU.max).then_inc(t_src, 1)
            dve.wait_ge(t_tab, 1)
            dve.wait_ge(s_moe, 16 * 4)

            def experts(t, u):
                if i := tile(t, u, -1):
                    n, v = i
                    e = dve.value_load(t_exp[0:1, bass.ds(n, 1)], min_val=0, max_val=NE - 1)
                    wait(dve, e_h, n - 1)
                    nc.vector.tensor_copy(w1c[:, v % 2, :], w1_sb[:, bass.ds(e, 1), :].rearrange("p e h -> p (e h)"))
                    wait(dve, e_o, n - 3)
                    nc.vector.tensor_copy(w2c[:, v % 4, :], w2_sb[:, bass.ds(e, 1), :, :].rearrange("p e k d -> p (e k d)"))
                    nc.vector.tensor_copy(b1c[:, v % 4, :], cols[:, bass.ds(NK * e + R_B1, NK)]).then_inc(e_w, 1)
                    wait(dve, e_y, n - 3)
                    nc.vector.tensor_copy(b2c[:, v % 4, :], b2B[:, bass.ds(e, 1), :].rearrange("p e d -> p (e d)")).then_inc(e_b, 1)
                if i := tile(t, u, 1):
                    n, v = i
                    dve.wait_ge(e_o, n + 1)
                    dve.wait_ge(e_b, n + 1)
                    wait(dve, e_sc[v % 4], 16 * nth(n, v, 4))
                    nc.vector.tensor_tensor(yt[:, v % 4, :], bank[4 + v % 2][:, 0:P], b2c[:, v % 4, :], ALU.add).then_inc(e_y, 1)
            tiles(dve, experts)

            for b in range(NB + 1):
                if b < NB:
                    dve.wait_ge(f_w, b + 1)
                    for c in range(NC):
                        ins = nc.vector.scalar_tensor_tensor(out=res[:, b, 0, c, :], in0=res[:, b, 1, c, :],
                                                             scalar=wts[:, 1, NC * b + c:NC * b + c + 1],
                                                             in1=res[:, b, 0, c, :], op0=ALU.mult, op1=ALU.add)
                    ins.then_inc(f_sum, 1)
                if b > 0:
                    dve.wait_ge(f_gb, b)
                    nc.vector.tensor_tensor(x_sb[:, b - 1, :, :], x_sb[:, b - 1, :, :], res[:, b - 1, 1, :, :], ALU.add
                                            ).then_inc(f_x, 1)

        @block.tensor
        def _(pe):
            pe.wait_ge(s_cst, 16 * 6)
            nc.tensor.transpose(bank[0][:, 0:NR], rows[0:NR, :], ident[0:NR, 0:NR]).then_inc(s_pre, 1)
            pe.wait_ge(s_wts, 16 * 9)
            pe.wait_ge(s_one, 1)
            nc.tensor.matmul(bank[1][:, 0:3 * NH], ones[0:1, :], small[:, :], start=True, stop=True).then_inc(s_pre, 1)
            nc.tensor.transpose(bank[2][:, 0:P], win[:, :], ident).then_inc(s_pre, 1)
            for j in range(NX + NBLK):
                nc.tensor.transpose(bank[3 + j // 4][:, (j % 4) * P:(j % 4 + 1) * P], wz_nat[:, j, :], ident)
            nc.tensor.transpose(bank[4][:, 2 * P:2 * P + NH], wdt_nat[:, :], ident[0:NH, 0:NH]).then_inc(s_pre, 1)
            pe.wait_ge(s_prd, 5)
            for j in range(6):
                mm = nc.tensor.matmul(bank[1][:, 64 + j * NB:64 + (j + 1) * NB], wmod_sb[:, j * P:(j + 1) * P], siluc[:, 1, :],
                                      start=True, stop=True)
            mm.then_inc(s_pre, 1)
            nc.tensor.matmul(bank[6][0:NB, 0:2 * P], siluc[:, 1, :], wmod_sb[:, 3 * P:5 * P], start=True, stop=True
                             ).then_inc(s_mr2, 1)

            pe.wait_ge(s_prd, 8)

            def conv_proj(n, b, j):
                wait(pe, b_tp, n - 1)
                nc.tensor.matmul(bank[j % 2][:, :], wzT[:, XB0 + j * P:XB0 + (j + 1) * P], tokens(hT, b),
                                 start=True, stop=True).then_inc(b_cv, 1)

            def gates(b):
                if b == 0:
                    pe.wait_ge(s_gd, 1)
                wait(pe, s_ge, b - 1)
                o = bank[g_bank[b % 2]]
                for k in range(NX):
                    nc.tensor.matmul(o[:, k * P:(k + 1) * P], wout_nat[:, k * P:(k + 1) * P], gad[:, b, :], start=True, stop=True)
                nc.tensor.matmul(o[:, NX * P:(NX + 1) * P], ones[:, :], gbd[:, b, :], start=True, stop=True).then_inc(s_gm, 1)

            def phase_a(s, par):
                if inside(s, NB):
                    pe.wait_ge(a_xh, s + 1)
                    wait(pe, a_ev, s)
                    for c in range(NC):
                        mm = nc.tensor.transpose(bank[0][:, c * P:(c + 1) * P], xh[:, par, c * P:(c + 1) * P], ident)
                    mm.then_inc(a_T, 1)
                if inside(s - 1, NB):
                    pe.wait_ge(a_ev, s)
                    wait(pe, a_t1, s - 1)
                    nc.tensor.matmul(bank[1][:, :], wqT[:, :], xnT[:, 1 - par, :], start=True, stop=True).then_inc(a_q, 1)
                    wait(pe, a_t2, s - 1)
                    nc.tensor.matmul(bank[2][:, :], wqrT[:, :], xnT[:, 1 - par, :], start=True, stop=True).then_inc(a_qr, 1)
                if inside(s - 2, NB):
                    pe.wait_ge(a_sq, s - 1)
                    wait(pe, a_ln, s - 2)
                    nc.tensor.matmul(bank[3][:, :], ones[:, :], sq, start=True, stop=True).then_inc(a_n, 1)
                if inside(s - 4, NB):
                    pe.wait_ge(a_h, s - 3)
                    nc.tensor.matmul(bank[4][0:NB * NH, :], wdtz[:, (NB - s + 4) * NH:(2 * NB - s + 4) * NH],
                                     tokens(hT, s - 4), start=(s == 4), stop=(s == NB + 3)).then_inc(a_d, 1)
                if inside(s - 1, NB):
                    gates(s - 1)
                if inside(s - NB, EARLY):
                    pe.wait_ge(a_ev, NB)
                    if s > NB:
                        pe.wait_ge(a_t1, NB)
                    conv_proj(s - NB, 0, s - NB)
            few_slots(NB, 1, 4, phase_a)
            pe.wait_ge(a_de, 1)
            for c in range(NC):
                mm = nc.tensor.transpose(bank[5][:, c * NB * NH:(c + 1) * NB * NH], dtT[:, c * P:(c + 1) * P],
                                         ident[0:NB * NH, 0:NB * NH])
            mm.then_inc(a_dT, 1)
            pe.wait_ge(s_dv, 4)
            dA = dtA[:, :, :].rearrange("p a h -> p (a h)")
            for i, m in enumerate((triS, triI, ones[:, :])):
                mm = nc.tensor.matmul(bank[5][:, i * NT * NH:(i + 1) * NT * NH], m, dA, start=True, stop=True)
            mm.then_inc(s_dp, 1)

            def slot(b, par, c):
                if i := at(b, par, c, LAG_Y):
                    k, kb, kpar, cc = i
                    q = cc % 2
                    pe.wait_ge(b_M, k + 1)
                    pe.wait_ge(b_xdt, k + 1)
                    wait(pe, b_yd, k)
                    for h in range(NH):
                        mm = nc.tensor.matmul(bank[7][:, h * HD:(h + 1) * HD], M4[q][:, h * P:(h + 1) * P],
                                              xdt[:, q, h * HD:(h + 1) * HD], start=True, stop=True)
                    if cc:
                        pe.wait_ge(b_S, (NC - 1) * kb + cc)
                        mm = nc.tensor.matmul(bank[7][:, DI:2 * DI], xbcT[:, kpar, NX + 1, cc * P:(cc + 1) * P],
                                              state[:, (cc + 1) % 2, :], start=True, stop=True)
                    mm.then_inc(b_Y, 1)
                    wait(pe, b_Gm, k + 1)
                    wait(pe, b_S, (NC - 1) * kb + cc)
                    if cc != NC - 1:
                        pe.wait_ge(b_xdec, (NC - 1) * kb + cc + 1)
                        mm = nc.tensor.matmul(bank[5][:, P:P + DI], xB[:, cc, DI:DI + P], xdec[:, q, :], start=True, stop=True)
                        mm.then_inc(b_St, 1)
                    else:
                        pe.sem_inc(b_St, 1)
                if i := at(b, par, c, 1):
                    k, kb, kpar, cc = i
                    wait(pe, b_Gm, k)
                    tok = slice(cc * P, (cc + 1) * P)
                    nc.tensor.matmul(bank[5][:, 0:P], xbcT[:, kpar, NX, tok], xbcT[:, kpar, NX + 1, tok],
                                     start=True, stop=True).then_inc(b_GS, 1)
                if i := at(b, par, c, 0):
                    k, kb, kpar, cc = i
                    tok = slice(cc * P, (cc + 1) * P)
                    if cc == 0:
                        pe.wait_ge(b_cs, NBLK * (kb + 1))
                    wait(pe, b_Te, k)
                    for i in range(NX + 1):
                        mm = nc.tensor.transpose(bank[2][:, i * P:(i + 1) * P], xbcT[:, kpar, i, tok], ident)
                    mm.then_inc(b_T, 1)
                if i := at(b, par, c, LAG_T):
                    k, _, _, cc = i
                    pe.wait_ge(b_yz, k + 1)
                    wait(pe, b_x2, k - 1)
                    for i in range(NX):
                        mm = nc.tensor.transpose(bank[6][:, i * P:(i + 1) * P], yz[:, cc % 2, i * P:(i + 1) * P], ident)
                    mm.then_inc(b_yT, 1)
                if i := at(b, par, c, 0):
                    k, kb, kpar, cc = i
                    tok = slice(cc * P, (cc + 1) * P)
                    pe.wait_ge(b_rl, k + 1)
                    wait(pe, b_E, k)
                    nc.tensor.matmul(bank[3][:, :], triS, rhsL[cc % 2], start=True, stop=True).then_inc(b_L, 1)
                    if cc == 0:
                        pe.wait_ge(s_hq[kpar], 16 * kb + 32 - 16 * kpar)
                    wait(pe, b_zs, k)
                    nc.tensor.matmul(bank[4][:, 0:DI], hq[:, kpar, 0, tok], wzT[:, 0:DI], start=True, stop=True).then_inc(b_z, 1)
                if i := late(at(b, par, c, CONV0)):
                    conv_proj(i[0], i[1], i[3])
                if i := at(b, par, c, LAG_O):
                    k, kb, kpar, cc = i
                    nxt = at(b, par, c, LAG_T)
                    pe.wait_ge(b_yTe, k + 2 if nxt else k + 1)
                    if not nxt:
                        wait(pe, b_x2, k)
                    for i in range(NX):
                        nc.tensor.matmul(bank[6][:, 2 * P:3 * P], ynT[:, cc % 2, i * P:(i + 1) * P],
                                         woB[:, bass.ds(kb, 1), i, :].rearrange("p b d -> p (b d)"),
                                         start=(i == 0), stop=(i == NX - 1))
                    nc.tensor.matmul(bank[6][:, 3 * P:4 * P], hq[:, kpar, 1, cc * P:(cc + 1) * P], tokens(gad, kb),
                                     start=True, stop=True).then_inc(b_O, 1)

            def turn(g):
                for i in range(2):
                    pe.wait_ge(c_xm, 2 * g + i + 1)
                    wait(pe, c_ev, 2 * g + i - 1)
                    for c in range(NC):
                        mm = nc.tensor.transpose(bank[i][:, c * P:(c + 1) * P],
                                                 xm[g % 2][:, i * T + c * P:i * T + (c + 1) * P], ident)
                    mm.then_inc(c_T, 1)
                for i in range(2):
                    b = 2 * g + i
                    pe.wait_ge(c_ev, b + 1)
                    nc.tensor.matmul(bank[2][0:NB * NE, :], wrz[:, (NB - b) * NE:(2 * NB - b) * NE], h2T[i][:, :],
                                     start=(b == 0), stop=(b == NB - 1)).then_inc(c_lg, 1)

            phase_b(pe, slot, lambda i: None)
            pe.wait_ge(s_moe, 16 * 4)
            for g in range(NB // 2):
                turn(g)
            pe.wait_ge(c_le, 1)
            for c in range(NC):
                mm = nc.tensor.transpose(bank[4][:, c * NB * NE:(c + 1) * NB * NE], lgT[:, c * P:(c + 1) * P],
                                         ident[0:NB * NE, 0:NB * NE])
            mm.then_inc(c_lT, 1)
            pe.wait_ge(c_scan, 1)
            nc.tensor.matmul(bank[3][:, 0:NA], triI, hold[:, 3 * NA:4 * NA], start=True, stop=False)
            nc.tensor.matmul(bank[3][:, 0:NA], ones[:, :], hold[:, 11 * NA:12 * NA], start=False, stop=True)
            nc.tensor.matmul(bank[3][:, NA:NA + NE], ones[:, :], scan[2][:, NT, :], start=True, stop=True).then_inc(c_rk, 1)
            for i in range(TOPK * NT):
                if i % 8 == 0:
                    pe.wait_ge(t_hot, i // 8 + 1)
                    pe.wait_ge(t_num, i // 8 + 1)
                mm = nc.tensor.matmul(bank[4][0:TILES, 0:P], istile[:, i % 16, :], isplace[:, i % 16, :],
                                      start=(i == 0), stop=(i == TOPK * NT - 1))
                if i % 8 == 7:
                    mm.then_inc(t_mm, 1)
            pe.wait_ge(t_flat, 1)
            nc.tensor.transpose(bank[5][:, 0:TILES], tbT, ident[0:TILES, 0:TILES]).then_inc(t_turn, 1)


            def experts(t, u):
                if i := tile(t, u, -1):
                    n, v = i
                    pe.wait_ge(e_ld[v], 16 * (nth(n, v, RING) + 1))
                    wait(pe, e_Te, n - 1)
                    nc.tensor.transpose(bank[2 + v % 2][:, 0:P], xt[:, v, 0:P], ident).then_inc(e_T, 1)
                if i := tile(t, u, 0):
                    n, v = i
                    pe.wait_ge(e_Te, n + 1)
                    pe.wait_ge(e_w, n + 1)
                    wait(pe, e_g, n - 1)
                    for k in range(NK):
                        mm = nc.tensor.matmul(bank[v % 2][:, k * P:(k + 1) * P], w1c[:, v % 2, k * P:(k + 1) * P], xtT[:, v % 2, :],
                                              start=True, stop=True)
                    mm.then_inc(e_h, 1)
                if i := tile(t, u, 1):
                    n, v = i
                    pe.wait_ge(e_g, n + 1)
                    wait(pe, e_y, n - 1)
                    for k in range(NK):
                        mm = nc.tensor.matmul(bank[4 + v % 2][:, 0:P], gT[:, v % 2, k * P:(k + 1) * P],
                                              w2c[:, v % 4, k * P:(k + 1) * P], start=(k == 0), stop=(k == NK - 1))
                    mm.then_inc(e_o, 1)
            tiles(pe, experts)


INPUTS = ["x", "W_in", "W_z", "conv_w", "conv_b", "dt_bias", "A_log", "D_param", "norm_pre_w", "norm_gated_w", "W_out",
          "w_router", "w1", "b1", "w2", "b2", "c_in", "wmod"]
NAMES = {"x": "L0_attn_x", "W_in": "L0_attn_W_in", "W_z": "L0_attn_W_zxbcdt", "conv_w": "L0_attn_conv_w",
         "conv_b": "L0_attn_conv_b", "dt_bias": "L0_attn_dt_bias", "A_log": "L0_attn_A_log", "D_param": "L0_attn_D_param",
         "norm_pre_w": "L0_attn_norm_pre_w", "norm_gated_w": "L0_attn_norm_gated_w", "W_out": "L0_attn_W_out",
         "w_router": "L0_ffn_w_router", "w1": "L0_ffn_w1", "b1": "L0_ffn_b1", "w2": "L0_ffn_w2", "b2": "L0_ffn_b2",
         "c_in": "L0_c", "wmod": "L0_wmod"}


def layout(NB, NC, NE, TILES):
    T, parts, at = NC * P, {}, 3 * P
    for name, n in (("cos", T), ("sin", T), ("ids", TOPK * NB * NC), ("lane", P), ("tile", TILES), ("nobody", TILES),
                    ("steps", NB * NC), ("upto", NE * NE)):
        parts[name] = slice(at, at + n)
        at += n
    parts["all"] = slice(0, at)
    return parts


def constants(NB, T, NE):
    NTOK, NT, NC = NB * T, NB * T // P, T // P
    TILES = TOPK * NT + NE - 1
    k, l = np.arange(P)[:, None], np.arange(P)[None, :]
    inv_freq = np.float32(1.0) / np.float32(10000.0) ** (np.arange(0, 8, 2, dtype=np.float32) / np.float32(8))
    ang = (np.arange(T, dtype=np.float32)[None, :] * inv_freq.astype(np.float32)[:, None]).astype(np.float32)
    cos = np.tile(np.cos(ang), (P // 4, 1))
    sin = np.tile(np.concatenate([-np.sin(ang), np.sin(ang)]), (P // 8, 1))
    e = np.arange(NE)

    def rows(a):
        return np.broadcast_to(a, (P, a.shape[-1]))
    i = np.arange(TOPK * NT)[None, :]
    parts = [k == l, k > l, k <= l, cos, sin,
             1 + i // NC * T + k * NC + i % NC,
             rows(l), rows(np.arange(TILES)[None, :]),
             1 + TOPK * NTOK + P * np.arange(TILES)[None, :] + k,
             rows(P * np.arange(NT)[None, :]),
             rows((e[None, :] <= e[:, None]).reshape(1, -1))]
    return np.concatenate(parts, axis=1).astype(np.float32)


def kernel(**inputs):
    import concourse.bacc as bacc
    from concourse.bass_utils import run_bass_kernel_spmd

    nc = bacc.Bacc("TRN2", target_bir_lowering=False, num_devices=1)
    arrays = {n: np.ascontiguousarray(inputs[NAMES[n]]) for n in INPUTS}
    arrays["consts"] = constants(*arrays["x"].shape[:2], arrays["w1"].shape[0])
    args = {n: nc.dram_tensor(n, a.shape, mybir.dt.from_np(a.dtype), kind="ExternalInput").ap() for n, a in arrays.items()}
    out = nc.dram_tensor("out", arrays["x"].shape, F32, kind="ExternalOutput").ap()
    build(nc, out=out, **args)
    r = run_bass_kernel_spmd(nc, [arrays], core_ids=[0])
    return r.results[0]["out"]
```
